# Optimizing a Trainium2 kernel written in Bass

```python
import numpy as np
import jax
import jax.numpy as jnp

def _softmax(x, axis=-1):
    return jax.nn.softmax(x, axis=axis)

def _gelu(x):
    return jax.nn.gelu(x, approximate=True)

def _silu(x):
    return jax.nn.silu(x)

def _sigmoid(x):
    return jax.nn.sigmoid(x)

def _layernorm(x, axis=-1, eps=1e-05):
    m = jnp.mean(x, axis=axis, keepdims=True)
    v = jnp.var(x, axis=axis, keepdims=True)
    return (x - m) / jnp.sqrt(v + eps)

def _scatter_add(tgt, idx, src, axis=0):
    return tgt.at[idx].add(src)

def _segment_sum(src, seg, n):
    return jax.ops.segment_sum(src, seg, n)
kernel_name = 'mk_adaln_d1_jaxref_r4_1ace7e'

def setup_inputs(seed: int=0):
    np.random.seed(seed)
    _w = jnp.asarray

    def _L0_attn_setup():
        import jax, jax.numpy as jnp
        import numpy as np
        from jax import lax
        H = 1024
        DIN = 2048
        N = 16
        K = 4
        R = 64
        B_SZ = 2
        L = 512
        EPS = 1e-06

        def rmsnorm(x, w):
            return x * lax.rsqrt(jnp.mean(x * x, axis=-1, keepdims=True) + EPS) * w

        def _selective_scan(x, dt, A, Bm, Cm):
            xT = jnp.transpose(x, (2, 0, 1))
            dtT = jnp.transpose(dt, (2, 0, 1))
            BT = jnp.transpose(Bm, (2, 0, 1))
            CT = jnp.transpose(Cm, (2, 0, 1))

            def step(h, inp):
                x_t, dt_t, B_t, C_t = inp
                dA = jnp.exp(dt_t[..., None] * A)
                dBx = dt_t[..., None] * B_t[:, None, :] * x_t[..., None]
                h = dA * h + dBx
                y = jnp.einsum('bdn,bn->bd', h, C_t)
                return (h, y)
            h0 = jnp.zeros((x.shape[0], x.shape[1], A.shape[1]), dtype=x.dtype)
            _, ys = lax.scan(step, h0, (xT, dtT, BT, CT))
            return jnp.transpose(ys, (1, 2, 0))
        key = jax.random.key(seed)
        ks = jax.random.split(key, 8)
        hidden_states = jax.random.normal(ks[0], (B_SZ, L, H), dtype=jnp.float32)
        s = 0.02
        in_proj_w = jax.random.normal(ks[1], (H, 2 * DIN), dtype=jnp.float32) * s
        conv_w = jax.random.normal(ks[2], (DIN, K), dtype=jnp.float32) * 0.2
        conv_b = jax.random.normal(ks[3], (DIN,), dtype=jnp.float32) * 0.02
        x_proj_w = jax.random.normal(ks[4], (R + 2 * N, DIN), dtype=jnp.float32) * s
        dt_proj_w = jax.random.normal(ks[5], (DIN, R), dtype=jnp.float32) * s
        dt_bias = jax.random.normal(ks[6], (DIN,), dtype=jnp.float32) * 0.5 - 4.0
        A_log = jnp.log(jnp.broadcast_to(jnp.arange(1, N + 1, dtype=jnp.float32)[None, :], (DIN, N)))
        D_param = jnp.ones((DIN,), dtype=jnp.float32)
        out_proj_w = jax.random.normal(ks[7], (H, DIN), dtype=jnp.float32) * s
        dt_ln_w = jnp.ones((R,), dtype=jnp.float32)
        B_ln_w = jnp.ones((N,), dtype=jnp.float32)
        C_ln_w = jnp.ones((N,), dtype=jnp.float32)
        return dict(hidden_states=hidden_states, in_proj_w=in_proj_w, conv_w=conv_w, conv_b=conv_b, x_proj_w=x_proj_w, dt_proj_w=dt_proj_w, dt_bias=dt_bias, A_log=A_log, D_param=D_param, out_proj_w=out_proj_w, dt_ln_w=dt_ln_w, B_ln_w=B_ln_w, C_ln_w=C_ln_w)
    _L0_attn_in = _L0_attn_setup()

    def _L0_ffn_setup():
        import jax, jax.numpy as jnp
        import numpy as np
        N_STREAMS = 4
        DIM = 256
        SINKHORN_ITERS = 50
        SINKHORN_TAU = 0.1
        RMS_EPS = 1.1920929e-07

        def sinkhorn_log(logits, num_iters=SINKHORN_ITERS, tau=SINKHORN_TAU):
            Z = logits / tau
            u0 = jnp.zeros(Z.shape[:-1], Z.dtype)
            v0 = jnp.zeros_like(u0)

            def step(carry, _):
                u, v = carry
                u = -jax.nn.logsumexp(Z + v[..., None, :], axis=-1)
                v = -jax.nn.logsumexp(Z + u[..., :, None], axis=-2)
                return ((u, v), None)
            (u, v), _ = jax.lax.scan(step, (u0, v0), None, length=num_iters)
            return jnp.exp(Z + u[..., :, None] + v[..., None, :])
        key = jax.random.key(seed)
        ks = jax.random.split(key, 6)
        B, T = (4, 512)
        n, C = (N_STREAMS, DIM)
        wd = n * C
        x = jax.random.normal(ks[0], (B, T, wd), dtype=jnp.float32)
        W_res = 0.01 * jax.random.normal(ks[1], (n * n, wd), dtype=jnp.float32)
        W_pre = 0.01 * jax.random.normal(ks[2], (n, wd), dtype=jnp.float32)
        W_post = 0.01 * jax.random.normal(ks[3], (n, wd), dtype=jnp.float32)
        H_res_base = jnp.full((n, n), -0.5, dtype=jnp.float32)
        H_res_base = H_res_base.at[jnp.arange(n), jnp.arange(n)].set(0.0)
        H_pre_base = jnp.zeros((n,), dtype=jnp.float32).at[0].set(1.0)
        H_post_base = jnp.zeros((n,), dtype=jnp.float32)
        gate = jnp.array([5.0], dtype=jnp.float32)
        W_branch = 1.0 / np.sqrt(C) * jax.random.normal(ks[4], (C, C), dtype=jnp.float32)
        return {'x': x, 'W_res': W_res, 'W_pre': W_pre, 'W_post': W_post, 'H_res_base': H_res_base, 'H_pre_base': H_pre_base, 'H_post_base': H_post_base, 'gate': gate, 'W_branch': W_branch}
    _L0_ffn_in = _L0_ffn_setup()
    _L0_c = _w((lambda *s: np.random.randn(*s).astype(np.float32) * 0.05)(4, 1024))
    _L0_wmod = _w((lambda *s: np.random.randn(*s).astype(np.float32) * 0.05)(1024, 6 * 1024) * 1024 ** (-0.5))
    _d = {'L0_attn_hidden_states': _L0_attn_in['hidden_states'], 'L0_attn_in_proj_w': _L0_attn_in['in_proj_w'], 'L0_attn_conv_w': _L0_attn_in['conv_w'], 'L0_attn_conv_b': _L0_attn_in['conv_b'], 'L0_attn_x_proj_w': _L0_attn_in['x_proj_w'], 'L0_attn_dt_proj_w': _L0_attn_in['dt_proj_w'], 'L0_attn_dt_bias': _L0_attn_in['dt_bias'], 'L0_attn_A_log': _L0_attn_in['A_log'], 'L0_attn_D_param': _L0_attn_in['D_param'], 'L0_attn_out_proj_w': _L0_attn_in['out_proj_w'], 'L0_attn_dt_ln_w': _L0_attn_in['dt_ln_w'], 'L0_attn_B_ln_w': _L0_attn_in['B_ln_w'], 'L0_attn_C_ln_w': _L0_attn_in['C_ln_w'], 'L0_ffn_W_res': _L0_ffn_in['W_res'], 'L0_ffn_W_pre': _L0_ffn_in['W_pre'], 'L0_ffn_W_post': _L0_ffn_in['W_post'], 'L0_ffn_H_res_base': _L0_ffn_in['H_res_base'], 'L0_ffn_H_pre_base': _L0_ffn_in['H_pre_base'], 'L0_ffn_H_post_base': _L0_ffn_in['H_post_base'], 'L0_ffn_gate': _L0_ffn_in['gate'], 'L0_ffn_W_branch': _L0_ffn_in['W_branch'], 'L0_c': _L0_c, 'L0_wmod': _L0_wmod}
    _x0 = _d['L0_attn_hidden_states']
    _d['L0_attn_hidden_states'] = jax.random.normal(jax.random.fold_in(jax.random.key(seed), 1), (4, 512, 1024), dtype=_x0.dtype)
    del _x0
    return _d

def reference(L0_attn_hidden_states, L0_attn_in_proj_w, L0_attn_conv_w, L0_attn_conv_b, L0_attn_x_proj_w, L0_attn_dt_proj_w, L0_attn_dt_bias, L0_attn_A_log, L0_attn_D_param, L0_attn_out_proj_w, L0_attn_dt_ln_w, L0_attn_B_ln_w, L0_attn_C_ln_w, L0_ffn_W_res, L0_ffn_W_pre, L0_ffn_W_post, L0_ffn_H_res_base, L0_ffn_H_pre_base, L0_ffn_H_post_base, L0_ffn_gate, L0_ffn_W_branch, L0_c, L0_wmod):

    def _L0_attn_ref(hidden_states, in_proj_w, conv_w, conv_b, x_proj_w, dt_proj_w, dt_bias, A_log, D_param, out_proj_w, dt_ln_w, B_ln_w, C_ln_w):
        import jax, jax.numpy as jnp
        import numpy as np
        from jax import lax
        H = 1024
        DIN = 2048
        N = 16
        K = 4
        R = 64
        B_SZ = 2
        L = 512
        EPS = 1e-06

        def rmsnorm(x, w):
            return x * lax.rsqrt(jnp.mean(x * x, axis=-1, keepdims=True) + EPS) * w

        def _selective_scan(x, dt, A, Bm, Cm):
            xT = jnp.transpose(x, (2, 0, 1))
            dtT = jnp.transpose(dt, (2, 0, 1))
            BT = jnp.transpose(Bm, (2, 0, 1))
            CT = jnp.transpose(Cm, (2, 0, 1))

            def step(h, inp):
                x_t, dt_t, B_t, C_t = inp
                dA = jnp.exp(dt_t[..., None] * A)
                dBx = dt_t[..., None] * B_t[:, None, :] * x_t[..., None]
                h = dA * h + dBx
                y = jnp.einsum('bdn,bn->bd', h, C_t)
                return (h, y)
            h0 = jnp.zeros((x.shape[0], x.shape[1], A.shape[1]), dtype=x.dtype)
            _, ys = lax.scan(step, h0, (xT, dtT, BT, CT))
            return jnp.transpose(ys, (1, 2, 0))
        proj = hidden_states @ in_proj_w
        x, z = jnp.split(proj, 2, axis=-1)
        x = jnp.transpose(x, (0, 2, 1))
        z = jnp.transpose(z, (0, 2, 1))
        Lq = x.shape[-1]
        xp = jnp.pad(x, ((0, 0), (0, 0), (K - 1, 0)))
        xc = conv_b[None, :, None]
        for k in range(K):
            xc = xc + conv_w[None, :, k:k + 1] * xp[:, :, k:k + Lq]
        xc = jax.nn.silu(xc)
        ssm_p = jnp.einsum('bdl,ed->ble', xc, x_proj_w)
        dt_r = rmsnorm(ssm_p[..., :R], dt_ln_w)
        Bm = rmsnorm(ssm_p[..., R:R + N], B_ln_w)
        Cm = rmsnorm(ssm_p[..., R + N:], C_ln_w)
        dt = jnp.einsum('blr,dr->bdl', dt_r, dt_proj_w)
        dt = jax.nn.softplus(dt + dt_bias[None, :, None])
        A = -jnp.exp(A_log)
        Bm = jnp.transpose(Bm, (0, 2, 1))
        Cm = jnp.transpose(Cm, (0, 2, 1))
        ys = _selective_scan(xc, dt, A, Bm, Cm)
        y = (ys + D_param[None, :, None] * xc) * jax.nn.silu(z)
        return jnp.einsum('bdl,hd->blh', y, out_proj_w)

    def _L0_ffn_ref(x, W_res, W_pre, W_post, H_res_base, H_pre_base, H_post_base, gate, W_branch):
        import jax, jax.numpy as jnp
        import numpy as np
        N_STREAMS = 4
        DIM = 256
        SINKHORN_ITERS = 50
        SINKHORN_TAU = 0.1
        RMS_EPS = 1.1920929e-07

        def sinkhorn_log(logits, num_iters=SINKHORN_ITERS, tau=SINKHORN_TAU):
            Z = logits / tau
            u0 = jnp.zeros(Z.shape[:-1], Z.dtype)
            v0 = jnp.zeros_like(u0)

            def step(carry, _):
                u, v = carry
                u = -jax.nn.logsumexp(Z + v[..., None, :], axis=-1)
                v = -jax.nn.logsumexp(Z + u[..., :, None], axis=-2)
                return ((u, v), None)
            (u, v), _ = jax.lax.scan(step, (u0, v0), None, length=num_iters)
            return jnp.exp(Z + u[..., :, None] + v[..., None, :])
        B, T, nC = x.shape
        n = N_STREAMS
        C = nC // n
        x_norm = x * jax.lax.rsqrt(jnp.mean(x * x, axis=-1, keepdims=True) + RMS_EPS)
        H_res_logits = (x_norm @ W_res.T).reshape(B, T, n, n) + H_res_base
        H_pre_logits = x_norm @ W_pre.T + H_pre_base
        H_post_logits = x_norm @ W_post.T + H_post_base
        H_res = sinkhorn_log(H_res_logits)
        H_pre = jax.nn.softmax(H_pre_logits, axis=-1)
        H_post = jax.nn.softmax(H_post_logits, axis=-1)
        g = jax.nn.sigmoid(gate)[0]
        I = jnp.eye(n, dtype=H_res.dtype)
        H_res = (1.0 - g) * I + g * H_res
        x_streams = x.reshape(B, T, n, C)
        x_pre = jnp.einsum('btnc,btn->btc', x_streams, H_pre)
        y = x_pre @ W_branch
        x_mixed = jnp.einsum('btij,btjc->btic', H_res, x_streams)
        y_distributed = jnp.einsum('btc,btn->btnc', y, H_post)
        return (x_mixed + y_distributed).reshape(B, T, nC)
    x = L0_attn_hidden_states
    mod = (_silu(L0_c) @ L0_wmod).reshape(L0_c.shape[0], 6, 1, -1)
    sa, ca, ga, sb, cb, gb = (mod[:, 0], mod[:, 1], mod[:, 2], mod[:, 3], mod[:, 4], mod[:, 5])
    ga = (2 * (ga >= 0) - 1) * jnp.maximum(jnp.abs(ga), 0.25)
    gb = (2 * (gb >= 0) - 1) * jnp.maximum(jnp.abs(gb), 0.25)
    h = _layernorm(x, axis=-1) * (1 + ca) + sa
    x = x + ga * _L0_attn_ref(h, L0_attn_in_proj_w, L0_attn_conv_w, L0_attn_conv_b, L0_attn_x_proj_w, L0_attn_dt_proj_w, L0_attn_dt_bias, L0_attn_A_log, L0_attn_D_param, L0_attn_out_proj_w, L0_attn_dt_ln_w, L0_attn_B_ln_w, L0_attn_C_ln_w)
    h = _layernorm(x, axis=-1) * (1 + cb) + sb
    x = x + gb * _L0_ffn_ref(h, L0_ffn_W_res, L0_ffn_W_pre, L0_ffn_W_post, L0_ffn_H_res_base, L0_ffn_H_pre_base, L0_ffn_H_post_base, L0_ffn_gate, L0_ffn_W_branch)
    return x

_drawn_inputs = setup_inputs


def setup_inputs(seed=0):
    import zlib

    import numpy as np

    out = dict(_drawn_inputs(seed))
    spreads = {'L0_attn_D_param': (1.0, 0.6),
     'L0_attn_dt_ln_w': (1.0, 0.6),
     'L0_attn_B_ln_w': (1.0, 0.6),
     'L0_attn_C_ln_w': (1.0, 0.6),
     'L0_ffn_H_post_base': (0.0, 0.8)}
    factors = {'L0_attn_in_proj_w': 4.881,
     'L0_attn_conv_w': 4.92,
     'L0_attn_conv_b': 8.0,
     'L0_attn_x_proj_w': 8.0,
     'L0_attn_dt_proj_w': 8.0,
     'L0_attn_dt_bias': 8.0,
     'L0_attn_A_log': 8.0,
     'L0_attn_out_proj_w': 4.855,
     'L0_ffn_W_pre': 6.921,
     'L0_ffn_W_post': 5.911,
     'L0_ffn_H_pre_base': 3.031}
    for name, (base, spread) in spreads.items():
        noise = np.random.default_rng([zlib.crc32(name.encode()), seed]).standard_normal(out[name].shape)
        drawn = base * np.exp(spread * noise) if base else spread * noise
        out[name] = jnp.asarray(drawn.astype(out[name].dtype))
    for name, factor in factors.items():
        out[name] = (out[name] * factor).astype(out[name].dtype)
    return out
```

```python
from contextlib import ExitStack

import concourse.bass as bass
from concourse import mybir

F32 = mybir.dt.float32
ALU = mybir.AluOpType
ACT = mybir.ActivationFunctionType
AX = mybir.AxisListType.X

P = 128
B, T, H = 4, 512, 1024
DIN, N, K, R = 2048, 16, 4, 64
TT = T // P
KH = H // P
KD = DIN // P
NT = B * TT
E = R + 2 * N
S, C = 4, 256
NL = S * S + 2 * S
NG = KD // 4
ITERS, REFRESH = 50, 16
TAU = 0.1
EPS_LN, EPS_RMS, EPS_FFN = 1e-5, 1e-6, 1.1920929e-07
G_MIN = 0.25

VR = 4
HR = 8
F_TAP, F_BIAS, F_C, F_W = 16, 20, 21, 25
CR_V, CR_SCAN, CR_TH, CR_STT, CR_PROJ = 32, 8, 8, 4, 4


class Steps:

    def __init__(self, eng, sem):
        self.eng, self.sem, self.base, self.n, self.outer = eng, sem, 0, 0, []

    def mark(self, ins):
        ins.then_inc(self.sem, 1)
        self.n += 1

    def done(self):
        return self.base + self.n

    def link(self, ins):
        self.mark(ins)
        self.eng.wait_ge(self.sem, self.done())

    def enter(self, turn, per):
        start = self.done()
        self.outer.append((start, self.base))
        self.base, self.n = start + turn * per, 0
        self.top = self.base

    def leave(self, turns, per):
        start, _ = self.outer.pop()
        self.base, self.n = start + turns * per, 0


def build(nc, x, ident, w_in, conv_w, conv_b, x_proj, dt_proj, dt_bias, A_log, D_param, w_out,
          dt_ln, B_ln, C_ln, W_res, W_pre, W_post, res_base, pre_base, post_base, gate, W_branch,
          c_cols, w_mod, out):
    z_s = nc.dram_tensor("z_s", (B, KD, P, T), F32).ap()
    xc_s = nc.dram_tensor("xc_s", (B, KD, P, T), F32).ap()
    b_s = nc.dram_tensor("b_s", (B, N, T), F32).ap()
    mod_s = nc.dram_tensor("mod_s", (B, 6 * H), F32).ap()
    x1_s = nc.dram_tensor("x1_s", (B, TT, P, H), F32).ap()
    h2_s = nc.dram_tensor("h2_s", (B, TT, P, H), F32).ap()

    with ExitStack() as ctx:
        def sb(name, shape):
            return ctx.enter_context(nc.sbuf_tensor(name, shape, F32))

        def sem(name):
            return ctx.enter_context(nc.semaphore(name))

        dt_sb = sb("dt_sb", [P, KD, T])
        u_sb = sb("u_sb", [P, KD, T])
        y_sb = sb("y_sb", [P, TT, DIN])
        hT = sb("hT", [P, KH, T])
        hring = sb("hring", [P, HR, T])
        wring = sb("wring", [P, 4, KH, P])
        vring = sb("vring", [P, VR, T])
        bbc = sb("bbc", [P, 2, T])
        acc = sb("acc", [P, 2, T])
        thx = sb("thx", [P, T])
        thz = sb("thz", [P, T])
        xcb = sb("xcb", [P, 2, T])
        szb = sb("szb", [P, 2, T])
        row = sb("row", [P, H])
        idn = sb("idn", [P, P])
        cols = sb("cols", [P, N, F_W])
        kcur = sb("kcur", [P, 2, F_W])
        alog = sb("alog", [P, N, KD])
        cw = sb("cw", [P, KD, K])
        cb = sb("cb", [P, KD])
        dsc = sb("dsc", [P, KD])
        xpw = sb("xpw", [P, KD, E])
        dpw = sb("dpw", [R + 1, DIN])
        dtln = sb("dtln", [R, 1])
        blnw = sb("blnw", [P, 2 * N])
        wcat = sb("wcat", [P, KH, NL])
        base = sb("base", [P, NL])
        gcol = sb("gcol", [P, 4])
        wbr = sb("wbr", [P, C // P, C])
        ccol = sb("ccol", [P, KH, B])
        modc = sb("modc", [P, B, 2 * KH])
        mcur = sb("mcur", [P, 2 * KH])
        mv = sb("mv", [P, NT, 2])
        mvcur = sb("mvcur", [P, TT, 2])
        st = sb("st", [P, 2, 2, 6])
        sm = sb("sm", [P, NT, 4])
        mv2 = sb("mv2", [P, TT, 2])
        st2 = sb("st2", [P, TT, 2, 6])
        Lcur = sb("Lcur", [P, TT, NL + 1])
        Lall = sb("Lall", [P, NT, NL + 1])
        ms = sb("ms", [P, TT, 4, 3])
        dtr = sb("dtr", [R + 1, T])

        ps = [ctx.enter_context(nc.psum_tensor(f"bank{i}", [P, T], F32)) for i in range(8)]

        names = """phase passed const_in modw0 modw1 modw2 mod_mm mod_tr mod_ev mod_rows mod_st silu_c modc_ready
            x_in0 x_in1 x_in2 x_in3 stat_done var_ready rstd_ready a_ready g_ready
            xn_done nt_done ne_done mc_ready
            w_in0 w_in1 w_in2 w_in3 proj_done tap_done conv_done thx_done xc_done thz_done z_done
            xc_st0 xc_st1 z_st0 z_st1 kcur_ready b_in0 b_in1 v_ready da_ready scan_done th_done stt_done
            g_in0 g_in1 gt_done gate_done wo_in0 wo_in1 wo_in2 wo_in3 wo_done out_done row_in rows_in
            x1_done x1_st res_in f_var f_rstd f_mul f_add f_sq f_tr f_ev f_lg h2_st
            u_in0 u_in1 u_in2 u_in3 xp_done xp_ev xp_tr rms_sq rms_rs bt_ready n_tr n_ev bs_st dt_mm e_done
            nw_done l_done q_done dt_done ask answer
            t3_in0 t3_in1 t3_pre t3_tr t3_ev t3_y t3_mix t3_st act_own dve_own""".split()
        s = {n: sem(n) for n in names}

        def slots(prefix, n):
            return [s[f"{prefix}{i}"] for i in range(n)]

        def barrier(eng, k):
            alone(eng, k)
            eng.drain().then_inc(s["phase"], 1)
            eng.wait_ge(s["phase"], 5 * (k + 1))
            alone(eng, k)

        def alone(eng, k=None):
            if not isinstance(k, int):
                eng.sem_inc(s["passed"], 1)

        PER_ROW, FIRST_ROW = 5, 5

        def ph(b, i):
            return b * PER_ROW + (FIRST_ROW + i)

        LAST_ROW = FIRST_ROW + PER_ROW * (B - 1)

        x4 = hring[:].rearrange("p (q j) t -> p q (j t)", q=TT)
        hT4 = hT[:].rearrange("p (q j) t -> p q (j t)", q=TT)
        h2 = y_sb[:, 0:2, :].rearrange("p a (b h) -> p (a b) h", h=H)
        h2T = wring[:, 0:2]
        frow = hring[:, 0:4, :].rearrange("p (q j) t -> p q (j t)", q=2)
        modr = u_sb[0:B].rearrange("p k t -> p (k t)")[:, 0:6 * H]
        bT = thx[0:N, :]
        sA = y_sb[:, 2, 0:TT * E].rearrange("p (q e) -> p q e", q=TT)
        sq = y_sb[:, 3, 0:TT * E].rearrange("p (q e) -> p q e", q=TT)
        ssmT = thz[0:E, :]
        e2, l2, nw2 = acc, xcb, szb
        trash = hring[:, 4:6, :].rearrange("p a t -> p (a t)")

        def mod_w(chunk):
            return [dt_sb[:, 0:8], dt_sb[:, 8:16], y_sb[:, 0:2].rearrange("p a (b t) -> p (a b) t", t=T)][chunk % 3]

        def mod_row(b, j):
            return mod_s[bass.ds(b, 1), j * H:(j + 1) * H].rearrange("o h -> (o h)").partition_broadcast(P)

        def skv(i, n):
            return dt_sb[:, i, 0:n]
        Zb, Kb, Tb = skv(0, NT * 16), skv(1, NT * 16), skv(2, NT * 16)
        Ub, Vb, Mb, Sb_ = skv(3, NT * S), skv(4, NT * S), skv(5, NT * S), skv(6, NT * S)
        ub, vb = skv(7, NT * S), skv(8, NT * S)
        Pb, Eb = skv(9, NT * 8), skv(10, NT * 8)
        rs0, rs1 = skv(11, NT), skv(12, NT)
        pm, psu = skv(13, NT * 2), skv(14, NT * 2)
        lnu, lnv = skv(15, NT * S), Mb
        Hall = hring[:, 0, 0:NT * NL].rearrange("p (q l) -> p q l", q=NT)
        Hcur = hring[:, 1, 0:TT * NL].rearrange("p (q l) -> p q l", q=TT)

        sink_requests = [[(rs1, rs0, ACT.Ln, 1.0), (rs1, rs1, ACT.Exp, -0.5)],
                         [(Eb, Pb, ACT.Exp, 1.0)],
                         [(Tb, Kb, ACT.Exp, 1.0)], [(Sb_, Sb_, ACT.Ln, 1.0)],
                         [(Tb, Kb, ACT.Exp, 1.0)], [(Sb_, Sb_, ACT.Ln, 1.0)],
                         [(Kb, Zb, ACT.Exp, 1.0)]]
        sink_requests += [[(lnu, ub, ACT.Ln, 1.0), (lnv, vb, ACT.Ln, 1.0)], [(Kb, Zb, ACT.Exp, 1.0)]] * 3

        block = ctx.enter_context(nc.Block())

        @block.sync
        def _(sp):
            sp.sem_inc(s["xc_st0"], 16)
            sp.sem_inc(s["xc_st1"], 16)
            sp.sem_inc(s["z_st0"], 16)
            sp.sem_inc(s["z_st1"], 16)

            consts = [(idn[:], ident), (ccol[:], c_cols), (alog[:], A_log), (cw[:], conv_w), (cb[:], conv_b),
                      (dsc[:], D_param), (xpw[:], x_proj), (dpw[0:R, :], dt_proj), (dpw[R:R + 1, :], dt_bias),
                      (dtln[:], dt_ln), (blnw[:, 0:N], B_ln.partition_broadcast(P)),
                      (blnw[:, N:2 * N], C_ln.partition_broadcast(P)),
                      (wcat[:, :, 0:S * S], W_res), (wcat[:, :, S * S:S * S + S], W_pre),
                      (wcat[:, :, S * S + S:NL], W_post),
                      (base[:, 0:S * S], res_base.partition_broadcast(P)),
                      (base[:, S * S:S * S + S], pre_base.partition_broadcast(P)),
                      (base[:, S * S + S:NL], post_base.partition_broadcast(P)),
                      (gcol[:, 0:1], gate.partition_broadcast(P)), (wbr[:], W_branch)]
            for dst, src in consts:
                sp.dma_start(dst, src).then_inc(s["const_in"], 16)

            modw = slots("modw", 3)

            def load_mod(chunk):
                if chunk >= 3:
                    sp.wait_ge(s["mod_mm"], chunk - 2)
                sp.dma_start(mod_w(chunk), w_mod[chunk]).then_inc(modw[chunk % 3], 16)

            for c in range(3):
                load_mod(c)
            x_in = slots("x_in", 4)
            for i in range(NT):
                if i >= 4:
                    sp.wait_ge(s["stat_done"], i - 3)
                sp.dma_start(hT4[:, i % 4, :], x[i // TT, i % TT]).then_inc(x_in[i % 4], 16)
            load_mod(3)
            barrier(sp, 0)

            def norm(b, count, k):
                for tt in range(TT):
                    sp.dma_start(x4[:, tt, :], x[bass.ds(b, 1), tt].rearrange("o p h -> (o p) h")
                                 ).then_inc(x_in[tt], 16)
                barrier(sp, k)

            w_slot = slots("w_in", 4)
            xc_st, z_st = slots("xc_st", 2), slots("z_st", 2)
            b_in = slots("b_in", 2)

            def dram3(t, b, n):
                return t[bass.ds(b, 1), bass.ds(n, 1)].rearrange("o q p t -> (o q p) t")

            def load_w(b, i, par):
                f = b * N + i * 2 + par
                sp.wait_ge(s["proj_done"], f * 2 + 1)
                sp.dma_start(wring[:, 2 * par], w_in[bass.ds(i * 2 + par, 1)].rearrange("o p k c -> (o p) k c")
                             ).then_inc(w_slot[2 * par], 16)
                sp.wait_ge(s["proj_done"], f * 2 + 2)
                sp.dma_start(wring[:, 2 * par + 1], w_in[bass.ds(i * 2 + (KD + par), 1)].rearrange("o p k c -> (o p) k c")
                             ).then_inc(w_slot[2 * par + 1], 16)

            def store_front(b, i, par):
                f = b * N + i * 2 + par
                sp.wait_ge(s["xc_done"], f + 3)
                sp.dma_start(dram3(xc_s, b, i * 2 + par), xcb[:, par]).then_inc(xc_st[par], 16)
                sp.wait_ge(s["z_done"], f + 2)
                sp.dma_start(dram3(z_s, b, i * 2 + par), szb[:, par]).then_inc(z_st[par], 16)

            def load_b(b, i, par):
                n = b * N + i * 2 + par
                sp.wait_ge(s["v_ready"], n * KD + KD)
                sp.dma_start(bbc[:, par], b_s[bass.ds(b, 1), bass.ds(i * 2 + par, 1)]
                             .rearrange("o n t -> (o n t)").partition_broadcast(P)).then_inc(b_in[par], 16)

            def stores_end(b):
                for par in range(2):
                    sp.wait_ge(xc_st[par], b * (8 * 16) + 9 * 16)
                    sp.wait_ge(z_st[par], b * (8 * 16) + 9 * 16)

            def scan(b, front, k):
                def step(i, first):
                    for par in range(2):
                        if front:
                            load_w(b + 1, i, par)
                        load_b(b, i, par)
                        if front and not first:
                            store_front(b + 1, i - 1, par)
                step(0, True)
                with sp.Fori(1, N // 2) as i:
                    step(i, False)
                if front:
                    for par in range(2):
                        store_front(b + 1, N // 2 - 1, par)
                    stores_end(b + 1)
                barrier(sp, k)

            g_in, wo_in = slots("g_in", 2), slots("wo_in", 4)

            def mix(b, k):
                for tt in range(TT):
                    sp.dma_start(hT4[:, tt, :], x[bass.ds(b, 1), tt].rearrange("o p h -> (o p) h")
                                 ).then_inc(s["res_in"], 16)
                sp.dma_start(row[:], mod_row(b, 2)).then_inc(s["row_in"], 16)
                sp.dma_start(frow[:, 0, :], mod_row(b, 4)).then_inc(s["rows_in"], 16)
                sp.dma_start(frow[:, 1, :], mod_row(b, 3)).then_inc(s["rows_in"], 16)

                def load_wo(t):
                    sp.wait_ge(s["wo_done"], b * KD + (t + 1))
                    sp.dma_start(wring[:, t % 4].rearrange("p k c -> p (k c)"), w_out[t]
                                 ).then_inc(wo_in[t % 4], 16)
                for t in range(4):
                    load_wo(t)
                for kt in range(KD):
                    sp.wait_ge(s["gate_done"], b * KD + (kt + 1))
                    sp.dma_start(xcb[:, kt % 2], xc_s[bass.ds(b, 1), kt].rearrange("o p t -> (o p) t")
                                 ).then_inc(g_in[kt % 2], 16)
                    sp.dma_start(szb[:, kt % 2], z_s[bass.ds(b, 1), kt].rearrange("o p t -> (o p) t")
                                 ).then_inc(g_in[kt % 2], 16)
                    if kt in (5, 7, 9, 11):
                        load_wo(4 + (kt - 5) // 2)
                for t in range(8, KD):
                    load_wo(t)
                for tt in range(TT):
                    sp.wait_ge(s["x1_done"], b * TT + (tt + 1))
                    sp.dma_start(x1_s[bass.ds(b, 1), tt].rearrange("o p h -> (o p) h"), hT4[:, tt, :]
                                 ).then_inc(s["x1_st"], 16)
                sp.wait_ge(s["x1_st"], b * (16 * TT) + 16 * TT)
                barrier(sp, k)

            def ffn1(b, k):
                for tt in range(TT):
                    sp.wait_ge(s["f_add"], b * TT + (tt + 1))
                    sp.dma_start(h2_s[bass.ds(b, 1), tt].rearrange("o p h -> (o p) h"), h2[:, tt, :]
                                 ).then_inc(s["h2_st"], 16)
                sp.wait_ge(s["h2_st"], b * (16 * TT) + 16 * TT)
                barrier(sp, k)

            u_in = slots("u_in", 4)

            def delta(b, k):
                for q in range(4):
                    sp.dma_start(u_sb[:, 4 * q:4 * q + 4, :],
                                 xc_s[bass.ds(b, 1), 4 * q:4 * q + 4].rearrange("o k p t -> (o p) k t")
                                 ).then_inc(u_in[q], 16)
                sp.wait_ge(s["n_ev"], b * 2 + 2)
                sp.dma_start(b_s[bass.ds(b, 1)].rearrange("o n t -> (o n) t"), bT[:]).then_inc(s["bs_st"], 16)
                sp.wait_ge(s["bs_st"], b * 16 + 16)
                barrier(sp, k)

            norm(0, 0, 1)

            def front_step(i, first):
                for par in range(2):
                    load_w(0, i, par)
                    if not first:
                        store_front(0, i - 1, par)
            front_step(0, True)
            with sp.Fori(1, N // 2) as i:
                front_step(i, False)
            for par in range(2):
                store_front(0, N // 2 - 1, par)
            stores_end(0)
            barrier(sp, 2)

            for c in range(4, 12):
                load_mod(c)
            sp.wait_ge(s["mod_rows"], 1)
            sp.dma_start(mod_s, modr[:]).then_inc(s["mod_st"], 16)
            sp.wait_ge(s["mod_st"], 16)
            barrier(sp, 3)
            delta(0, 4)
            with sp.Fori(0, B - 1) as b:
                norm(b + 1, 0, ph(b, 0))
                scan(b, True, ph(b, 1))
                mix(b, ph(b, 2))
                ffn1(b, ph(b, 3))
                delta(b + 1, ph(b, 4))
            scan(B - 1, False, LAST_ROW)
            mix(B - 1, LAST_ROW + 1)
            ffn1(B - 1, LAST_ROW + 2)

            t3_in, t3_st = slots("t3_in", 2), s["t3_st"]
            barrier(sp, LAST_ROW + 3)
            with sp.Fori(0, B) as b:
                sp.dma_start(h2[:], h2_s[bass.ds(b, 1)].rearrange("o q p h -> (o p) q h")).then_inc(t3_in[0], 16)
                sp.dma_start(hT4[:], x1_s[bass.ds(b, 1)].rearrange("o q p h -> (o p) q h")).then_inc(t3_in[1], 16)
                sp.dma_start(row[:], mod_row(b, 5)).then_inc(s["row_in"], 16)
                for tt in range(TT):
                    sp.wait_ge(s["t3_mix"], b * TT + (tt + 1))
                    sp.dma_start(out[bass.ds(b, 1), tt].rearrange("o p h -> (o p) h"), hT4[:, tt, :]
                                 ).then_inc(t3_st, 16)
                sp.wait_ge(t3_st, b * (16 * TT) + 16 * TT)
                alone(sp)
            sp.wait_ge(t3_st, 16 * NT)

        @block.tensor
        def _(pe):
            pe.wait_ge(s["const_in"], 16 * 20)
            for name, credit in (("proj_done", CR_PROJ), ("th_done", CR_TH), ("wo_done", 4)):
                pe.sem_inc(s[name], credit)
            pe.wait_ge(s["silu_c"], 1)
            modw = slots("modw", 3)

            def mod_chunk(c):
                pe.wait_ge(modw[c % 3], 16 * (c // 3 + 1))
                if c >= 2:
                    pe.wait_ge(s["mod_ev"], c - 1)
                for k in range(KH):
                    mm = pe.matmul(ps[c % 2][0:B, :], ccol[:, k, :], mod_w(c)[:, k, :], start=(k == 0), stop=(k == KH - 1))
                mm.then_inc(s["mod_mm"], 1)

            for c in range(4):
                mod_chunk(c)
            pe.wait_ge(s["mod_ev"], 4)
            for j in range(2 * KH):
                mm = pe.transpose(ps[2][:, j * B:(j + 1) * B], modr[:, j * P:(j + 1) * P], idn[0:B, 0:B])
            mm.then_inc(s["mod_tr"], 1)
            barrier(pe, 0)

            def norm(b, k):
                for h in range(KH):
                    for tt in range(TT):
                        if h == 0:
                            pe.wait_ge(s["xn_done"], b * TT + (tt + 1))
                        if tt == 0:
                            pe.wait_ge(s["ne_done"], b * KH + (h + 1))
                        mm = pe.transpose(ps[h % 4][:, tt * P:(tt + 1) * P], x4[:, tt, h * P:(h + 1) * P], idn[:])
                    mm.then_inc(s["nt_done"], 1)
                barrier(pe, k)

            w_slot = slots("w_in", 4)

            def project(b, i, par, which, half):
                f = b * N + i * 2 + par
                if half == 0:
                    pe.wait_ge(w_slot[2 * par + which], b * (8 * 16) + i * 16 + 16)
                    pe.wait_ge(s["z_done" if which else "conv_done"], f + 1)
                for k in range(4 * half, 4 * half + 4):
                    mm = pe.matmul(ps[6 + which][:], wring[:, 2 * par + which, k, :], hT[:, k, :],
                                   start=(k == 0), stop=(k == KH - 1))
                if half:
                    mm.then_inc(s["proj_done"], 1)

            def scan(b, front, k):
                def step(i):
                    for par in range(2):
                        for g in range(NG):
                            grp = (b * N + i * 2 + par) * NG + g
                            pe.wait_ge(s["scan_done"], grp * 4 + (CR_SCAN + 4))
                            for tt in range(TT):
                                pe.wait_ge(s["stt_done"], grp * 4 + (tt + 1))
                                for j in range(4):
                                    mm = pe.transpose(ps[tt][:, j * P:(j + 1) * P],
                                                      hring[:, (4 * g + j) % HR, tt * P:(tt + 1) * P], idn[:])
                                mm.then_inc(s["th_done"], 1)
                            if front:
                                project(b + 1, i, par, g // 2, g % 2)
                with pe.Fori(0, N // 2) as i:
                    step(i)
                barrier(pe, k)

            wo_in = slots("wo_in", 4)

            def mix(b, k):
                def turn(kt):
                    pe.wait_ge(s["gate_done"], b * KD + (kt + 1))
                    for tt in range(TT):
                        mm = pe.transpose(ps[4 + kt % 2][:, tt * P:(tt + 1) * P], y_sb[:, tt, kt * P:(kt + 1) * P], idn[:])
                    mm.then_inc(s["gt_done"], 1)
                turn(0)
                turn(1)
                for half in range(2):
                    for kt in range(KD):
                        t = half * 8 + kt // 2
                        if half == 0:
                            pe.wait_ge(s["gate_done"], b * KD + (kt + 3))
                        if kt % 2 == 0:
                            pe.wait_ge(wo_in[t % 4], b * 64 + 16 * (t // 4 + 1))
                        for tt in range(TT):
                            mm = pe.matmul(ps[4 * half + tt][:], u_sb[:, kt, tt * P:(tt + 1) * P],
                                           wring[:, t % 4].rearrange("p k c -> p (k c)")[:, (kt % 2) * 512:(kt % 2) * 512 + 512],
                                           start=(kt == 0), stop=(kt == KD - 1))
                            if kt == KD - 1:
                                mm.then_inc(s["out_done"], 1)
                        if kt == KD - 1:
                            pe.drain().then_inc(s["wo_done"], 1)
                        elif kt % 2:
                            mm.then_inc(s["wo_done"], 1)
                        if half == 0 and kt + 2 < KD:
                            turn(kt + 2)
                barrier(pe, k)

            def ffn1(b, k):
                for tt in range(TT):
                    pe.wait_ge(s["f_add"], b * TT + (tt + 1))
                    for h in range(KH):
                        if h % 4 == 0 and tt:
                            pe.wait_ge(s["f_ev"], b * 8 + (2 * tt - 1 + h // 4))
                        mm = pe.transpose(ps[h // 4][:, (h % 4) * P:(h % 4 + 1) * P], h2[:, tt, h * P:(h + 1) * P], idn[:])
                        if h % 4 == 3:
                            mm.then_inc(s["f_tr"], 1)
                    pe.wait_ge(s["f_ev"], b * 8 + (2 * tt + 2))
                    for h in range(KH):
                        mm = pe.matmul(ps[2 + tt][:, 0:NL], h2T[:, tt % 2, h, :], wcat[:, h, :],
                                       start=(h == 0), stop=(h == KH - 1))
                    mm.then_inc(s["f_lg"], 1)
                barrier(pe, k)

            def delta(b, k):
                for kt in range(KD):
                    if kt % 4 == 0:
                        pe.wait_ge(s[f"u_in{kt // 4}"], b * 16 + 16)
                    mm = pe.matmul(ps[6][0:E, :], xpw[:, kt, :], u_sb[:, kt, :], start=(kt == 0), stop=(kt == KD - 1))
                mm.then_inc(s["xp_done"], 1)
                pe.wait_ge(s["xp_ev"], b + 1)
                for tt in range(TT):
                    mm = pe.transpose(ps[7][:, tt * E:(tt + 1) * E], ssmT[:, tt * P:(tt + 1) * P], idn[0:E, 0:E])
                mm.then_inc(s["xp_tr"], 1)
                pe.wait_ge(s["bt_ready"], b + 1)
                alone(pe)
                for tt in range(TT):
                    mm = pe.transpose(ps[6][0:R, tt * P:(tt + 1) * P], sA[:, tt, 0:R], idn[:])
                for tt in range(TT):
                    mm = pe.transpose(ps[7][0:N, tt * P:(tt + 1) * P], sA[:, tt, R:R + N], idn[:])
                mm.then_inc(s["n_tr"], 1)
                pe.wait_ge(s["n_ev"], b * 2 + 1)
                for kt in range(KD):
                    pe.wait_ge(s["dt_done"], b * KD + (kt + 1))
                    pe.matmul(ps[kt % 4][:], dpw[:, kt * P:(kt + 1) * P], dtr[:], start=True, stop=True
                              ).then_inc(s["dt_mm"], 1)
                barrier(pe, k)

            norm(0, 1)
            with pe.Fori(0, N // 2) as i:
                for par in range(2):
                    for q in range(4):
                        project(0, i, par, q // 2, q % 2)
            barrier(pe, 2)
            for c in range(4, 12):
                mod_chunk(c)
            barrier(pe, 3)
            delta(0, 4)
            with pe.Fori(0, B - 1) as b:
                norm(b + 1, ph(b, 0))
                scan(b, True, ph(b, 1))
                mix(b, ph(b, 2))
                ffn1(b, ph(b, 3))
                delta(b + 1, ph(b, 4))
            scan(B - 1, False, LAST_ROW)
            mix(B - 1, LAST_ROW + 1)
            ffn1(B - 1, LAST_ROW + 2)
            barrier(pe, LAST_ROW + 3)
            with pe.Fori(0, B) as b:
                for tt in range(TT):
                    pe.wait_ge(s["t3_pre"], b * TT + (tt + 1))
                    for j in range(2):
                        mm = pe.transpose(ps[tt % 2][:, j * P:(j + 1) * P], acc[:, tt % 2, j * P:(j + 1) * P], idn[:])
                    mm.then_inc(s["t3_tr"], 1)
                    pe.wait_ge(s["t3_ev"], b * TT + (tt + 1))
                    for j in range(2):
                        mm = pe.matmul(ps[2 + tt % 2][:, 0:C], thx[:, (tt % 2) * C + j * P:(tt % 2) * C + (j + 1) * P],
                                       wbr[:, j, :], start=(j == 0), stop=(j == 1))
                    mm.then_inc(s["t3_y"], 1)

        @block.scalar
        def _(act):
            own = Steps(act, s["act_own"])
            act.sem_inc(s["ne_done"], 4)
            act.wait_ge(s["const_in"], 16 * 20)
            cth = sm[:].rearrange("p a b -> p (a b)")[:, 0:KH * B]
            act.activation(cth, ccol[:].rearrange("p k b -> p (k b)"), ACT.Tanh, scale=0.5).then_inc(s["a_ready"], 1)
            act.activation(alog[:], alog[:], ACT.Exp).then_inc(s["a_ready"], 1)
            act.activation(gcol[:, 1:2], gcol[:, 0:1], ACT.Exp, scale=-1.0).then_inc(s["a_ready"], 1)

            def evict_mod(c):
                act.wait_ge(s["mod_mm"], c + 1)
                act.activation(modr[:, c * T:(c + 1) * T], ps[c % 2][0:B, :], ACT.Identity, scale=0.5
                               ).then_inc(s["mod_ev"], 1)

            for c in range(4):
                evict_mod(c)
            act.preload_act_table_set("natural_log_exp_and_others")
            act.wait_ge(s["var_ready"], 1)
            own.link(act.activation(sm[:, :, 1], sm[:, :, 0], ACT.Ln))
            act.activation(sm[:, :, 1], sm[:, :, 1], ACT.Exp, scale=-0.5).then_inc(s["rstd_ready"], 1)
            barrier(act, 0)

            def norm(b, k):
                act.wait_ge(s["mc_ready"], b + 1)
                for h in range(KH):
                    act.wait_ge(s["nt_done"], b * KH + (h + 1))
                    act.activation(hT[:, h, :], ps[h % 4][:], ACT.Identity, bias=mcur[:, h:h + 1],
                                   scale=mcur[:, KH + h:KH + h + 1]).then_inc(s["ne_done"], 1)
                barrier(act, k)

            def first_tap(b, i, par):
                f = b * N + i * 2 + par
                act.wait_ge(s["proj_done"], f * 2 + (CR_PROJ + 1))
                act.wait_ge(s["xc_done"], f + 1)
                act.activation(acc[:, par, :], ps[6][:], ACT.Identity, bias=kcur[:, par, F_BIAS:F_BIAS + 1],
                               scale=kcur[:, par, F_TAP + K - 1:F_TAP + K]).then_inc(s["tap_done"], 1)

            def tanh_x(b, i, par):
                f = b * N + i * 2 + par
                act.wait_ge(s["conv_done"], f + 2)
                act.wait_ge(s["xc_done"], f + 2)
                act.activation(thx[:], acc[:, par, :], ACT.Tanh).then_inc(s["thx_done"], 1)

            def tanh_z(b, i, par):
                f = b * N + i * 2 + par
                act.wait_ge(s["proj_done"], f * 2 + (CR_PROJ + 2))
                act.wait_ge(s["z_done"], f + 1)
                act.activation(thz[:], ps[7][:], ACT.Tanh, scale=0.5).then_inc(s["thz_done"], 1)

            def scan(b, front, k):
                def step(i, first):
                    for par in range(2):
                        pi, pp = (i, 0) if par else (i - 1, 1)
                        act.wait_ge(s["kcur_ready"], b * N + i * 2 + (N + par + 1))
                        for kt in range(KD):
                            if front and kt == 2 and not (first and par == 0):
                                tanh_x(b + 1, pi, pp)
                            if front and kt == 4 and not (first and par == 0):
                                tanh_z(b + 1, pi, pp)
                            if front and kt == 12:
                                first_tap(b + 1, i, par)
                            g = (b * N + i * 2 + par) * KD + kt
                            act.wait_ge(s["scan_done"], g + (CR_SCAN - 1))
                            act.activation(ps[4 + kt % 2][:], dt_sb[:, kt, :], ACT.Exp, scale=kcur[:, par, kt:kt + 1]
                                           ).then_inc(s["da_ready"], 1)
                step(0, True)
                with act.Fori(1, N // 2) as i:
                    step(i, False)
                if front:
                    tanh_x(b + 1, N // 2 - 1, 1)
                    tanh_z(b + 1, N // 2 - 1, 1)
                barrier(act, k)

            def mix(b, k):
                barrier(act, k)

            def ffn1(b, k):
                act.preload_act_table_set("natural_log_exp_and_others")
                act.wait_ge(s["f_var"], b + 1)
                own.link(act.activation(ms[:, :, 0, 1], ms[:, :, 0, 0], ACT.Ln))
                act.activation(ms[:, :, 0, 1], ms[:, :, 0, 1], ACT.Exp, scale=-0.5).then_inc(s["f_rstd"], 1)
                for tt in range(TT):
                    act.wait_ge(s["f_add"], b * TT + (tt + 1))
                    if tt:
                        act.wait_ge(s["f_sq"], b * TT + tt)
                    act.activation(trash, h2[:, tt, :], ACT.Square, accum_out=Lcur[:, tt, NL:NL + 1]
                                   ).then_inc(s["f_sq"], 1)
                    for j in range(2):
                        act.wait_ge(s["f_tr"], b * 8 + (2 * tt + j + 1))
                        if tt >= 2:
                            act.wait_ge(s["f_lg"], b * TT + (tt - 1))
                        act.activation(h2T[:, tt % 2, 4 * j:4 * j + 4, :].rearrange("p k c -> p (k c)"), ps[j][:], ACT.Copy
                                       ).then_inc(s["f_ev"], 1)
                barrier(act, k)

            def delta(b, k):
                act.preload_act_table_set("natural_log_exp_and_others")
                act.wait_ge(s["xp_done"], b + 1)
                act.activation(ssmT, ps[6][0:E, :], ACT.Copy).then_inc(s["xp_ev"], 1)
                act.wait_ge(s["rms_sq"], b + 1)
                own.link(act.activation(ms[:, :, 1, :], ms[:, :, 0, :], ACT.Ln))
                act.activation(ms[:, :, 1, :], ms[:, :, 1, :], ACT.Exp, scale=-0.5).then_inc(s["rms_rs"], 1)
                act.wait_ge(s["n_tr"], b + 1)
                act.activation(dtr[0:R, :], ps[6][0:R, :], ACT.Copy, scale=dtln[:]).then_inc(s["n_ev"], 1)
                act.activation(bT, ps[7][0:N, :], ACT.Copy).then_inc(s["n_ev"], 1)
                for kt in range(KD):
                    act.wait_ge(s["dt_mm"], b * KD + (kt + 1))
                    act.wait_ge(s["dt_done"], b * KD + (kt + 3))
                    own.link(act.activation(e2[:, kt % 2, :], ps[kt % 4][:], ACT.Abs))
                    own.link(act.activation(e2[:, kt % 2, :], e2[:, kt % 2, :], ACT.Exp, scale=-1.0))
                    act.activation(l2[:, kt % 2, :], e2[:, kt % 2, :], ACT.Ln, bias=1.0).then_inc(s["e_done"], 1)
                barrier(act, k)

            norm(0, 1)
            with act.Fori(0, N // 2) as i:
                for par in range(2):
                    act.wait_ge(s["kcur_ready"], i * 2 + (par + 1))
                    first_tap(0, i, par)
                    tanh_x(0, i, par)
                    tanh_z(0, i, par)
            barrier(act, 2)
            for c in range(4, 12):
                evict_mod(c)
            barrier(act, 3)
            delta(0, 4)
            per_loop = 1 + 1 + 2 * KD
            with act.Fori(0, B - 1) as b:
                own.enter(b, per_loop)
                norm(b + 1, ph(b, 0))
                scan(b, True, ph(b, 1))
                mix(b, ph(b, 2))
                ffn1(b, ph(b, 3))
                delta(b + 1, ph(b, 4))
            own.leave(B - 1, per_loop)
            scan(B - 1, False, LAST_ROW)
            mix(B - 1, LAST_ROW + 1)
            ffn1(B - 1, LAST_ROW + 2)

            act.preload_act_table_set("natural_log_exp_and_others")
            for k, steps in enumerate(sink_requests):
                act.wait_ge(s["ask"], k + 1)
                for n, (dst, src, func, scale) in enumerate(steps):
                    ins = act.activation(dst, src, func, scale=scale)
                    if n < len(steps) - 1:
                        own.link(ins)
                    else:
                        ins.then_inc(s["answer"], 1)
            barrier(act, LAST_ROW + 3)
            with act.Fori(0, B) as b:
                for tt in range(TT):
                    act.wait_ge(s["t3_tr"], b * TT + (tt + 1))
                    act.activation(thx[:, (tt % 2) * C:(tt % 2) * C + C], ps[tt % 2][:, 0:C], ACT.Copy
                                   ).then_inc(s["t3_ev"], 1)

        @block.gpsimd
        def _(pool):
            pool.sem_inc(s["v_ready"], CR_V)
            barrier(pool, 0)
            barrier(pool, 1)
            barrier(pool, 2)
            barrier(pool, 3)

            def scan(b, k):
                b_in = slots("b_in", 2)

                def step(i):
                    for par in range(2):
                        pool.wait_ge(b_in[par], b * (8 * 16) + i * 16 + 16)
                        for kt in range(KD):
                            g = (b * N + i * 2 + par) * KD + kt
                            pool.wait_ge(s["scan_done"], g + (CR_SCAN - VR + 1))
                            pool.tensor_tensor(vring[:, kt % VR, :], u_sb[:, kt, :], bbc[:, par, :], ALU.mult
                                               ).then_inc(s["v_ready"], 1)
                with pool.Fori(0, N // 2) as i:
                    step(i)
                barrier(pool, k)

            def delta(b, k):
                for kt in range(KD):
                    pool.wait_ge(s["nw_done"], b * KD + (kt + 1))
                    pool.tensor_tensor(e2[:, kt % 2, :], e2[:, kt % 2, :], nw2[:, kt % 2, :], ALU.subtract
                                       ).then_inc(s["l_done"], 1)
                    pool.wait_ge(s["l_done"], b * KD + (kt + 1))
                    pool.tensor_tensor(l2[:, kt % 2, :], l2[:, kt % 2, :], e2[:, kt % 2, :], ALU.add
                                       ).then_inc(s["q_done"], 1)
                pool.wait_ge(s["n_tr"], b + 1)
                alone(pool)
                pool.memset(y_sb[:], 0.0)
                barrier(pool, k)

            def ffn1(b, k):
                for tt in range(TT):
                    pool.wait_ge(s["f_mul"], b * TT + (tt + 1))
                    pool.tensor_tensor(h2[:, tt, :], h2[:, tt, :], frow[:, 1, :], ALU.add).then_inc(s["f_add"], 1)
                barrier(pool, k)

            delta(0, 4)
            with pool.Fori(0, B - 1) as b:
                barrier(pool, ph(b, 0))
                scan(b, ph(b, 1))
                barrier(pool, ph(b, 2))
                ffn1(b, ph(b, 3))
                delta(b + 1, ph(b, 4))
            scan(B - 1, LAST_ROW)
            barrier(pool, LAST_ROW + 1)
            ffn1(B - 1, LAST_ROW + 2)
            barrier(pool, LAST_ROW + 3)

        @block.vector
        def _(dve):
            own = Steps(dve, s["dve_own"])
            for name, credit in (("scan_done", CR_SCAN), ("stt_done", CR_STT), ("conv_done", 1), ("z_done", 1),
                                 ("xc_done", 2), ("gate_done", 2), ("dt_done", 4)):
                dve.sem_inc(s[name], credit)

            def ts(out_, in_, a, b_, op0, op1=None):
                return dve.tensor_scalar(out_, in_, a, b_, op0, op1) if op1 is not None else dve.tensor_scalar(out_, in_, a, None, op0)

            def newton(r, v, t):
                own.link(dve.tensor_tensor(t, r, r, ALU.mult))
                own.link(dve.tensor_tensor(t, t, v, ALU.mult))
                own.link(ts(t, t, -0.5, 1.5, ALU.mult, ALU.add))
                own.link(dve.tensor_tensor(r, r, t, ALU.mult))

            own.mark(dve.memset(cols[:], 0.0))
            dve.memset(dtr[R:R + 1, :], 1.0)
            dve.wait_ge(s["const_in"], 16 * 20)
            dve.wait_ge(s["dve_own"], own.done())
            ts(cols[:, :, F_TAP:F_TAP + K], cw[:], 0.5, None, ALU.mult)
            ts(cols[:, :, F_BIAS], cb[:], 0.5, None, ALU.mult)
            dve.wait_ge(s["a_ready"], 2)
            ts(cols[:, :, 0:KD], alog[:], -1.0, None, ALU.mult)
            cth = sm[:].rearrange("p a b -> p (a b)")[:, 0:KH * B]
            ccf = ccol[:].rearrange("p k b -> p (k b)")
            dve.scalar_tensor_tensor(ccf, cth, 1.0, ccf, ALU.add, ALU.mult).then_inc(s["silu_c"], 1)
            dve.wait_ge(s["a_ready"], 3)
            own.link(ts(gcol[:, 1:2], gcol[:, 1:2], 1.0, None, ALU.add))
            own.link(dve.reciprocal(gcol[:, 2:3], gcol[:, 1:2]))
            own.link(ts(gcol[:, 3:4], gcol[:, 2:3], -1.0, 1.0, ALU.mult, ALU.add))
            x_in = slots("x_in", 4)
            for i in range(NT):
                dve.wait_ge(x_in[i % 4], 16 * (i // 4 + 1))
                dve.bn_stats(st[:, i % 2, 0, :], hT4[:, i % 4, 0:512])
                dve.bn_stats(st[:, i % 2, 1, :], hT4[:, i % 4, 512:1024]).then_inc(s["stat_done"], 1)
                dve.wait_ge(s["stat_done"], i + 1)
                ins = dve.bn_aggr(mv[:, i, :], st[:, i % 2].rearrange("p a b -> p (a b)"))
            own.link(ins)
            dve.wait_ge(s["silu_c"], 1)
            ts(sm[:, :, 0], mv[:, :, 1], EPS_LN, None, ALU.add).then_inc(s["var_ready"], 1)
            dve.wait_ge(s["rstd_ready"], 1)
            newton(sm[:, :, 1], sm[:, :, 0], sm[:, :, 2])
            own.link(dve.tensor_copy(mv[:, :, 1], sm[:, :, 1]))
            dve.wait_ge(s["mod_tr"], 1)
            pv = ps[2][:, 0:2 * KH * B].rearrange("p (j b) -> p b j", b=B)
            dve.tensor_copy(modc[:, :, 0:KH], pv[:, :, 0:KH])
            ts(modc[:, :, KH:2 * KH], pv[:, :, KH:2 * KH], 1.0, None, ALU.add)
            barrier(dve, 0)

            def norm(b, k):
                ts(mcur[:], modc[:, bass.ds(b, 1), :].rearrange("p o j -> p (o j)"), 1.0, None, ALU.mult)
                (ts(mvcur[:].rearrange("p q s -> p (q s)"),
                            mv[:].rearrange("p (b q) s -> p b (q s)", b=B)[:, bass.ds(b, 1), :].rearrange("p o j -> p (o j)"),
                    1.0, None, ALU.mult)).then_inc(s["mc_ready"], 1)
                dve.wait_ge(s["mc_ready"], b + 1)
                for tt in range(TT):
                    dve.wait_ge(s[f"x_in{tt}"], b * 16 + (4 * 16 + 16))
                    ts(x4[:, tt, :], x4[:, tt, :], mvcur[:, tt, 0:1], mvcur[:, tt, 1:2], ALU.subtract, ALU.mult
                       ).then_inc(s["xn_done"], 1)
                barrier(dve, k)

            def columns(n, par):
                ts(kcur[:, par, :], cols[:, bass.ds(n, 1), :].rearrange("p o j -> p (o j)"), 1.0, None, ALU.mult
                   ).then_inc(s["kcur_ready"], 1)

            def tap(b, i, par, q):
                f = b * N + i * 2 + par
                if q == 1:
                    dve.wait_ge(s["tap_done"], f + 1)
                else:
                    dve.wait_ge(s["dve_own"], own.done())
                ins = dve.scalar_tensor_tensor(acc[:, par, q:T], ps[6][:, 0:T - q], kcur[:, par, F_TAP + K - 1 - q:F_TAP + K - q],
                                               acc[:, par, q:T], ALU.mult, ALU.add)
                if q == K - 1:
                    ins.then_inc(s["conv_done"], 1)
                else:
                    own.mark(ins)

            def finish_x(b, i, par):
                f = b * N + i * 2 + par
                dve.wait_ge(s["thx_done"], f + 1)
                dve.wait_ge(s[f"xc_st{par}"], b * (8 * 16) + i * 16 + 16)
                dve.scalar_tensor_tensor(xcb[:, par, :], thx[:], 1.0, acc[:, par, :], ALU.add, ALU.mult
                                         ).then_inc(s["xc_done"], 1)

            def finish_z(b, i, par):
                f = b * N + i * 2 + par
                dve.wait_ge(s["thz_done"], f + 1)
                dve.wait_ge(s[f"z_st{par}"], b * (8 * 16) + i * 16 + 16)
                dve.scalar_tensor_tensor(szb[:, par, :], thz[:], 1.0, ps[7][:], ALU.add, ALU.mult
                                         ).then_inc(s["z_done"], 1)

            def scan(b, front, k):
                def over_states(b, i, par, g, tt):
                    grp = (b * N + i * 2 + par) * NG + g
                    dve.wait_ge(s["th_done"], grp * 4 + (CR_TH + tt + 1))
                    yv = y_sb[:, tt, g * 512:(g + 1) * 512]
                    dve.scalar_tensor_tensor(yv, ps[tt][:], kcur[:, par, F_C + tt:F_C + tt + 1], yv, ALU.mult, ALU.add
                                             ).then_inc(s["stt_done"], 1)

                def step(i, first):
                    for par in range(2):
                        pi, pp = (i, 0) if par else (i - 1, 1)
                        before = not (first and par == 0)
                        columns(i * 2 + par, par)
                        for kt in range(KD):
                            g = (b * N + i * 2 + par) * KD + kt
                            grp = (b * N + i * 2 + par) * NG + kt // 4
                            if kt % 4 == 0:
                                dve.wait_ge(s["th_done"], grp * 4 + 4)
                            dve.wait_ge(s["v_ready"], g + (CR_V + 1))
                            dve.wait_ge(s["da_ready"], g + 1)
                            dve.tensor_tensor_scan(hring[:, kt % HR, :], ps[4 + kt % 2][:], vring[:, kt % VR, :], 0.0,
                                                   ALU.mult, ALU.add).then_inc(s["scan_done"], 1)
                            if kt == 4:
                                dve.wait_ge(s["kcur_ready"], b * N + i * 2 + (N + par + 1))
                            if kt >= 4:
                                over_states(b, i, par, kt // 4 - 1, kt % 4)
                            elif before:
                                over_states(b, pi, pp, NG - 1, kt % 4)
                            if front:
                                if kt == 3 and before:
                                    finish_x(b + 1, pi, pp)
                                if kt == 5 and before:
                                    finish_z(b + 1, pi, pp)
                                if kt in (13, 14, 15):
                                    tap(b + 1, i, par, kt - 12)
                per = 4 if front else 0
                step(0, True)
                with dve.Fori(1, N // 2) as i:
                    own.enter(i - 1, per)
                    step(i, False)
                own.leave(N // 2 - 1, per)
                for tt in range(TT):
                    over_states(b, N // 2 - 1, 1, NG - 1, tt)
                if front:
                    finish_x(b + 1, N // 2 - 1, 1)
                    finish_z(b + 1, N // 2 - 1, 1)
                barrier(dve, k)

            def mix(b, k):
                for kt in range(KD):
                    dve.wait_ge(s["gt_done"], b * KD + (kt + 1))
                    dve.wait_ge(s[f"g_in{kt % 2}"], b * (8 * 32) + 32 * (kt // 2 + 1))
                    own.link(dve.scalar_tensor_tensor(acc[:, kt % 2, :], xcb[:, kt % 2, :], dsc[:, kt:kt + 1],
                                                      ps[4 + kt % 2][:], ALU.mult, ALU.add))
                    dve.scalar_tensor_tensor(u_sb[:, kt, :], acc[:, kt % 2, :], 0.5, szb[:, kt % 2, :], ALU.mult, ALU.mult
                                             ).then_inc(s["gate_done"], 1)
                dve.wait_ge(s["res_in"], b * (16 * TT) + 16 * TT)
                dve.wait_ge(s["row_in"], b * 16 + 16)
                for half in range(2):
                    for tt in range(TT):
                        dve.wait_ge(s["out_done"], b * 8 + (4 * half + tt + 1))
                        xv = hT4[:, tt, 512 * half:512 * half + 512]
                        own.link(dve.tensor_tensor(acc[:, tt % 2, :], ps[4 * half + tt][:], row[:, 512 * half:512 * half + 512], ALU.mult))
                        own.link(dve.tensor_tensor(xv, acc[:, tt % 2, :], xv, ALU.add))
                        own.link(dve.bn_stats(st2[:, tt, half, :], xv))
                        if half:
                            alone(dve)
                            dve.bn_aggr(mv2[:, tt, :], st2[:, tt].rearrange("p a b -> p (a b)")).then_inc(s["x1_done"], 1)
                barrier(dve, k)

            def ffn1(b, k):
                ts(ms[:, :, 0, 0], mv2[:, :, 1], EPS_LN, None, ALU.add).then_inc(s["f_var"], 1)
                dve.wait_ge(s["f_rstd"], b + 1)
                newton(ms[:, :, 0, 1], ms[:, :, 0, 0], ms[:, :, 0, 2])
                dve.wait_ge(s["rows_in"], b * 32 + 32)
                for tt in range(TT):
                    own.link(ts(h2[:, tt, :], hT4[:, tt, :], mv2[:, tt, 0:1], ms[:, tt, 0, 1:2], ALU.subtract, ALU.mult))
                    dve.tensor_tensor(h2[:, tt, :], h2[:, tt, :], frow[:, 0, :], ALU.mult).then_inc(s["f_mul"], 1)
                for tt in range(TT):
                    dve.wait_ge(s["f_lg"], b * TT + (tt + 1))
                    own.mark(dve.tensor_copy(Lcur[:, tt, 0:NL], ps[2 + tt][:, 0:NL]))
                dve.wait_ge(s["dve_own"], own.done())
                dve.wait_ge(s["f_sq"], b * TT + TT)
                ts(Lall[:].rearrange("p (b q) l -> p b (q l)", b=B)[:, bass.ds(b, 1), :].rearrange("p o j -> p (o j)"),
                   Lcur[:].rearrange("p q l -> p (q l)"), 1.0, None, ALU.mult)
                barrier(dve, k)

            def delta(b, k):
                dve.wait_ge(s["xp_tr"], b + 1)
                own.link(dve.tensor_copy(sA, ps[7][:, 0:TT * E].rearrange("p (q e) -> p q e", q=TT)))
                own.link(dve.tensor_tensor(sq, sA, sA, ALU.mult))
                for j, (lo, hi) in enumerate(((0, R), (R, R + N), (R + N, E))):
                    own.link(dve.tensor_reduce(ms[:, :, 0, j], sq[:, :, lo:hi], AX, ALU.add))
                    ins = ts(ms[:, :, 0, j], ms[:, :, 0, j], 1.0 / (hi - lo), EPS_RMS, ALU.mult, ALU.add)
                ins.then_inc(s["rms_sq"], 1)
                dve.wait_ge(s["rms_rs"], b + 1)
                newton(ms[:, :, 1, :], ms[:, :, 0, :], ms[:, :, 2, :])
                for tt in range(TT):
                    for j, (lo, hi) in enumerate(((0, R), (R, R + N), (R + N, E))):
                        own.mark(ts(sA[:, tt, lo:hi], sA[:, tt, lo:hi], ms[:, tt, 1, j:j + 1], None, ALU.mult))
                dve.wait_ge(s["dve_own"], own.done())
                for tt in range(TT):
                    dve.tensor_tensor(sA[:, tt, R:R + N], sA[:, tt, R:R + N], blnw[:, 0:N], ALU.mult)
                    ins = dve.tensor_tensor(cols[:, :, F_C + tt], sA[:, tt, R + N:E], blnw[:, N:2 * N], ALU.mult)
                ins.then_inc(s["bt_ready"], 1)
                for kt in range(KD):
                    dve.wait_ge(s["e_done"], b * KD + (kt + 1))
                    ts(nw2[:, kt % 2, :], e2[:, kt % 2, :], 1.0, -1.0, ALU.add, ALU.add).then_inc(s["nw_done"], 1)
                    dve.wait_ge(s["q_done"], b * KD + (kt + 1))
                    own.link(dve.scalar_tensor_tensor(dt_sb[:, kt, :], ps[kt % 4][:], 0.0, l2[:, kt % 2, :], ALU.max, ALU.add))
                    dve.tensor_tensor(u_sb[:, kt, :], dt_sb[:, kt, :], u_sb[:, kt, :], ALU.mult).then_inc(s["dt_done"], 1)
                barrier(dve, k)

            norm(0, 1)
            with dve.Fori(0, N // 2) as i:
                own.enter(i, 4)
                for par in range(2):
                    columns(i * 2 + par, par)
                    dve.wait_ge(s["kcur_ready"], i * 2 + (par + 1))
                    for q in range(1, K):
                        tap(0, i, par, q)
                    finish_x(0, i, par)
                    finish_z(0, i, par)
            own.leave(N // 2, 4)
            barrier(dve, 2)
            dve.wait_ge(s["mod_ev"], 12)
            for j in (2, 5):
                g = modr[:, j * H:(j + 1) * H]
                t0, t1 = y_sb[0:B, 2, 0:H], y_sb[0:B, 3, 0:H]
                own.link(ts(t0, g, -1.0, None, ALU.mult))
                own.link(dve.tensor_tensor(t0, t0, g, ALU.max))
                own.link(ts(t0, t0, G_MIN, None, ALU.max))
                own.link(ts(t1, g, 0.0, 2.0, ALU.is_ge, ALU.mult))
                own.link(dve.scalar_tensor_tensor(g, t1, -1.0, t0, ALU.add, ALU.mult))
            ts(modr[:, 4 * H:5 * H], modr[:, 4 * H:5 * H], 1.0, None, ALU.add).then_inc(s["mod_rows"], 1)
            barrier(dve, 3)
            delta(0, 4)
            per_loop = 2 * N + (KD + 6 * TT) + (4 + 2 * TT) + (2 + 3 + 4 + 3 * TT + KD)
            with dve.Fori(0, B - 1) as b:
                own.enter(b, per_loop)
                norm(b + 1, ph(b, 0))
                scan(b, True, ph(b, 1))
                mix(b, ph(b, 2))
                ffn1(b, ph(b, 3))
                delta(b + 1, ph(b, 4))
            own.leave(B - 1, per_loop)
            scan(B - 1, False, LAST_ROW)
            mix(B - 1, LAST_ROW + 1)
            ffn1(B - 1, LAST_ROW + 2)

            asked = [0]

            def ask(ins):
                asked[0] += 1
                ins.then_inc(s["ask"], 1)
                dve.wait_ge(s["answer"], asked[0])

            def v4(t):
                return t.rearrange("p (q i j) -> p q i j", q=NT, i=S)

            def v4t(t):
                return t.rearrange("p (q i j) -> p q j i", q=NT, i=S)

            def v3(t):
                return t.rearrange("p (q i) -> p q i", q=NT)

            def row_b(t):
                return t.rearrange("p (q i o) -> p q i o", q=NT, o=1).to_broadcast([P, NT, S, S])

            def flat(t):
                return t.rearrange("p (r j) -> p r j", j=S)

            def over_j(t):
                return t.rearrange("p (r o) -> p r o", o=1).to_broadcast([P, NT * S, S])

            def over_i(t, i):
                return t.rearrange("p (q j) -> p q j", q=NT)

            def tt_i(dst, a, v, op):
                return dve.tensor_tensor(v4(dst), v4(a), v.rearrange("p (q o j) -> p q o j", q=NT, o=1)
                                         .to_broadcast([P, NT, S, S]), op)

            def tt_j(dst, a, u, op):
                return dve.tensor_tensor(flat(dst), flat(a), over_j(u), op)

            def red_j(dst, a, op):
                return dve.tensor_reduce(dst.rearrange("p (r o) -> p r o", o=1), flat(a), AX, op)

            def red_i(dst, a, op):
                return dve.tensor_reduce(v3(dst), v4t(a), AX, op)

            ask(ts(rs0, Lall[:, :, NL], 1.0 / H, EPS_FFN, ALU.mult, ALU.add))
            newton(rs1, rs0, skv(13, NT))
            for q in range(NT):
                own.mark(dve.scalar_tensor_tensor(Lall[:, q, 0:NL], Lall[:, q, 0:NL], rs1[:, q:q + 1], base[:], ALU.mult, ALU.add))
            dve.wait_ge(s["dve_own"], own.done())
            PL = Lall[:, :, S * S:NL].rearrange("p q (g j) -> p q g j", g=2)
            pm3 = pm.rearrange("p (q g) -> p q g", q=NT)
            psu3 = psu.rearrange("p (q g) -> p q g", q=NT)
            pmb = pm.rearrange("p (q g o) -> p q g o", q=NT, o=1).to_broadcast([P, NT, 2, S])
            psb = psu.rearrange("p (q g o) -> p q g o", q=NT, o=1).to_broadcast([P, NT, 2, S])
            Pv = Pb.rearrange("p (q g j) -> p q g j", q=NT, g=2)
            Ev = Eb.rearrange("p (q g j) -> p q g j", q=NT, g=2)
            own.link(dve.tensor_reduce(pm3, PL, AX, ALU.max))
            ask(dve.tensor_tensor(Pv, PL, pmb, ALU.subtract))
            own.link(dve.tensor_reduce(psu3, Ev, AX, ALU.add))
            own.link(dve.reciprocal(psu, psu))
            own.link(dve.tensor_tensor(Hall[:, :, S * S:NL].rearrange("p q (g j) -> p q g j", g=2), Ev, psb, ALU.mult))
            own.link(ts(Zb.rearrange("p (q r) -> p q r", q=NT), Lall[:, :, 0:S * S], 1.0 / TAU, None, ALU.mult))
            own.link(red_j(Mb, Zb, ALU.max))
            ask(tt_j(Kb, Zb, Mb, ALU.subtract))
            ask(red_j(Sb_, Tb, ALU.add))
            own.link(dve.scalar_tensor_tensor(Ub, Sb_, -1.0, Mb, ALU.mult, ALU.subtract))
            own.link(tt_j(Zb, Zb, Ub, ALU.add))
            own.link(red_i(Mb, Zb, ALU.max))
            ask(tt_i(Kb, Zb, Mb, ALU.subtract))
            ask(red_i(Sb_, Tb, ALU.add))
            own.link(dve.scalar_tensor_tensor(Vb, Sb_, -1.0, Mb, ALU.mult, ALU.subtract))
            ask(tt_i(Zb, Zb, Vb, ALU.add))
            def balance(last):
                own.link(tt_i(Tb, Kb, vb, ALU.mult))
                own.link(red_j(Sb_, Tb, ALU.add))
                own.link(dve.reciprocal(ub, Sb_))
                own.link(tt_j(Tb, Kb, ub, ALU.mult))
                own.link(red_i(Sb_, Tb, ALU.add))
                last(dve.reciprocal(vb, Sb_))

            left = ITERS - 1
            for r in range(3):
                turns = left if r == 2 else REFRESH
                left -= turns
                own.link(dve.memset(vb, 1.0))
                with dve.Fori(0, turns - 1) as it:
                    own.enter(it, 6)
                    balance(own.link)
                own.leave(turns - 1, 6)
                balance(ask)
                own.link(tt_j(Zb, Zb, lnu, ALU.add))
                ask(tt_i(Zb, Zb, lnv, ALU.add))
            own.link(ts(Hall[:, :, 0:S * S], Kb.rearrange("p (q r) -> p q r", q=NT), gcol[:, 2:3], None, ALU.mult))
            own.link(ts(Hall[:, :, 0:S * S:S + 1], Hall[:, :, 0:S * S:S + 1], gcol[:, 3:4], None, ALU.add))
            barrier(dve, LAST_ROW + 3)

            mixb = dt_sb[:, 0:8].rearrange("p (a b) t -> p a (b t)", a=TT)
            xp, yb = acc, thz
            per = TT * 24 + 1
            with dve.Fori(0, B) as b:
                own.enter(b, per)
                own.link(ts(Hcur.rearrange("p q l -> p (q l)"),
                            Hall.rearrange("p (b q) l -> p b (q l)", b=B)[:, bass.ds(b, 1), :].rearrange("p o j -> p (o j)"),
                            1.0, None, ALU.mult))
                dve.wait_ge(s["t3_in0"], b * 16 + 16)
                dve.wait_ge(s["t3_in1"], b * 16 + 16)
                dve.wait_ge(s["row_in"], b * 16 + (16 * B + 16))
                for tt in range(TT):
                    xv = xp[:, tt % 2, 0:C]
                    st_ = [h2[:, tt, j * C:(j + 1) * C] for j in range(S)]
                    own.link(ts(xv, st_[0], Hcur[:, tt, 16:17], None, ALU.mult))
                    for j in range(1, S):
                        ins = dve.scalar_tensor_tensor(xv, st_[j], Hcur[:, tt, 16 + j:17 + j], xv, ALU.mult, ALU.add)
                        if j < S - 1:
                            own.link(ins)
                        else:
                            ins.then_inc(s["t3_pre"], 1)
                    mo = [mixb[:, tt, i * C:(i + 1) * C] for i in range(S)]
                    for i in range(S):
                        own.mark(ts(mo[i], st_[0], Hcur[:, tt, 4 * i:4 * i + 1], None, ALU.mult))
                    for j in range(1, S):
                        dve.wait_ge(s["dve_own"], own.done())
                        for i in range(S):
                            own.mark(dve.scalar_tensor_tensor(mo[i], st_[j], Hcur[:, tt, 4 * i + j:4 * i + j + 1], mo[i], ALU.mult, ALU.add))
                    dve.wait_ge(s["dve_own"], own.done())
                    dve.wait_ge(s["t3_y"], b * TT + (tt + 1))
                    for i in range(S):
                        own.mark(dve.scalar_tensor_tensor(mo[i], ps[2 + tt % 2][:, 0:C], Hcur[:, tt, 20 + i:21 + i], mo[i], ALU.mult, ALU.add))
                    dve.wait_ge(s["dve_own"], own.done())
                    own.link(dve.tensor_tensor(mixb[:, tt, :], mixb[:, tt, :], row[:], ALU.mult))
                    dve.tensor_tensor(hT4[:, tt, :], hT4[:, tt, :], mixb[:, tt, :], ALU.add).then_inc(s["t3_mix"], 1)
            own.leave(B, per)


def kernel(**inputs):
    import numpy as np
    import concourse.bacc as bacc
    from concourse.bass_utils import run_bass_kernel_spmd as run

    a = {k: np.asarray(v) for k, v in inputs.items()}

    def cols(w, k):
        return w.reshape(k, P, *w.shape[1:]).swapaxes(0, 1)

    att = {k[len("L0_attn_"):]: v for k, v in a.items() if k.startswith("L0_attn_")}
    ffn = {k[len("L0_ffn_"):]: v for k, v in a.items() if k.startswith("L0_ffn_")}
    arrays = {
        "x": att["hidden_states"].reshape(B, TT, P, H),
        "ident": np.eye(P, dtype=np.float32),
        "w_in": att["in_proj_w"].reshape(KH, P, 2 * KD, P).transpose(2, 1, 0, 3),
        "conv_w": cols(att["conv_w"], KD),
        "conv_b": cols(att["conv_b"], KD),
        "x_proj": cols(att["x_proj_w"].T, KD),
        "dt_proj": att["dt_proj_w"].T,
        "dt_bias": att["dt_bias"].reshape(1, DIN),
        "A_log": att["A_log"].reshape(KD, P, N).transpose(1, 2, 0),
        "D_param": cols(att["D_param"], KD),
        "w_out": att["out_proj_w"].T.reshape(KD // 2, 2, P, 2, 512).transpose(3, 0, 2, 1, 4).reshape(KD, P, 2 * 512),
        "dt_ln": att["dt_ln_w"].reshape(R, 1),
        "B_ln": att["B_ln_w"],
        "C_ln": att["C_ln_w"],
        "W_res": cols(ffn["W_res"].T, KH),
        "W_pre": cols(ffn["W_pre"].T, KH),
        "W_post": cols(ffn["W_post"].T, KH),
        "res_base": ffn["H_res_base"].reshape(S * S),
        "pre_base": ffn["H_pre_base"],
        "post_base": ffn["H_post_base"],
        "gate": ffn["gate"],
        "W_branch": cols(ffn["W_branch"], C // P),
        "c_cols": cols(a["L0_c"].T, KH),
        "w_mod": a["L0_wmod"].reshape(KH, P, 12, 512).transpose(2, 1, 0, 3),
    }
    nc = bacc.Bacc("TRN2", target_bir_lowering=False, num_devices=1)
    args, maps = {}, {}
    for name, v in arrays.items():
        v = np.ascontiguousarray(v)
        maps[f"in_{name}"] = v
        args[name] = nc.dram_tensor(f"in_{name}", v.shape, mybir.dt.from_np(v.dtype), kind="ExternalInput").ap()
    out = nc.dram_tensor("out_y", (B, TT, P, H), F32, kind="ExternalOutput").ap()
    build(nc, out=out, **args)
    r = run(nc, [maps], core_ids=[0])
    return r.results[0]["out_y"].reshape(B, T, H)
```

```python
from contextlib import ExitStack

import concourse.bass as bass
from concourse import mybir

F32 = mybir.dt.float32
ALU = mybir.AluOpType
ACT = mybir.ActivationFunctionType
AX = mybir.AxisListType.X

P = 128
B, T, H = 4, 512, 1024
DIN, N, K, R = 2048, 16, 4, 64
TT = T // P
KH = H // P
KD = DIN // P
NT = B * TT
E = R + 2 * N
S, C = 4, 256
NL = S * S + 2 * S
NG = KD // 4
ITERS, REFRESH = 50, 16
TAU = 0.1
EPS_LN, EPS_RMS, EPS_FFN = 1e-5, 1e-6, 1.1920929e-07
G_MIN = 0.25

STEP = 4
VR = 4
HR = 8
F_TAP, F_BIAS, F_C, F_W = 16, 20, 21, 25
CR_V, CR_SCAN, CR_TH, CR_STT, CR_PROJ = 32, 8, 8, 4, 4


class Steps:

    def __init__(self, eng, sem):
        self.eng, self.sem, self.base, self.n, self.outer = eng, sem, 0, 0, []

    def mark(self, ins):
        ins.then_inc(self.sem, 1)
        self.n += 1

    def done(self):
        return self.base + self.n

    def link(self, ins):
        self.mark(ins)
        self.eng.wait_ge(self.sem, self.done())

    def enter(self, turn, per):
        start = self.done()
        self.outer.append((start, self.base))
        self.base, self.n = start + turn * per, 0
        self.top = self.base

    def leave(self, turns, per):
        start, _ = self.outer.pop()
        self.base, self.n = start + turns * per, 0


def build(nc, x, ident, w_in, conv_w, conv_b, x_proj, dt_proj, dt_bias, A_log, D_param, w_out,
          dt_ln, B_ln, C_ln, W_res, W_pre, W_post, res_base, pre_base, post_base, gate, W_branch,
          c_cols, w_mod, out):
    z_s = nc.dram_tensor("z_s", (B, KD, P, T), F32).ap()
    xc_s = nc.dram_tensor("xc_s", (B, KD, P, T), F32).ap()
    b_s = nc.dram_tensor("b_s", (B, N, T), F32).ap()
    mod_s = nc.dram_tensor("mod_s", (B, 6 * H), F32).ap()
    x1_s = nc.dram_tensor("x1_s", (B, TT, P, H), F32).ap()
    h2_s = nc.dram_tensor("h2_s", (B, TT, P, H), F32).ap()

    with ExitStack() as ctx:
        def sb(name, shape):
            return ctx.enter_context(nc.sbuf_tensor(name, shape, F32))

        def sem(name):
            return ctx.enter_context(nc.semaphore(name))

        dt_sb = sb("dt_sb", [P, KD, T])
        u_sb = sb("u_sb", [P, KD, T])
        y_sb = sb("y_sb", [P, TT, DIN])
        hT = sb("hT", [P, KH, T])
        hring = sb("hring", [P, HR, T])
        wring = sb("wring", [P, 4, KH, P])
        vring = sb("vring", [P, VR, T])
        bbc = sb("bbc", [P, 2, T])
        acc = sb("acc", [P, 2, T])
        thx = sb("thx", [P, T])
        thz = sb("thz", [P, T])
        xcb = sb("xcb", [P, 2, T])
        szb = sb("szb", [P, 2, T])
        row = sb("row", [P, H])
        idn = sb("idn", [P, P])
        cols = sb("cols", [P, N + 1, F_W])
        kcur = sb("kcur", [P, 2, F_W])
        alog = sb("alog", [P, N, KD])
        cw = sb("cw", [P, KD, K])
        cb = sb("cb", [P, KD])
        dsc = sb("dsc", [P, KD])
        xpw = sb("xpw", [P, KD, E])
        dpw = sb("dpw", [R + 1, DIN])
        dtln = sb("dtln", [R, 1])
        blnw = sb("blnw", [P, 2 * N])
        wcat = sb("wcat", [P, KH, NL])
        base = sb("base", [P, NL])
        gcol = sb("gcol", [P, 4])
        wbr = sb("wbr", [P, C // P, C])
        ccol = sb("ccol", [P, KH, B])
        modc = sb("modc", [P, B, 2 * KH])
        mcur = sb("mcur", [P, 2 * KH])
        mv = sb("mv", [P, NT, 2])
        mvcur = sb("mvcur", [P, TT, 2])
        st = sb("st", [P, 2, 2, 6])
        sm = sb("sm", [P, NT, 4])
        mv2 = sb("mv2", [P, TT, 2])
        mv2all = sb("mv2all", [P, NT, 2])
        st2 = sb("st2", [P, TT, 2, 6])
        Lcur = sb("Lcur", [P, TT, NL + 1])
        Lall = sb("Lall", [P, NT, NL + 1])
        ms = sb("ms", [P, TT, 4, 3])
        dtr = sb("dtr", [R + 1, T])

        ps = [ctx.enter_context(nc.psum_tensor(f"bank{i}", [P, T], F32)) for i in range(8)]

        names = """phase passed const_in modw0 modw1 modw2 modw3 mod_mm mod_tr mod_ev mod_rows mod_st silu_c modc_ready
            x_in0 x_in1 x_in2 x_in3 stat_done var_ready rstd_ready a_ready g_ready
            xn_done nt_done ne_done mc_ready
            w_in0 w_in1 w_in2 w_in3 proj_done tap_done conv_done thx_done xc_done thz_done z_done
            xc_st0 xc_st1 z_st0 z_st1 kcur_ready b_in0 b_in1 v_ready da_ready scan_done th_done stt_done
            g_in0 g_in1 gt_done gate_done wo_in0 wo_in1 wo_in2 wo_in3 wo_done out_done row_in rows_in
            row_tail x1_done x1_st res_in half_done f_var f_rstd f_mul f_add f_sq f_tr f_ev f_lg f_lv f_lrow h2_st
            u_in0 u_in1 u_in2 u_in3 xp_done xp_ev xp_tr rms_sq rms_rs bt_ready n_tr n_ev bs_st dt_mm e_done
            nw_done q_done dt_done ask answer
            f_in0 f_in1 r_in0 r_in1 t3_in0 t3_in1 t3_pre t3_cur t3_first t3_gb t3_tr t3_ev t3_y t3_mix t3_st0 t3_st1 act_own dve_own""".split()
        s = {n: sem(n) for n in names}

        def slots(prefix, n):
            return [s[f"{prefix}{i}"] for i in range(n)]

        def barrier(eng, k):
            alone(eng, k)
            eng.drain().then_inc(s["phase"], 1)
            eng.wait_ge(s["phase"], 5 * (k + 1))
            alone(eng, k)

        def alone(eng, k=None):
            if not isinstance(k, int):
                eng.sem_inc(s["passed"], 1)

        def ph(b, i):
            return b * 2 + (4 + i)

        TAIL = 4 + 2 * B

        x4 = hring[:].rearrange("p (q j) t -> p q (j t)", q=TT)
        hT4 = hT[:].rearrange("p (q j) t -> p q (j t)", q=TT)
        h2 = [y_sb[:, 2 * r:2 * r + 2, :].rearrange("p a (b h) -> p (a b) h", h=H) for r in range(2)]
        x1 = [hT4, x4]
        frow = [wring[:, 2 * r:2 * r + 2].rearrange("p q k c -> p q (k c)") for r in range(2)]
        gbrow = [wring[:, r].rearrange("p k c -> p (k c)") for r in range(2)]
        h2T = vring[:].rearrange("p (r a) (k c) -> p r (a k) c", r=2, c=P)
        trash = acc[:].rearrange("p a t -> p (a t)")
        modr = u_sb[0:B].rearrange("p k t -> p (k t)")[:, 0:2 * H]
        modg = wring[0:B].rearrange("p q k c -> p (q k c)")
        xres = vring
        prod = hring
        bT = thx[0:N, :]
        sA = bbc[:, 0, 0:TT * E].rearrange("p (q e) -> p q e", q=TT)
        sq = bbc[:, 1, 0:TT * E].rearrange("p (q e) -> p q e", q=TT)
        ssmT = thz[0:E, :]
        e3 = [hring[:, 2 + i, :] for i in range(3)]
        l3 = [hring[:, 5 + i, :] for i in range(3)]
        c3 = [xcb[:, 0, :], xcb[:, 1, :], szb[:, 0, :]]

        def gated(kt, tt):
            return y_sb[:, tt, kt * P:(kt + 1) * P]

        MOD_ORDER = [0, 1, 2, 3, 4, 5, 10, 11, 6, 7, 8, 9]
        MOD_SLOT = [0, 1, 2, 0, 2, 3, 0, 1, 2, 3, 2, 3]
        mod_slots = [dt_sb[:, 0:8], dt_sb[:, 8:16]] + [
            y_sb[:, 2 * r:2 * r + 2].rearrange("p a (b t) -> p (a b) t", t=T) for r in range(2)]
        MOD_EARLY = 4

        def mod_w(m):
            return mod_slots[MOD_SLOT[m]]

        def mod_load(m):
            return MOD_SLOT[:m + 1].count(MOD_SLOT[m])

        def mod_before(m):
            return max((i for i in range(m) if MOD_SLOT[i] == MOD_SLOT[m]), default=None)

        def mod_row(b, j):
            return mod_s[bass.ds(b, 1), j * H:(j + 1) * H].rearrange("o h -> (o h)").partition_broadcast(P)

        mixb = dt_sb[:, 0:8].rearrange("p (a b) t -> p a (b t)", a=TT)

        def skv(i, n):
            return dt_sb[:, i, 0:n]
        Zb, Kb, Tb = skv(0, NT * 16), skv(1, NT * 16), skv(2, NT * 16)
        Ub, Vb, Mb, Sb_ = skv(3, NT * S), skv(4, NT * S), skv(5, NT * S), skv(6, NT * S)
        ub, vb = skv(7, NT * S), skv(8, NT * S)
        Pb, Eb = skv(9, NT * 8), skv(10, NT * 8)
        rs0, rs1 = skv(11, NT), skv(12, NT)
        pm, psu = skv(13, NT * 2), skv(14, NT * 2)
        lnu, lnv = skv(15, NT * S), Mb
        Hall = u_sb[:, 0, 0:NT * NL].rearrange("p (q l) -> p q l", q=NT)
        Hcur = u_sb[:, 1, 0:TT * NL].rearrange("p (q l) -> p q l", q=TT)

        sink_requests = [[(rs1, rs0, ACT.Ln, 1.0), (rs1, rs1, ACT.Exp, -0.5)],
                         [(Eb, Pb, ACT.Exp, 1.0)],
                         [(Tb, Kb, ACT.Exp, 1.0)], [(Sb_, Sb_, ACT.Ln, 1.0)],
                         [(Tb, Kb, ACT.Exp, 1.0)], [(Sb_, Sb_, ACT.Ln, 1.0)],
                         [(Kb, Zb, ACT.Exp, 1.0)]]
        sink_requests += [[(lnu, ub, ACT.Ln, 1.0), (lnv, vb, ACT.Ln, 1.0)], [(Kb, Zb, ACT.Exp, 1.0)]] * 3

        block = ctx.enter_context(nc.Block())

        @block.sync
        def _(sp):
            sp.sem_inc(s["xc_st0"], 16)
            sp.sem_inc(s["xc_st1"], 16)
            sp.sem_inc(s["z_st0"], 16)
            sp.sem_inc(s["z_st1"], 16)
            sp.sem_inc(s["t3_st0"], 16)
            sp.sem_inc(s["t3_st1"], 16)
            sp.sem_inc(s["row_tail"], 2)

            consts = [(idn[:], ident), (ccol[:], c_cols), (alog[:], A_log), (cw[:], conv_w), (cb[:], conv_b),
                      (dsc[:], D_param), (xpw[:], x_proj), (dpw[0:R, :], dt_proj), (dpw[R:R + 1, :], dt_bias),
                      (dtln[:], dt_ln), (blnw[:, 0:N], B_ln.partition_broadcast(P)),
                      (blnw[:, N:2 * N], C_ln.partition_broadcast(P)),
                      (wcat[:, :, 0:S * S], W_res), (wcat[:, :, S * S:S * S + S], W_pre),
                      (wcat[:, :, S * S + S:NL], W_post),
                      (base[:, 0:S * S], res_base.partition_broadcast(P)),
                      (base[:, S * S:S * S + S], pre_base.partition_broadcast(P)),
                      (base[:, S * S + S:NL], post_base.partition_broadcast(P)),
                      (gcol[:, 0:1], gate.partition_broadcast(P)), (wbr[:], W_branch)]
            for dst, src in consts:
                sp.dma_start(dst, src).then_inc(s["const_in"], 16)

            modw = slots("modw", 4)

            def load_mod(m):
                if mod_before(m) is not None:
                    sp.wait_ge(s["mod_mm"], mod_before(m) + 1)
                sp.dma_start(mod_w(m), w_mod[MOD_ORDER[m]]).then_inc(modw[MOD_SLOT[m]], 16)

            for c in range(3):
                load_mod(c)
            x_in = slots("x_in", 4)
            for i in range(NT):
                if i >= 4:
                    sp.wait_ge(s["stat_done"], i - 3)
                sp.dma_start(hT4[:, i % 4, :], x[i // TT, i % TT]).then_inc(x_in[i % 4], 16)
            load_mod(3)
            barrier(sp, 0)

            def norm(b):
                for tt in range(TT):
                    sp.dma_start(x4[:, tt, :], x[bass.ds(b, 1), tt].rearrange("o p h -> (o p) h")
                                 ).then_inc(x_in[tt], 16)

            w_slot = slots("w_in", 4)
            xc_st, z_st = slots("xc_st", 2), slots("z_st", 2)
            b_in = slots("b_in", 2)

            def dram3(t, b, n):
                return t[bass.ds(b, 1), bass.ds(n, 1)].rearrange("o q p t -> (o q p) t")

            def load_w(b, i, par):
                f = b * N + i * 2 + par
                sp.wait_ge(s["proj_done"], f * 2 + 1)
                sp.dma_start(wring[:, 2 * par], w_in[bass.ds(i * 2 + par, 1)].rearrange("o p k c -> (o p) k c")
                             ).then_inc(w_slot[2 * par], 16)
                sp.wait_ge(s["proj_done"], f * 2 + 2)
                sp.dma_start(wring[:, 2 * par + 1], w_in[bass.ds(i * 2 + (KD + par), 1)].rearrange("o p k c -> (o p) k c")
                             ).then_inc(w_slot[2 * par + 1], 16)

            def store_front(b, i, par):
                f = b * N + i * 2 + par
                sp.wait_ge(s["xc_done"], f + 3)
                sp.dma_start(dram3(xc_s, b, i * 2 + par), xcb[:, par]).then_inc(xc_st[par], 16)
                sp.wait_ge(s["z_done"], f + 2)
                sp.dma_start(dram3(z_s, b, i * 2 + par), szb[:, par]).then_inc(z_st[par], 16)

            def load_b(b, i, par):
                n = b * N + i * 2 + par
                sp.wait_ge(s["v_ready"], n * KD + KD)
                sp.dma_start(bbc[:, par], b_s[bass.ds(b, 1), bass.ds(i * 2 + par, 1)]
                             .rearrange("o n t -> (o n t)").partition_broadcast(P)).then_inc(b_in[par], 16)

            def stores_end(b):
                for par in range(2):
                    sp.wait_ge(xc_st[par], b * (8 * 16) + 9 * 16)
                    sp.wait_ge(z_st[par], b * (8 * 16) + 9 * 16)

            def scan(b, front, k):
                def step(i, first):
                    for par in range(2):
                        if front:
                            load_w(b + 1, i, par)
                        if not first:
                            load_b(b, i, par)
                        if front and not first:
                            store_front(b + 1, i - 1, par)
                step(0, True)
                with sp.Fori(1, N // 2) as i:
                    step(i, False)
                if front:
                    for par in range(2):
                        store_front(b + 1, N // 2 - 1, par)
                    stores_end(b + 1)
                barrier(sp, k)

            g_in, wo_in = slots("g_in", 2), slots("wo_in", 4)

            u_in = slots("u_in", 4)

            def middle(b, k, gate=True, delta=True, ln=True):
                def load_gate(kt):
                    sp.wait_ge(s["gate_done"], b * KD + (kt + 1))
                    sp.dma_start(xcb[:, kt % 2], xc_s[bass.ds(b, 1), kt].rearrange("o p t -> (o p) t")
                                 ).then_inc(g_in[kt % 2], 16)
                    sp.dma_start(szb[:, kt % 2], z_s[bass.ds(b, 1), kt].rearrange("o p t -> (o p) t")
                                 ).then_inc(g_in[kt % 2], 16)

                def load_wo(t):
                    sp.wait_ge(s["wo_done"], b * KD + (t + 1))
                    sp.dma_start(wring[:, t % 4].rearrange("p k c -> p (k c)"), w_out[t]
                                 ).then_inc(wo_in[t % 4], 16)

                def half_rows(t, tt, half):
                    return t[bass.ds(b, 1), tt].rearrange("o p h -> (o p) h")[:, 512 * half:512 * half + 512]

                def load_residual(half):
                    for tt in range(TT):
                        sp.dma_start(xres[:, tt, :], half_rows(x, tt, half)).then_inc(s["res_in"], 16)

                def store_x1(half):
                    for tt in range(TT):
                        sp.wait_ge(s["x1_done"], b * 8 + (4 * half + tt + 1))
                        sp.dma_start(half_rows(x1_s, tt, half), xres[:, tt, :]).then_inc(s["x1_st"], 16)
                    sp.wait_ge(s["x1_st"], b * 128 + 64 * (half + 1))
                    alone(sp)

                def load_u(q):
                    sp.dma_start(u_sb[:, 4 * q:4 * q + 4, :],
                                 xc_s[bass.ds(b + 1, 1), 4 * q:4 * q + 4].rearrange("o k p t -> (o p) k t")
                                 ).then_inc(u_in[q], 16)

                for kt in range(KD):
                    if gate:
                        load_gate(kt)
                    if delta and kt % 4 == 1:
                        load_u(kt // 4)
                    if gate and kt % 2:
                        load_wo(kt // 2)
                    if ln and kt == 5:
                        norm(b + 2)
                if gate:
                    sp.dma_start(row[:], mod_row(b, 2)).then_inc(s["row_in"], 16)
                    load_residual(0)
                    for t in range(8, 12):
                        load_wo(t)
                if not gate:
                    load_mod(8)
                    load_mod(9)
                if delta:
                    sp.wait_ge(s["n_ev"], b * 2 + 4)
                    sp.dma_start(b_s[bass.ds(b + 1, 1)].rearrange("o n t -> (o n) t"), bT).then_inc(s["bs_st"], 16)
                    sp.wait_ge(s["bs_st"], b * 16 + 32)
                if gate:
                    store_x1(0)
                    load_residual(1)
                    for t in range(12, KD):
                        load_wo(t)
                    store_x1(1)
                if not gate:
                    load_mod(10)
                    load_mod(11)
                    sp.wait_ge(s["mod_ev"], 12)
                    sp.wait_ge(s["mod_rows"], 2)
                    sp.dma_start(mod_s[:, 2 * H:6 * H], modg).then_inc(s["mod_st"], 16)
                    sp.wait_ge(s["mod_st"], 16)
                if delta:
                    load_b(b + 1, 0, 0)
                    load_b(b + 1, 0, 1)
                barrier(sp, k)

            norm(0)
            barrier(sp, 1)

            def front_step(i, first):
                for par in range(2):
                    load_w(0, i, par)
                    if not first:
                        store_front(0, i - 1, par)
            front_step(0, True)
            for m, (lo, hi) in enumerate(((1, 2), (2, 4), (4, 6), (6, N // 2))):
                load_mod(MOD_EARLY + m)
                with sp.Fori(lo, hi) as i:
                    front_step(i, False)
            for par in range(2):
                store_front(0, N // 2 - 1, par)
            stores_end(0)
            barrier(sp, 2)

            middle(-1, 3, gate=False)
            with sp.Fori(0, B - 2) as b:
                scan(b, True, ph(b, 0))
                middle(b, ph(b, 1))
            scan(B - 2, True, ph(B - 2, 0))
            middle(B - 2, ph(B - 2, 1), ln=False)
            scan(B - 1, False, ph(B - 1, 0))
            middle(B - 1, ph(B - 1, 1), delta=False, ln=False)

            f_in, r_in = slots("f_in", 2), slots("r_in", 2)

            def row_tiles(t, b):
                return t[bass.ds(b, 1)].rearrange("o q p h -> (o p) q h")

            with sp.Fori(0, B // 2) as i:
                for r in range(2):
                    b = i * 2 + r
                    sp.wait_ge(s["row_tail"], b + 1)
                    sp.dma_start(x1[r], row_tiles(x1_s, b)).then_inc(f_in[r], 16)
                    sp.dma_start(frow[r][:, 0, :], mod_row(b, 4)).then_inc(r_in[r], 16)
                    sp.dma_start(frow[r][:, 1, :], mod_row(b, 3)).then_inc(r_in[r], 16)
                for r in range(2):
                    b = i * 2 + r
                    for tt in range(TT):
                        sp.wait_ge(s["f_add"], b * TT + (tt + 1))
                        sp.dma_start(h2_s[bass.ds(b, 1), tt].rearrange("o p h -> (o p) h"), h2[r][:, tt, :]
                                     ).then_inc(s["h2_st"], 16)
                    sp.wait_ge(s["h2_st"], b * (16 * TT) + 16 * TT)
                    sp.sem_inc(s["row_tail"], 1)
            barrier(sp, TAIL)

            sp.sem_inc(s["phase"], 1)
            t3_in, t3_st = slots("t3_in", 2), slots("t3_st", 2)
            with sp.Fori(0, B // 2) as i:
                for r in range(2):
                    b = i * 2 + r
                    sp.wait_ge(t3_st[r], i * (16 * TT) + 16)
                    sp.dma_start(h2[r], row_tiles(h2_s, b)).then_inc(t3_in[r], 16)
                    sp.dma_start(x1[r], row_tiles(x1_s, b)).then_inc(t3_in[r], 16)
                    sp.dma_start(gbrow[r], mod_row(b, 5)).then_inc(t3_in[r], 16)
                for r in range(2):
                    b = i * 2 + r
                    for tt in range(TT):
                        sp.wait_ge(s["t3_mix"], b * TT + (tt + 5))
                        sp.dma_start(out[bass.ds(b, 1), tt].rearrange("o p h -> (o p) h"), x1[r][:, tt, :]
                                     ).then_inc(t3_st[r], 16)
            for r in range(2):
                sp.wait_ge(t3_st[r], 16 + 16 * TT * (B // 2))

        @block.tensor
        def _(pe):
            pe.wait_ge(s["const_in"], 16 * 20)
            for name, credit in (("proj_done", CR_PROJ), ("th_done", CR_TH), ("wo_done", 4), ("f_lg", 2)):
                pe.sem_inc(s[name], credit)
            pe.wait_ge(s["silu_c"], 1)
            modw = slots("modw", 4)

            def mod_turn(m):
                pe.wait_ge(modw[MOD_SLOT[m]], 16 * mod_load(m))
                if m >= 2:
                    pe.wait_ge(s["mod_ev"], m - 1)
                for k in range(KH):
                    mm = pe.matmul(ps[4 + m % 2][0:B, :], ccol[:, k, :], mod_w(m)[:, k, :], start=(k == 0), stop=(k == KH - 1))
                mm.then_inc(s["mod_mm"], 1)

            for m in range(MOD_EARLY):
                mod_turn(m)
            pe.wait_ge(s["mod_ev"], 4)
            for j in range(2 * KH):
                mm = pe.transpose(ps[2][:, j * B:(j + 1) * B], modr[:, j * P:(j + 1) * P], idn[0:B, 0:B])
            mm.then_inc(s["mod_tr"], 1)
            barrier(pe, 0)

            def turn_ln(b, h, bank, ring):
                pe.wait_ge(s["ne_done"], b * KH + (h + 5 - ring))
                for tt in range(TT):
                    if h == 0:
                        pe.wait_ge(s["xn_done"], b * TT + (tt + 1))
                    mm = pe.transpose(ps[bank][:, tt * P:(tt + 1) * P], x4[:, tt, h * P:(h + 1) * P], idn[:])
                mm.then_inc(s["nt_done"], 1)

            w_slot = slots("w_in", 4)

            def project(b, i, par, which, k0, k1):
                f = b * N + i * 2 + par
                if k0 == 0:
                    pe.wait_ge(w_slot[2 * par + which], b * (8 * 16) + i * 16 + 16)
                    pe.wait_ge(s["z_done" if which else "conv_done"], f + 1)
                for k in range(k0, k1):
                    mm = pe.matmul(ps[6 + which][:], wring[:, 2 * par + which, k, :], hT[:, k, :],
                                   start=(k == 0), stop=(k == KH - 1))
                if k1 == KH:
                    mm.then_inc(s["proj_done"], 1)

            def scan(b, front, k):
                def step(i):
                    for par in range(2):
                        for g in range(NG):
                            grp = (b * N + i * 2 + par) * NG + g
                            pe.wait_ge(s["scan_done"], grp * 4 + (CR_SCAN + 4))
                            for tt in range(TT):
                                pe.wait_ge(s["stt_done"], grp * 4 + (tt + 1))
                                for j in range(4):
                                    mm = pe.transpose(ps[tt][:, j * P:(j + 1) * P],
                                                      hring[:, (4 * g + j) % HR, tt * P:(tt + 1) * P], idn[:])
                                mm.then_inc(s["th_done"], 1)
                                if front:
                                    k0 = 4 * (g % 2) + tt
                                    project(b + 1, i, par, g // 2, k0, k0 + 1)
                with pe.Fori(0, N // 2) as i:
                    step(i)
                barrier(pe, k)

            wo_in = slots("wo_in", 4)

            def middle(b, k, gate=True, delta=True, ln=True):
                def turn(kt):
                    pe.wait_ge(s["gate_done"], b * KD + (kt + 1))
                    for tt in range(TT):
                        mm = pe.transpose(ps[4 + kt % 2][:, tt * P:(tt + 1) * P], y_sb[:, tt, kt * P:(kt + 1) * P], idn[:])
                    mm.then_inc(s["gt_done"], 1)

                def out_products(half, kt, tiles=range(TT)):
                    t = half * 8 + kt // 2
                    if kt % 2 == 0:
                        pe.wait_ge(wo_in[t % 4], b * 64 + 16 * (t // 4 + 1))
                    for tt in tiles:
                        mm = pe.matmul(ps[4 * half + tt][:], gated(kt, tt),
                                       wring[:, t % 4].rearrange("p k c -> p (k c)")[:, (kt % 2) * 512:(kt % 2) * 512 + 512],
                                       start=(kt == 0), stop=(kt == KD - 1))
                        if kt == KD - 1:
                            mm.then_inc(s["out_done"], 1)
                    if kt == KD - 1 and TT - 1 in tiles:
                        pe.drain().then_inc(s["wo_done"], 1)
                    elif kt % 2 and TT - 1 in tiles:
                        mm.then_inc(s["wo_done"], 1)

                def turn_norms():
                    pe.wait_ge(s["bt_ready"], b + 2)
                    alone(pe)
                    for tt in range(TT):
                        mm = pe.transpose(ps[6][0:R, tt * P:(tt + 1) * P], sA[:, tt, 0:R], idn[:])
                    for tt in range(TT):
                        mm = pe.transpose(ps[7][0:N, tt * P:(tt + 1) * P], sA[:, tt, R:R + N], idn[:])
                    mm.then_inc(s["n_tr"], 1)

                def dt_product(kt):
                    if kt == 0:
                        pe.wait_ge(s["n_ev"], b * 2 + 4)
                    if kt < 4 and gate:
                        pe.wait_ge(s["half_done"], b * TT + (kt + 1))
                    pe.wait_ge(s["dt_done"], b * KD + (KD + kt + 1))
                    pe.matmul(ps[kt % 4][:], dpw[:, kt * P:(kt + 1) * P], dtr[:], start=True, stop=True
                              ).then_inc(s["dt_mm"], 1)

                if gate:
                    turn(0)
                    turn(1)
                else:
                    mod_turn(4)
                    mod_turn(5)
                for kt in range(KD):
                    if delta:
                        if kt % 4 == 0:
                            pe.wait_ge(s[f"u_in{kt // 4}"], b * 16 + 32)
                        mm = pe.matmul(ps[6][0:E, :], xpw[:, kt, :], u_sb[:, kt, :], start=(kt == 0), stop=(kt == KD - 1))
                        if kt == KD - 1:
                            mm.then_inc(s["xp_done"], 1)
                    if gate and kt + 2 < KD:
                        turn(kt + 2)
                    if gate:
                        pe.wait_ge(s["gate_done"], b * KD + (kt + 3))
                        out_products(0, kt)
                    if ln and 7 <= kt < 7 + KH:
                        turn_ln(b + 2, kt - 7, 7, 1)
                if delta:
                    pe.wait_ge(s["xp_ev"], b + 2)
                    if ln:
                        pe.wait_ge(s["ne_done"], b * KH + (3 * KH + 4))
                    for tt in range(TT):
                        mm = pe.transpose(ps[7][:, tt * E:(tt + 1) * E], ssmT[:, tt * P:(tt + 1) * P], idn[0:E, 0:E])
                    mm.then_inc(s["xp_tr"], 1)
                if gate:
                    split = KD // 2
                    for kt in range(split):
                        out_products(1, kt, range(TT // 2))
                    if delta:
                        turn_norms()
                        pe.wait_ge(s["n_ev"], b * 2 + 4)
                        alone(pe)
                    for kt in range(split):
                        out_products(1, kt, range(TT // 2, TT))
                        if delta:
                            dt_product(kt)
                    count = 0
                    for tt in range(TT):
                        for kt in range(split, KD):
                            out_products(1, kt, [tt])
                            count += 1
                            if delta and count % 3 == 0 and count <= 3 * split:
                                dt_product(split + count // 3 - 1)
                else:
                    mod_turn(6)
                    turn_norms()
                    mod_turn(7)
                    for kt in range(KD):
                        dt_product(kt)
                        if kt in (2, 5, 8, 11):
                            mod_turn(8 + kt // 3)
                barrier(pe, k)

            for h in range(KH):
                turn_ln(0, h, h % 4, 4)
            barrier(pe, 1)
            with pe.Fori(0, N // 2) as i:
                for par in range(2):
                    for which in range(2):
                        project(0, i, par, which, 0, KH)
            barrier(pe, 2)
            middle(-1, 3, gate=False)
            with pe.Fori(0, B - 2) as b:
                scan(b, True, ph(b, 0))
                middle(b, ph(b, 1))
            scan(B - 2, True, ph(B - 2, 0))
            middle(B - 2, ph(B - 2, 1), ln=False)
            scan(B - 1, False, ph(B - 1, 0))
            middle(B - 1, ph(B - 1, 1), delta=False, ln=False)

            with pe.Fori(0, B // 2) as i:
                for r in range(2):
                    for tt in range(TT):
                        n = (i * 2 + r) * TT + tt
                        pe.wait_ge(s["f_add"], n + 1)
                        for h in range(KH):
                            if h % 4 == 0:
                                pe.wait_ge(s["f_ev"], n * 2 + (h // 4 + 1))
                            mm = pe.transpose(ps[h // 4][:, (h % 4) * P:(h % 4 + 1) * P], h2[r][:, tt, h * P:(h + 1) * P], idn[:])
                            if h % 4 == 3:
                                mm.then_inc(s["f_tr"], 1)
                        pe.wait_ge(s["f_ev"], n * 2 + 4)
                        pe.wait_ge(s["f_lv"], n + 1)
                        for h in range(KH):
                            mm = pe.matmul(ps[2 + tt][:, 0:NL], h2T[:, tt % 2, h, :], wcat[:, h, :],
                                           start=(h == 0), stop=(h == KH - 1))
                        mm.then_inc(s["f_lg"], 1)
            barrier(pe, TAIL)
            barrier(pe, TAIL + 1)
            with pe.Fori(0, B) as b:
                for tt in range(TT):
                    pe.wait_ge(s["t3_pre"], b * TT + (tt + 1))
                    for j in range(2):
                        mm = pe.transpose(ps[tt % 2][:, j * P:(j + 1) * P], acc[:, tt % 2, j * P:(j + 1) * P], idn[:])
                    mm.then_inc(s["t3_tr"], 1)
                    pe.wait_ge(s["t3_ev"], b * TT + (tt + 1))
                    for j in range(2):
                        mm = pe.matmul(ps[2 + tt % 2][:, 0:C], thx[:, (tt % 2) * C + j * P:(tt % 2) * C + (j + 1) * P],
                                       wbr[:, j, :], start=(j == 0), stop=(j == 1))
                    mm.then_inc(s["t3_y"], 1)

        @block.scalar
        def _(act):
            own = Steps(act, s["act_own"])
            act.sem_inc(s["ne_done"], 4)
            act.sem_inc(s["f_ev"], 2)
            act.sem_inc(s["f_sq"], 1)
            act.wait_ge(s["const_in"], 16 * 20)
            cth = sm[:].rearrange("p a b -> p (a b)")[:, 0:KH * B]
            act.activation(cth, ccol[:].rearrange("p k b -> p (k b)"), ACT.Tanh, scale=0.5).then_inc(s["a_ready"], 1)
            act.activation(alog[:], alog[:], ACT.Exp).then_inc(s["a_ready"], 1)
            act.activation(gcol[:, 1:2], gcol[:, 0:1], ACT.Exp, scale=-1.0).then_inc(s["a_ready"], 1)

            def evict_mod(m):
                act.wait_ge(s["mod_mm"], m + 1)
                c = MOD_ORDER[m]
                dst = modr[:, c * T:(c + 1) * T] if c < 4 else modg[:, (c - 4) * T:(c - 3) * T]
                act.activation(dst, ps[4 + m % 2][0:B, :], ACT.Identity, bias=1.0 if c in (8, 9) else 0.0, scale=0.5
                               ).then_inc(s["mod_ev"], 1)

            for m in range(MOD_EARLY):
                evict_mod(m)
            act.preload_act_table_set("natural_log_exp_and_others")
            act.wait_ge(s["var_ready"], 1)
            own.link(act.activation(sm[:, :, 1], sm[:, :, 0], ACT.Ln))
            act.activation(sm[:, :, 1], sm[:, :, 1], ACT.Exp, scale=-0.5).then_inc(s["rstd_ready"], 1)
            barrier(act, 0)

            def evict_ln(b, h, bank):
                if h == 0:
                    act.wait_ge(s["mc_ready"], b + 1)
                act.wait_ge(s["nt_done"], b * KH + (h + 1))
                act.activation(hT[:, h, :], ps[bank][:], ACT.Identity, bias=mcur[:, h:h + 1],
                               scale=mcur[:, KH + h:KH + h + 1]).then_inc(s["ne_done"], 1)

            def first_tap(b, i, par):
                f = b * N + i * 2 + par
                act.wait_ge(s["proj_done"], f * 2 + (CR_PROJ + 1))
                act.wait_ge(s["xc_done"], f + 1)
                act.activation(acc[:, par, :], ps[6][:], ACT.Identity, bias=kcur[:, par, F_BIAS:F_BIAS + 1],
                               scale=kcur[:, par, F_TAP + K - 1:F_TAP + K]).then_inc(s["tap_done"], 1)

            def tanh_x(b, i, par):
                f = b * N + i * 2 + par
                act.wait_ge(s["conv_done"], f + 2)
                act.wait_ge(s["xc_done"], f + 2)
                act.activation(thx[:], acc[:, par, :], ACT.Tanh).then_inc(s["thx_done"], 1)

            def tanh_z(b, i, par):
                f = b * N + i * 2 + par
                act.wait_ge(s["proj_done"], f * 2 + (CR_PROJ + 2))
                act.wait_ge(s["z_done"], f + 1)
                act.activation(thz[:], ps[7][:], ACT.Tanh, scale=0.5).then_inc(s["thz_done"], 1)

            def scan(b, front, k):
                def step(i, first):
                    for par in range(2):
                        pi, pp = (i, 0) if par else (i - 1, 1)
                        act.wait_ge(s["kcur_ready"], b * (N + 1) + i * 2 + (N + par + 1))
                        for kt in range(KD):
                            if front and kt == 3 and not (first and par == 0):
                                tanh_z(b + 1, pi, pp)
                            if front and kt == 5 and not (first and par == 0):
                                tanh_x(b + 1, pi, pp)
                            if front and kt == 14:
                                first_tap(b + 1, i, par)
                            g = (b * N + i * 2 + par) * KD + kt
                            act.wait_ge(s["scan_done"], g + (CR_SCAN - 1))
                            act.activation(ps[4 + kt % 2][:], dt_sb[:, kt, :], ACT.Exp, scale=kcur[:, par, kt:kt + 1]
                                           ).then_inc(s["da_ready"], 1)
                step(0, True)
                with act.Fori(1, N // 2) as i:
                    step(i, False)
                if front:
                    tanh_x(b + 1, N // 2 - 1, 1)
                    tanh_z(b + 1, N // 2 - 1, 1)
                barrier(act, k)

            def middle(b, k, gate=True, delta=True, ln=True):
                act.preload_act_table_set("natural_log_exp_and_others")
                if not gate:
                    evict_mod(4)
                    evict_mod(5)
                if ln:
                    for h in range(KH):
                        evict_ln(b + 2, h, 7)
                if delta:
                    act.wait_ge(s["xp_done"], b + 2)
                    act.activation(ssmT, ps[6][0:E, :], ACT.Copy).then_inc(s["xp_ev"], 1)
                if delta:
                    act.wait_ge(s["rms_sq"], b + 2)
                    own.link(act.activation(ms[:, :, 1, :], ms[:, :, 0, :], ACT.Ln))
                    act.activation(ms[:, :, 1, :], ms[:, :, 1, :], ACT.Exp, scale=-0.5).then_inc(s["rms_rs"], 1)
                    if not gate:
                        evict_mod(6)
                    act.wait_ge(s["n_tr"], b + 2)
                    act.activation(dtr[0:R, :], ps[6][0:R, :], ACT.Copy, scale=dtln[:]).then_inc(s["n_ev"], 1)
                    act.activation(bT, ps[7][0:N, :], ACT.Copy).then_inc(s["n_ev"], 1)
                    if not gate:
                        evict_mod(7)
                    for kt in range(KD):
                        if not gate and kt in (4, 7, 10, 13):
                            evict_mod(7 + kt // 3)
                        act.wait_ge(s["dt_mm"], b * KD + (KD + kt + 1))
                        act.wait_ge(s["dt_done"], b * KD + (KD + kt + 2))
                        e = e3[kt % 3]
                        own.link(act.activation(e, ps[kt % 4][:], ACT.Abs))
                        own.link(act.activation(e, e, ACT.Exp, scale=-1.0))
                        act.activation(l3[kt % 3], e, ACT.Ln, bias=1.0).then_inc(s["e_done"], 1)
                barrier(act, k)

            for h in range(KH):
                evict_ln(0, h, h % 4)
            barrier(act, 1)
            with act.Fori(0, N // 2) as i:
                for par in range(2):
                    act.wait_ge(s["kcur_ready"], i * 2 + (par + 1))
                    first_tap(0, i, par)
                    tanh_x(0, i, par)
                    tanh_z(0, i, par)
            barrier(act, 2)
            middle(-1, 3, gate=False)
            per_loop = 1 + 2 * KD
            with act.Fori(0, B - 2) as b:
                own.enter(b, per_loop)
                scan(b, True, ph(b, 0))
                middle(b, ph(b, 1))
            own.leave(B - 2, per_loop)
            scan(B - 2, True, ph(B - 2, 0))
            middle(B - 2, ph(B - 2, 1), ln=False)
            scan(B - 1, False, ph(B - 1, 0))
            middle(B - 1, ph(B - 1, 1), delta=False, ln=False)

            act.preload_act_table_set("natural_log_exp_and_others")
            act.wait_ge(s["f_var"], 1)
            own.link(act.activation(sm[:, :, 1], sm[:, :, 0], ACT.Ln))
            act.activation(sm[:, :, 1], sm[:, :, 1], ACT.Exp, scale=-0.5).then_inc(s["f_rstd"], 1)
            with act.Fori(0, B // 2) as i:
                for r in range(2):
                    for tt in range(TT):
                        n = (i * 2 + r) * TT + tt
                        act.wait_ge(s["f_add"], n + 1)
                        if tt == 0:
                            act.wait_ge(s["f_lrow"], i * 2 + (r + 1))
                        act.wait_ge(s["f_sq"], n + 1)
                        act.activation(trash, h2[r][:, tt, :], ACT.Square, accum_out=Lcur[:, tt, NL:NL + 1]
                                       ).then_inc(s["f_sq"], 1)
                        for j in range(2):
                            act.wait_ge(s["f_tr"], n * 2 + (j + 1))
                            if j == 0:
                                act.wait_ge(s["f_lg"], n + 1)
                            act.activation(h2T[:, tt % 2, 4 * j:4 * j + 4, :].rearrange("p k c -> p (k c)"), ps[j][:], ACT.Copy
                                           ).then_inc(s["f_ev"], 1)
            barrier(act, TAIL)

            act.preload_act_table_set("natural_log_exp_and_others")
            for k, steps in enumerate(sink_requests):
                act.wait_ge(s["ask"], k + 1)
                for n, (dst, src, func, scale) in enumerate(steps):
                    ins = act.activation(dst, src, func, scale=scale)
                    if n < len(steps) - 1:
                        own.link(ins)
                    else:
                        ins.then_inc(s["answer"], 1)
            barrier(act, TAIL + 1)

            t3_in = slots("t3_in", 2)
            with act.Fori(0, B // 2) as i:
                for r in range(2):
                    b = i * 2 + r
                    act.wait_ge(t3_in[r], i * 48 + 48)
                    act.wait_ge(s["t3_cur"], b + 1)

                    def first_terms(tt):
                        act.wait_ge(s["t3_gb"], b * TT + (tt + 1))
                        act.wait_ge(s["t3_mix"], b * TT + (tt + 1))
                        h = h2[r][:, tt, 0:C]
                        act.activation(acc[:, tt % 2, 0:C], h, ACT.Copy, scale=Hcur[:, tt, 16:17])
                        for j in range(S):
                            ins = act.activation(mixb[:, tt, j * C:(j + 1) * C], h, ACT.Copy, scale=Hcur[:, tt, 4 * j:4 * j + 1])
                        ins.then_inc(s["t3_first"], 1)

                    first_terms(0)
                    for tt in range(TT):
                        if tt + 1 < TT:
                            first_terms(tt + 1)
                        act.wait_ge(s["t3_tr"], b * TT + (tt + 1))
                        act.activation(thx[:, (tt % 2) * C:(tt % 2) * C + C], ps[tt % 2][:, 0:C], ACT.Copy
                                       ).then_inc(s["t3_ev"], 1)

        @block.gpsimd
        def _(pool):
            pool.sem_inc(s["v_ready"], CR_V)
            pool.sem_inc(s["t3_mix"], 4)
            for k in range(3):
                barrier(pool, k)

            def scan(b, k):
                b_in = slots("b_in", 2)

                def step(i):
                    for par in range(2):
                        pool.wait_ge(b_in[par], b * (8 * 16) + i * 16 + 16)
                        for kt in range(KD):
                            g = (b * N + i * 2 + par) * KD + kt
                            pool.wait_ge(s["scan_done"], g + (CR_SCAN - VR + 1))
                            pool.tensor_tensor(vring[:, kt % VR, :], u_sb[:, kt, :], bbc[:, par, :], ALU.mult
                                               ).then_inc(s["v_ready"], 1)
                with pool.Fori(0, N // 2) as i:
                    step(i)
                barrier(pool, k)

            def middle(b, k, delta=True):
                if delta:
                    for kt in range(KD):
                        pool.wait_ge(s["nw_done"], b * KD + (KD + kt + 1))
                        pool.tensor_tensor(c3[kt % 3], e3[kt % 3], c3[kt % 3], ALU.subtract).then_inc(s["q_done"], 1)
                barrier(pool, k)

            middle(-1, 3)
            with pool.Fori(0, B - 2) as b:
                scan(b, ph(b, 0))
                middle(b, ph(b, 1))
            scan(B - 2, ph(B - 2, 0))
            middle(B - 2, ph(B - 2, 1))
            scan(B - 1, ph(B - 1, 0))
            middle(B - 1, ph(B - 1, 1), delta=False)
            with pool.Fori(0, B // 2) as i:
                for r in range(2):
                    for tt in range(TT):
                        pool.wait_ge(s["f_mul"], (i * 2 + r) * TT + (tt + 1))
                        pool.tensor_tensor(h2[r][:, tt, :], h2[r][:, tt, :], frow[r][:, 1, :], ALU.add
                                           ).then_inc(s["f_add"], 1)
            barrier(pool, TAIL)
            barrier(pool, TAIL + 1)
            with pool.Fori(0, B // 2) as i:
                for r in range(2):
                    for tt in range(TT):
                        pool.wait_ge(s["t3_gb"], (i * 2 + r) * TT + (tt + 3))
                        pool.tensor_tensor(x1[r][:, tt, :], x1[r][:, tt, :], mixb[:, tt, :], ALU.add
                                           ).then_inc(s["t3_mix"], 1)

        @block.vector
        def _(dve):
            own = Steps(dve, s["dve_own"])
            for name, credit in (("scan_done", CR_SCAN), ("stt_done", CR_STT), ("conv_done", 1), ("z_done", 1),
                                 ("xc_done", 2), ("gate_done", 2), ("dt_done", 4),
                                 ("f_lv", 4), ("f_lrow", 1), ("t3_gb", 2)):
                dve.sem_inc(s[name], credit)

            def ts(out_, in_, a, b_, op0, op1=None):
                return dve.tensor_scalar(out_, in_, a, b_, op0, op1) if op1 is not None else dve.tensor_scalar(out_, in_, a, None, op0)

            def newton(r, v, t):
                own.link(dve.tensor_tensor(t, r, r, ALU.mult))
                own.link(dve.tensor_tensor(t, t, v, ALU.mult))
                own.link(ts(t, t, -0.5, 1.5, ALU.mult, ALU.add))
                own.link(dve.tensor_tensor(r, r, t, ALU.mult))

            own.mark(dve.memset(cols[:], 0.0))
            dve.memset(dtr[R:R + 1, :], 1.0)
            dve.wait_ge(s["const_in"], 16 * 20)
            dve.wait_ge(s["dve_own"], own.done())
            ts(cols[:, 0:N, F_TAP:F_TAP + K], cw[:], 0.5, None, ALU.mult)
            ts(cols[:, 0:N, F_BIAS], cb[:], 0.5, None, ALU.mult)
            dve.wait_ge(s["a_ready"], 2)
            ts(cols[:, 0:N, 0:KD], alog[:], -1.0, None, ALU.mult)
            cth = sm[:].rearrange("p a b -> p (a b)")[:, 0:KH * B]
            ccf = ccol[:].rearrange("p k b -> p (k b)")
            dve.scalar_tensor_tensor(ccf, cth, 1.0, ccf, ALU.add, ALU.mult).then_inc(s["silu_c"], 1)
            dve.wait_ge(s["a_ready"], 3)
            own.link(ts(gcol[:, 1:2], gcol[:, 1:2], 1.0, None, ALU.add))
            own.link(dve.reciprocal(gcol[:, 2:3], gcol[:, 1:2]))
            own.link(ts(gcol[:, 3:4], gcol[:, 2:3], -1.0, 1.0, ALU.mult, ALU.add))
            x_in = slots("x_in", 4)
            for i in range(NT):
                dve.wait_ge(x_in[i % 4], 16 * (i // 4 + 1))
                dve.bn_stats(st[:, i % 2, 0, :], hT4[:, i % 4, 0:512])
                dve.bn_stats(st[:, i % 2, 1, :], hT4[:, i % 4, 512:1024]).then_inc(s["stat_done"], 1)
                dve.wait_ge(s["stat_done"], i + 1)
                ins = dve.bn_aggr(mv[:, i, :], st[:, i % 2].rearrange("p a b -> p (a b)"))
            own.link(ins)
            dve.wait_ge(s["silu_c"], 1)
            ts(sm[:, :, 0], mv[:, :, 1], EPS_LN, None, ALU.add).then_inc(s["var_ready"], 1)
            dve.wait_ge(s["rstd_ready"], 1)
            newton(sm[:, :, 1], sm[:, :, 0], sm[:, :, 2])
            own.link(dve.tensor_copy(mv[:, :, 1], sm[:, :, 1]))
            dve.wait_ge(s["mod_tr"], 1)
            pv = ps[2][:, 0:2 * KH * B].rearrange("p (j b) -> p b j", b=B)
            dve.tensor_copy(modc[:, :, 0:KH], pv[:, :, 0:KH])
            ts(modc[:, :, KH:2 * KH], pv[:, :, KH:2 * KH], 1.0, None, ALU.add)
            barrier(dve, 0)

            def norm(b):
                ts(mcur[:], modc[:, bass.ds(b, 1), :].rearrange("p o j -> p (o j)"), 1.0, None, ALU.mult)
                ts(mvcur[:].rearrange("p q s -> p (q s)"),
                   mv[:].rearrange("p (b q) s -> p b (q s)", b=B)[:, bass.ds(b, 1), :].rearrange("p o j -> p (o j)"),
                   1.0, None, ALU.mult).then_inc(s["mc_ready"], 1)
                dve.wait_ge(s["mc_ready"], b + 1)
                for tt in range(TT):
                    dve.wait_ge(s[f"x_in{tt}"], b * 16 + (4 * 16 + 16))
                    ts(x4[:, tt, :], x4[:, tt, :], mvcur[:, tt, 0:1], mvcur[:, tt, 1:2], ALU.subtract, ALU.mult
                       ).then_inc(s["xn_done"], 1)

            def columns(n, par):
                ts(kcur[:, par, :], cols[:, bass.ds(n, 1), :].rearrange("p o j -> p (o j)"), 1.0, None, ALU.mult
                   ).then_inc(s["kcur_ready"], 1)

            def tap(b, i, par, q):
                f = b * N + i * 2 + par
                if q == 1:
                    dve.wait_ge(s["tap_done"], f + 1)
                else:
                    dve.wait_ge(s["dve_own"], own.done())
                ins = dve.scalar_tensor_tensor(acc[:, par, q:T], ps[6][:, 0:T - q], kcur[:, par, F_TAP + K - 1 - q:F_TAP + K - q],
                                               acc[:, par, q:T], ALU.mult, ALU.add)
                if q == K - 1:
                    ins.then_inc(s["conv_done"], 1)
                else:
                    own.mark(ins)

            def finish_x(b, i, par):
                f = b * N + i * 2 + par
                dve.wait_ge(s["thx_done"], f + 1)
                dve.wait_ge(s[f"xc_st{par}"], b * (8 * 16) + i * 16 + 16)
                dve.scalar_tensor_tensor(xcb[:, par, :], thx[:], 1.0, acc[:, par, :], ALU.add, ALU.mult
                                         ).then_inc(s["xc_done"], 1)

            def finish_z(b, i, par):
                f = b * N + i * 2 + par
                dve.wait_ge(s["thz_done"], f + 1)
                dve.wait_ge(s[f"z_st{par}"], b * (8 * 16) + i * 16 + 16)
                dve.scalar_tensor_tensor(szb[:, par, :], thz[:], 1.0, ps[7][:], ALU.add, ALU.mult
                                         ).then_inc(s["z_done"], 1)

            def scan(b, front, k):
                def over_states(b, i, par, g, tt, zeroth):
                    grp = (b * N + i * 2 + par) * NG + g
                    dve.wait_ge(s["th_done"], grp * 4 + (CR_TH + tt + 1))
                    yv = y_sb[:, tt, g * 512:(g + 1) * 512]
                    ccol_ = kcur[:, par, F_C + tt:F_C + tt + 1]
                    if zeroth:
                        ins = ts(yv, ps[tt][:], ccol_, None, ALU.mult)
                    else:
                        ins = dve.scalar_tensor_tensor(yv, ps[tt][:], ccol_, yv, ALU.mult, ALU.add)
                    ins.then_inc(s["stt_done"], 1)

                def step(i, first):
                    for par in range(2):
                        pi, pp = (i, 0) if par else (i - 1, 1)
                        before = not (first and par == 0)
                        for kt in range(KD):
                            g = (b * N + i * 2 + par) * KD + kt
                            grp = (b * N + i * 2 + par) * NG + kt // 4
                            if kt % 4 == 0:
                                dve.wait_ge(s["th_done"], grp * 4 + 4)
                            dve.wait_ge(s["v_ready"], g + (CR_V + 1))
                            dve.wait_ge(s["da_ready"], g + 1)
                            dve.tensor_tensor_scan(hring[:, kt % HR, :], ps[4 + kt % 2][:], vring[:, kt % VR, :], 0.0,
                                                   ALU.mult, ALU.add).then_inc(s["scan_done"], 1)
                            if kt == 4:
                                dve.wait_ge(s["kcur_ready"], b * (N + 1) + i * 2 + (N + par + 1))
                            if kt >= 4:
                                over_states(b, i, par, kt // 4 - 1, kt % 4, first and par == 0)
                            elif before:
                                over_states(b, pi, pp, NG - 1, kt % 4, first and par == 1)
                            if kt == 8:
                                columns(i * 2 + (par + 1), 1 - par)
                            if front and before:
                                if kt < 3:
                                    tap(b + 1, pi, pp, kt + 1)
                                if kt == 5:
                                    finish_z(b + 1, pi, pp)
                                if kt == 7:
                                    finish_x(b + 1, pi, pp)
                per = 4 if front else 0
                columns(0, 0)
                step(0, True)
                with dve.Fori(1, N // 2) as i:
                    own.enter(i - 1, per)
                    step(i, False)
                own.leave(N // 2 - 1, per)
                for tt in range(TT):
                    over_states(b, N // 2 - 1, 1, NG - 1, tt, False)
                if front:
                    for q in range(1, K):
                        tap(b + 1, N // 2 - 1, 1, q)
                    finish_x(b + 1, N // 2 - 1, 1)
                    finish_z(b + 1, N // 2 - 1, 1)
                barrier(dve, k)

            def middle(b, k, gate=True, delta=True, ln=True):
                def evict(half):
                    for tt in range(TT):
                        dve.wait_ge(s["out_done"], b * 8 + (4 * half + tt + 1))
                        if tt == 0:
                            dve.wait_ge(s["res_in"], b * 128 + 64 * (half + 1))
                        if tt == 0 and half == 0:
                            dve.wait_ge(s["row_in"], b * 16 + 16)
                            if ln:
                                dve.wait_ge(s["nt_done"], b * KH + 3 * KH)
                        ins = dve.tensor_tensor(prod[:, tt % 2, :], ps[4 * half + tt][:], row[:, 512 * half:512 * half + 512], ALU.mult)
                        if half == 0:
                            ins.then_inc(s["half_done"], 1)
                            dve.wait_ge(s["half_done"], b * TT + (tt + 1))
                        else:
                            own.link(ins)
                        own.link(dve.tensor_tensor(xres[:, tt, :], prod[:, tt % 2, :], xres[:, tt, :], ALU.add))
                        dve.bn_stats(st2[:, tt, half, :], xres[:, tt, :]).then_inc(s["x1_done"], 1)
                        if half:
                            dve.wait_ge(s["x1_done"], b * 8 + (4 + tt + 1))
                            alone(dve)
                            ins = dve.bn_aggr(mv2[:, tt, :], st2[:, tt].rearrange("p a b -> p (a b)"))
                    if half:
                        own.link(ins)
                        ts(mv2all[:].rearrange("p (b q) l -> p b (q l)", b=B)[:, bass.ds(b, 1), :].rearrange("p o j -> p (o j)"),
                           mv2[:].rearrange("p q l -> p (q l)"), 1.0, None, ALU.mult)

                for kt in range(KD):
                    if gate:
                        dve.wait_ge(s["gt_done"], b * KD + (kt + 1))
                        dve.wait_ge(s[f"g_in{kt % 2}"], b * (8 * 32) + 32 * (kt // 2 + 1))
                        own.link(dve.scalar_tensor_tensor(acc[:, kt % 2, :], xcb[:, kt % 2, :], dsc[:, kt:kt + 1],
                                                          ps[4 + kt % 2][:], ALU.mult, ALU.add))
                        dve.scalar_tensor_tensor(y_sb[:, :, kt * P:(kt + 1) * P],
                                                 acc[:, kt % 2, :].rearrange("p (q c) -> p q c", q=TT), 0.5,
                                                 szb[:, kt % 2, :].rearrange("p (q c) -> p q c", q=TT), ALU.mult, ALU.mult
                                                 ).then_inc(s["gate_done"], 1)
                    if ln and kt == 6:
                        norm(b + 2)
                if not gate:
                    finish_mod(2, 6)
                if delta:
                    norms(b + 1)
                if gate:
                    evict(0)
                if delta:
                    softplus(b + 1, not gate)
                if gate:
                    evict(1)
                barrier(dve, k)

            def norms(b):
                dve.wait_ge(s["xp_tr"], b + 1)
                own.link(dve.tensor_copy(sA, ps[7][:, 0:TT * E].rearrange("p (q e) -> p q e", q=TT)))
                own.link(dve.tensor_tensor(sq, sA, sA, ALU.mult))
                for j, (lo, hi) in enumerate(((0, R), (R, R + N), (R + N, E))):
                    own.link(dve.tensor_reduce(ms[:, :, 0, j], sq[:, :, lo:hi], AX, ALU.add))
                    ins = ts(ms[:, :, 0, j], ms[:, :, 0, j], 1.0 / (hi - lo), EPS_RMS, ALU.mult, ALU.add)
                ins.then_inc(s["rms_sq"], 1)
                dve.wait_ge(s["rms_rs"], b + 1)
                newton(ms[:, :, 1, :], ms[:, :, 0, :], ms[:, :, 2, :])
                for tt in range(TT):
                    for j, (lo, hi) in enumerate(((0, R), (R, R + N), (R + N, E))):
                        ins = ts(sA[:, tt, lo:hi], sA[:, tt, lo:hi], ms[:, tt, 1, j:j + 1], None, ALU.mult)
                own.link(ins)
                for tt in range(TT):
                    dve.tensor_tensor(sA[:, tt, R:R + N], sA[:, tt, R:R + N], blnw[:, 0:N], ALU.mult)
                    ins = dve.tensor_tensor(cols[:, 0:N, F_C + tt], sA[:, tt, R + N:E], blnw[:, N:2 * N], ALU.mult)
                ins.then_inc(s["bt_ready"], 1)

            def finish_mod(j, turns):
                dve.wait_ge(s["mod_ev"], turns)
                g = modg[:, (j - 2) * H:(j - 1) * H]
                t0, t1 = acc[0:B].rearrange("p a t -> p (a t)"), row[0:B, :]
                own.link(ts(t0, g, -1.0, None, ALU.mult))
                own.link(dve.tensor_tensor(t0, t0, g, ALU.max))
                own.link(ts(t0, t0, G_MIN, None, ALU.max))
                own.link(ts(t1, g, 0.0, 2.0, ALU.is_ge, ALU.mult))
                dve.scalar_tensor_tensor(g, t1, -1.0, t0, ALU.add, ALU.mult).then_inc(s["mod_rows"], 1)
                dve.wait_ge(s["mod_rows"], 1 if j == 2 else 2)

            def softplus(b, mod=False):
                def rounded(kt):
                    dve.wait_ge(s["e_done"], b * KD + (kt + 1))
                    ts(c3[kt % 3], e3[kt % 3], 1.0, -1.0, ALU.add, ALU.add).then_inc(s["nw_done"], 1)
                    own.mark(dve.scalar_tensor_tensor(dt_sb[:, kt, :], ps[kt % 4][:], 0.0, l3[kt % 3], ALU.max, ALU.add))
                rounded(0)
                for kt in range(KD):
                    if mod and kt == 4:
                        finish_mod(5, 8)
                    summed = own.done()
                    if kt + 1 < KD:
                        rounded(kt + 1)
                    dve.wait_ge(s["dve_own"], summed)
                    dve.wait_ge(s["q_done"], b * KD + (kt + 1))
                    own.link(dve.tensor_tensor(dt_sb[:, kt, :], dt_sb[:, kt, :], c3[kt % 3], ALU.add))
                    dve.tensor_tensor(u_sb[:, kt, :], dt_sb[:, kt, :], u_sb[:, kt, :], ALU.mult).then_inc(s["dt_done"], 1)

            norm(0)
            barrier(dve, 1)
            with dve.Fori(0, N // 2) as i:
                own.enter(i, 4)
                for par in range(2):
                    columns(i * 2 + par, par)
                    dve.wait_ge(s["kcur_ready"], i * 2 + (par + 1))
                    for q in range(1, K):
                        tap(0, i, par, q)
                    finish_x(0, i, par)
                    finish_z(0, i, par)
            own.leave(N // 2, 4)
            barrier(dve, 2)
            middle(-1, 3, gate=False)
            per_loop = 2 * N + (KD + 3 * TT + 1) + (2 + 3 + 4 + 1) + 2 * KD
            with dve.Fori(0, B - 2) as b:
                own.enter(b, per_loop)
                scan(b, True, ph(b, 0))
                middle(b, ph(b, 1))
            own.leave(B - 2, per_loop)
            scan(B - 2, True, ph(B - 2, 0))
            middle(B - 2, ph(B - 2, 1), ln=False)
            scan(B - 1, False, ph(B - 1, 0))
            middle(B - 1, ph(B - 1, 1), delta=False, ln=False)

            ts(sm[:, :, 0], mv2all[:, :, 1], EPS_LN, None, ALU.add).then_inc(s["f_var"], 1)
            dve.wait_ge(s["f_rstd"], 1)
            newton(sm[:, :, 1], sm[:, :, 0], sm[:, :, 2])
            own.link(dve.tensor_copy(mv2all[:, :, 1], sm[:, :, 1]))
            per_turn = 2 * (1 + TT)
            with dve.Fori(0, B // 2) as i:
                own.enter(i, per_turn)
                for r in range(2):
                    b = i * 2 + r
                    own.link(ts(mv2[:].rearrange("p q l -> p (q l)"),
                                mv2all[:].rearrange("p (b q) l -> p b (q l)", b=B)[:, bass.ds(b, 1), :].rearrange("p o j -> p (o j)"),
                                1.0, None, ALU.mult))
                    dve.wait_ge(s[f"f_in{r}"], i * 16 + 16)
                    dve.wait_ge(s[f"r_in{r}"], i * 32 + 32)

                    def logits(tt):
                        dve.wait_ge(s["f_lg"], b * TT + (tt + 3))
                        dve.tensor_copy(Lcur[:, tt, 0:NL], ps[2 + tt][:, 0:NL]).then_inc(s["f_lv"], 1)

                    for tt in range(TT):
                        own.link(ts(h2[r][:, tt, :], x1[r][:, tt, :], mv2[:, tt, 0:1], mv2[:, tt, 1:2], ALU.subtract, ALU.mult))
                        dve.tensor_tensor(h2[r][:, tt, :], h2[r][:, tt, :], frow[r][:, 0, :], ALU.mult).then_inc(s["f_mul"], 1)
                        if tt >= 2:
                            logits(tt - 2)
                    logits(TT - 2)
                    logits(TT - 1)
                    dve.wait_ge(s["f_lv"], b * TT + (TT + 4))
                    dve.wait_ge(s["f_sq"], b * TT + (TT + 1))
                    ts(Lall[:].rearrange("p (b q) l -> p b (q l)", b=B)[:, bass.ds(b, 1), :].rearrange("p o j -> p (o j)"),
                       Lcur[:].rearrange("p q l -> p (q l)"), 1.0, None, ALU.mult).then_inc(s["f_lrow"], 1)
            own.leave(B // 2, per_turn)
            barrier(dve, TAIL)

            asked = [0]

            def ask(ins):
                asked[0] += 1
                ins.then_inc(s["ask"], 1)
                dve.wait_ge(s["answer"], asked[0])

            def v4(t):
                return t.rearrange("p (q i j) -> p q i j", q=NT, i=S)

            def v4t(t):
                return t.rearrange("p (q i j) -> p q j i", q=NT, i=S)

            def v3(t):
                return t.rearrange("p (q i) -> p q i", q=NT)

            def row_b(t):
                return t.rearrange("p (q i o) -> p q i o", q=NT, o=1).to_broadcast([P, NT, S, S])

            def flat(t):
                return t.rearrange("p (r j) -> p r j", j=S)

            def over_j(t):
                return t.rearrange("p (r o) -> p r o", o=1).to_broadcast([P, NT * S, S])

            def over_i(t, i):
                return t.rearrange("p (q j) -> p q j", q=NT)

            def tt_i(dst, a, v, op):
                return dve.tensor_tensor(v4(dst), v4(a), v.rearrange("p (q o j) -> p q o j", q=NT, o=1)
                                         .to_broadcast([P, NT, S, S]), op)

            def tt_j(dst, a, u, op):
                return dve.tensor_tensor(flat(dst), flat(a), over_j(u), op)

            def red_j(dst, a, op):
                return dve.tensor_reduce(dst.rearrange("p (r o) -> p r o", o=1), flat(a), AX, op)

            def red_i(dst, a, op):
                return dve.tensor_reduce(v3(dst), v4t(a), AX, op)

            ask(ts(rs0, Lall[:, :, NL], 1.0 / H, EPS_FFN, ALU.mult, ALU.add))
            newton(rs1, rs0, skv(13, NT))
            for q in range(NT):
                own.mark(dve.scalar_tensor_tensor(Lall[:, q, 0:NL], Lall[:, q, 0:NL], rs1[:, q:q + 1], base[:], ALU.mult, ALU.add))
            dve.wait_ge(s["dve_own"], own.done())
            PL = Lall[:, :, S * S:NL].rearrange("p q (g j) -> p q g j", g=2)
            pm3 = pm.rearrange("p (q g) -> p q g", q=NT)
            psu3 = psu.rearrange("p (q g) -> p q g", q=NT)
            pmb = pm.rearrange("p (q g o) -> p q g o", q=NT, o=1).to_broadcast([P, NT, 2, S])
            psb = psu.rearrange("p (q g o) -> p q g o", q=NT, o=1).to_broadcast([P, NT, 2, S])
            Pv = Pb.rearrange("p (q g j) -> p q g j", q=NT, g=2)
            Ev = Eb.rearrange("p (q g j) -> p q g j", q=NT, g=2)
            own.link(dve.tensor_reduce(pm3, PL, AX, ALU.max))
            ask(dve.tensor_tensor(Pv, PL, pmb, ALU.subtract))
            own.link(dve.tensor_reduce(psu3, Ev, AX, ALU.add))
            own.link(dve.reciprocal(psu, psu))
            own.link(dve.tensor_tensor(Hall[:, :, S * S:NL].rearrange("p q (g j) -> p q g j", g=2), Ev, psb, ALU.mult))
            own.link(ts(Zb.rearrange("p (q r) -> p q r", q=NT), Lall[:, :, 0:S * S], 1.0 / TAU, None, ALU.mult))
            own.link(red_j(Mb, Zb, ALU.max))
            ask(tt_j(Kb, Zb, Mb, ALU.subtract))
            ask(red_j(Sb_, Tb, ALU.add))
            own.link(dve.scalar_tensor_tensor(Ub, Sb_, -1.0, Mb, ALU.mult, ALU.subtract))
            own.link(tt_j(Zb, Zb, Ub, ALU.add))
            own.link(red_i(Mb, Zb, ALU.max))
            ask(tt_i(Kb, Zb, Mb, ALU.subtract))
            ask(red_i(Sb_, Tb, ALU.add))
            own.link(dve.scalar_tensor_tensor(Vb, Sb_, -1.0, Mb, ALU.mult, ALU.subtract))
            ask(tt_i(Zb, Zb, Vb, ALU.add))
            def balance(last):
                own.link(tt_i(Tb, Kb, vb, ALU.mult))
                own.link(red_j(Sb_, Tb, ALU.add))
                own.link(dve.reciprocal(ub, Sb_))
                own.link(tt_j(Tb, Kb, ub, ALU.mult))
                own.link(red_i(Sb_, Tb, ALU.add))
                last(dve.reciprocal(vb, Sb_))

            left = ITERS - 1
            for r in range(3):
                turns = left if r == 2 else REFRESH
                left -= turns
                loops, rest = (turns - 1) // STEP, (turns - 1) % STEP
                own.link(dve.memset(vb, 1.0))
                with dve.Fori(0, loops) as it:
                    own.enter(it, 6 * STEP)
                    for _ in range(STEP):
                        balance(own.link)
                own.leave(loops, 6 * STEP)
                for _ in range(rest):
                    balance(own.link)
                balance(ask)
                own.link(tt_j(Zb, Zb, lnu, ALU.add))
                ask(tt_i(Zb, Zb, lnv, ALU.add))
            own.link(ts(Hall[:, :, 0:S * S], Kb.rearrange("p (q r) -> p q r", q=NT), gcol[:, 2:3], None, ALU.mult))
            own.link(ts(Hall[:, :, 0:S * S:S + 1], Hall[:, :, 0:S * S:S + 1], gcol[:, 3:4], None, ALU.add))
            barrier(dve, TAIL + 1)

            per = 2 * TT * 4
            with dve.Fori(0, B // 2) as i:
                own.enter(i, per)
                for r in range(2):
                    b = i * 2 + r
                    ts(Hcur.rearrange("p q l -> p (q l)"),
                       Hall.rearrange("p (b q) l -> p b (q l)", b=B)[:, bass.ds(b, 1), :].rearrange("p o j -> p (o j)"),
                       1.0, None, ALU.mult).then_inc(s["t3_cur"], 1)
                    dve.wait_ge(s["t3_cur"], b + 1)
                    for tt in range(TT):
                        h = [h2[r][:, tt, j * C:(j + 1) * C] for j in range(S)]
                        dve.wait_ge(s["t3_first"], b * TT + (tt + 1))
                        xv = acc[:, tt % 2, 0:C]
                        mo = [mixb[:, tt, n * C:(n + 1) * C] for n in range(S)]
                        for j in range(1, S):
                            if j > 1:
                                dve.wait_ge(s["dve_own"], own.done())
                            ins = dve.scalar_tensor_tensor(xv, h[j], Hcur[:, tt, 16 + j:17 + j], xv, ALU.mult, ALU.add)
                            if j == S - 1:
                                ins.then_inc(s["t3_pre"], 1)
                            for n in range(S):
                                ins = dve.scalar_tensor_tensor(mo[n], h[j], Hcur[:, tt, 4 * n + j:4 * n + j + 1], mo[n], ALU.mult, ALU.add)
                                if n == S - 1:
                                    own.mark(ins)
                        dve.wait_ge(s["dve_own"], own.done())
                        dve.wait_ge(s["t3_y"], b * TT + (tt + 1))
                        for n in range(S):
                            ins = dve.scalar_tensor_tensor(mo[n], ps[2 + tt % 2][:, 0:C], Hcur[:, tt, 20 + n:21 + n], mo[n], ALU.mult, ALU.add)
                        own.link(ins)
                        dve.tensor_tensor(mixb[:, tt, :], mixb[:, tt, :], gbrow[r], ALU.mult).then_inc(s["t3_gb"], 1)
            own.leave(B // 2, per)


def kernel(**inputs):
    import numpy as np
    import concourse.bacc as bacc
    from concourse.bass_utils import run_bass_kernel_spmd as run

    a = {k: np.asarray(v) for k, v in inputs.items()}

    def cols(w, k):
        return w.reshape(k, P, *w.shape[1:]).swapaxes(0, 1)

    att = {k[len("L0_attn_"):]: v for k, v in a.items() if k.startswith("L0_attn_")}
    ffn = {k[len("L0_ffn_"):]: v for k, v in a.items() if k.startswith("L0_ffn_")}
    arrays = {
        "x": att["hidden_states"].reshape(B, TT, P, H),
        "ident": np.eye(P, dtype=np.float32),
        "w_in": att["in_proj_w"].reshape(KH, P, 2 * KD, P).transpose(2, 1, 0, 3),
        "conv_w": cols(att["conv_w"], KD),
        "conv_b": cols(att["conv_b"], KD),
        "x_proj": cols(att["x_proj_w"].T, KD),
        "dt_proj": att["dt_proj_w"].T,
        "dt_bias": att["dt_bias"].reshape(1, DIN),
        "A_log": att["A_log"].reshape(KD, P, N).transpose(1, 2, 0),
        "D_param": cols(att["D_param"], KD),
        "w_out": att["out_proj_w"].T.reshape(KD // 2, 2, P, 2, 512).transpose(3, 0, 2, 1, 4).reshape(KD, P, 2 * 512),
        "dt_ln": att["dt_ln_w"].reshape(R, 1),
        "B_ln": att["B_ln_w"],
        "C_ln": att["C_ln_w"],
        "W_res": cols(ffn["W_res"].T, KH),
        "W_pre": cols(ffn["W_pre"].T, KH),
        "W_post": cols(ffn["W_post"].T, KH),
        "res_base": ffn["H_res_base"].reshape(S * S),
        "pre_base": ffn["H_pre_base"],
        "post_base": ffn["H_post_base"],
        "gate": ffn["gate"],
        "W_branch": cols(ffn["W_branch"], C // P),
        "c_cols": cols(a["L0_c"].T, KH),
        "w_mod": a["L0_wmod"].reshape(KH, P, 12, 512).transpose(2, 1, 0, 3),
    }
    nc = bacc.Bacc("TRN2", target_bir_lowering=False, num_devices=1)
    args, maps = {}, {}
    for name, v in arrays.items():
        v = np.ascontiguousarray(v)
        maps[f"in_{name}"] = v
        args[name] = nc.dram_tensor(f"in_{name}", v.shape, mybir.dt.from_np(v.dtype), kind="ExternalInput").ap()
    out = nc.dram_tensor("out_y", (B, TT, P, H), F32, kind="ExternalOutput").ap()
    build(nc, out=out, **args)
    r = run(nc, [maps], core_ids=[0])
    return r.results[0]["out_y"].reshape(B, T, H)
```

```python
from contextlib import ExitStack

import concourse.bass as bass
from concourse import mybir

F32 = mybir.dt.float32
ALU = mybir.AluOpType
ACT = mybir.ActivationFunctionType
AX = mybir.AxisListType.X

P = 128
B, T, H = 4, 512, 1024
DIN, N, K, R = 2048, 16, 4, 64
TT = T // P
KH = H // P
KD = DIN // P
NT = B * TT
E = R + 2 * N
S, C = 4, 256
NL = S * S + 2 * S
NG = KD // 4
ITERS, REFRESH = 50, 16
TAU = 0.1
EPS_LN, EPS_RMS, EPS_FFN = 1e-5, 1e-6, 1.1920929e-07
G_MIN = 0.25

STEP = 4
VR = 4
HR = 8
F_TAP, F_BIAS, F_C, F_W = 16, 20, 21, 25
LENT = (1, 3)
LEND_AT, ADD_AT = (15, 6), (2, 10)
OWN_SUMS = 4 * NG - len(LENT)
CR_V, CR_SCAN, CR_TH, CR_STT, CR_PROJ = 32, 8, 8, 4, 4


class Steps:

    def __init__(self, eng, sem):
        self.eng, self.sem, self.base, self.n, self.outer = eng, sem, 0, 0, []

    def mark(self, ins):
        ins.then_inc(self.sem, 1)
        self.n += 1

    def done(self):
        return self.base + self.n

    def link(self, ins):
        self.mark(ins)
        self.eng.wait_ge(self.sem, self.done())

    def enter(self, turn, per):
        self.outer.append(self.done())
        self.base, self.n = self.done() + turn * per, 0

    def leave(self, turns, per):
        self.base, self.n = self.outer.pop() + turns * per, 0


def build(nc, x, ident, w_in, conv_w, conv_b, x_proj, dt_proj, dt_bias, A_log, D_param, w_out,
          dt_ln, B_ln, C_ln, W_res, W_pre, W_post, res_base, pre_base, post_base, gate, W_branch,
          c_cols, w_mod, out):
    z_s = nc.dram_tensor("z_s", (B, KD, P, T), F32).ap()
    xc_s = nc.dram_tensor("xc_s", (B, KD, P, T), F32).ap()
    b_s = nc.dram_tensor("b_s", (B, N, T), F32).ap()
    mod_s = nc.dram_tensor("mod_s", (B, 6 * H), F32).ap()
    x1_s = nc.dram_tensor("x1_s", (B, TT, P, H), F32).ap()

    with ExitStack() as ctx:
        def sb(name, shape):
            return ctx.enter_context(nc.sbuf_tensor(name, shape, F32))

        def sem(name):
            return ctx.enter_context(nc.semaphore(name))

        dt_sb = sb("dt_sb", [P, KD, T])
        u_sb = sb("u_sb", [P, KD, T])
        y_sb = sb("y_sb", [P, TT, DIN])
        hT = sb("hT", [P, KH, T])
        hring = sb("hring", [P, HR, T])
        wring = sb("wring", [P, 4, KH, P])
        vring = sb("vring", [P, VR, T])
        bbc = sb("bbc", [P, 2, T])
        acc = sb("acc", [P, 2, T])
        thx = sb("thx", [P, T])
        thz = sb("thz", [P, T])
        xcb = sb("xcb", [P, 2, T])
        szb = sb("szb", [P, 2, T])
        row = sb("row", [P, H])
        idn = sb("idn", [P, P])
        cols = sb("cols", [P, N + 1, F_W])
        kcur = sb("kcur", [P, 2, F_W])
        alog = sb("alog", [P, N, KD])
        cw = sb("cw", [P, KD, K])
        cb = sb("cb", [P, KD])
        dsc = sb("dsc", [P, KD])
        xpw = sb("xpw", [P, KD, E])
        dpw = sb("dpw", [R + 1, DIN])
        dtln = sb("dtln", [R, 1])
        blnw = sb("blnw", [P, 2 * N])
        wcat = sb("wcat", [P, KH, NL])
        base = sb("base", [P, NL])
        gcol = sb("gcol", [P, 4])
        wbr = sb("wbr", [P, C // P, C])
        ccol = sb("ccol", [P, KH, B])
        modc = sb("modc", [P, B, 2 * KH])
        mcur = sb("mcur", [P, 2 * KH])
        mv = sb("mv", [P, TT, 2])
        st = sb("st", [P, TT, 2, 6])
        sm = sb("sm", [P, NT, 4])
        mv2 = sb("mv2", [P, TT, 2])
        mv2all = sb("mv2all", [P, NT, 2])
        st2 = sb("st2", [P, TT, 2, 6])
        Lall = sb("Lall", [P, NT, NL + 1])
        ms = sb("ms", [P, TT, 4, 3])
        dtr = sb("dtr", [R + 1, T])

        ps = [ctx.enter_context(nc.psum_tensor(f"bank{i}", [P, T], F32)) for i in range(8)]

        names = """phase passed const_in later_in modw0 modw1 modw2 modw3 mod_mm mod_tr mod_ev mod_rows mod_st
            silu_c x_in0 x_in1 x_in2 x_in3 var_ready rstd_ready a_ready xn_done nt_done ne_done mc_ready
            w_in0 w_in1 w_in2 w_in3 proj_done tap_done conv_done thx_done xc_done thz_done z_done xc_st0
            xc_st1 z_st0 z_st1 kcur_ready b_in0 b_in1 v_ready da_ready scan_done th_done stt_done lent_out
            lent_sum y_zero g_in0 g_in1 g_in2 g_in3 gt_done gate_done wo_in0 wo_in1 wo_in2 wo_in3 wo_done
            out_done row_in x1_done x1_st0 x1_st1 x1_st2 x1_st3 res_in half_done f_var f_rstd f_mul f_add
            f_sq f_tr f_ev f_mm f_lt f_lg f_lv u_in0 u_in1 u_in2 u_in3 xp_done xp_ev xp_tr rms_sq rms_rs
            bt_ready n_tr n_ev bs_st dt_mm e_done nw_done q_done dt_done ask answer f_in0 f_in1 t3_in0
            t3_in1 t3_pre t3_first t3_sec t3_second t3_sum t3_gb t3_last t3_tr t3_ev t3_y t3_mix t3_st0
            t3_st1 act_own dve_own""".split()
        s = {n: sem(n) for n in names}

        def slots(prefix, n):
            return [s[f"{prefix}{i}"] for i in range(n)]

        def barrier(eng, k):
            alone(eng, k)
            eng.drain().then_inc(s["phase"], 1)
            eng.wait_ge(s["phase"], 5 * (k + 1))
            alone(eng, k)

        def alone(eng, k=None):
            if not isinstance(k, int):
                eng.sem_inc(s["passed"], 1)

        def ph(b, i):
            return b * 2 + (3 + i)

        TAIL = 3 + 2 * B

        def lent(front, g, tt):
            return front and g in LENT and tt == TT - 1

        def sums_before(b, n, g, tt, front):
            if front:
                return (b * N + n) * OWN_SUMS + (g * 4 - sum(l < g for l in LENT) + tt)
            return (B - 1) * N * OWN_SUMS + n * (4 * NG) + g * 4 + tt

        x4 = hring[:].rearrange("p (q j) t -> p q (j t)", q=TT)
        hT4 = hT[:].rearrange("p (q j) t -> p q (j t)", q=TT)
        h2 = [t[:, 2 * r:2 * r + 2, :].rearrange("p a (b h) -> p (a b) h", h=H)
              for t in (y_sb, u_sb[:].rearrange("p (a c) t -> p a (c t)", a=TT)) for r in range(2)]
        x1 = [hT4, x4]
        frow = [wring[:, 2 * r:2 * r + 2].rearrange("p q k c -> p q (k c)") for r in range(2)]
        gbrow = [wring[:, r].rearrange("p k c -> p (k c)") for r in range(2)]
        h2T = [dt_sb[:, 0:KH], dt_sb[:, KH:2 * KH]]
        lgT = [thx[0:NL, :], thz[0:NL, :]]
        trash = acc[:].rearrange("p a t -> p (a t)")
        modr = u_sb[0:B].rearrange("p k t -> p (k t)")[:, 0:2 * H]
        modg = wring[0:B].rearrange("p q k c -> p (q k c)")
        gx = [vring[:, 0, :], vring[:, 1, :], xcb[:, 0, :], xcb[:, 1, :]]
        gz = [vring[:, 2, :], vring[:, 3, :], szb[:, 0, :], szb[:, 1, :]]
        xres = vring
        prod = hring
        bT = thx[0:N, :]
        sA = bbc[:, 0, 0:TT * E].rearrange("p (q e) -> p q e", q=TT)
        sq = bbc[:, 1, 0:TT * E].rearrange("p (q e) -> p q e", q=TT)
        ssmT = thz[0:E, :]
        lent_sb = row[:].rearrange("p (a t) -> p a t", t=T)
        e3 = [hring[:, 2 + i, :] for i in range(3)]
        l3 = [hring[:, 5 + i, :] for i in range(3)]
        c3 = [xcb[:, 0, :], xcb[:, 1, :], szb[:, 0, :]]

        def gated(kt, tt):
            return y_sb[:, tt, kt * P:(kt + 1) * P]

        MOD_ORDER = [0, 1, 2, 3, 4, 5, 10, 11, 6, 7, 8, 9]
        MOD_SLOT = [0, 1, 2, 0, 2, 3, 0, 1, 2, 3, 2, 3]
        mod_slots = [dt_sb[:, 0:8], dt_sb[:, 8:16]] + [
            y_sb[:, 2 * r:2 * r + 2].rearrange("p a (b t) -> p (a b) t", t=T) for r in range(2)]
        MOD_EARLY = 4

        def mod_w(m):
            return mod_slots[MOD_SLOT[m]]

        def mod_load(m):
            return MOD_SLOT[:m + 1].count(MOD_SLOT[m])

        def mod_before(m):
            return max((i for i in range(m) if MOD_SLOT[i] == MOD_SLOT[m]), default=None)

        def mod_row(b, j):
            return mod_s[bass.ds(b, 1), j * H:(j + 1) * H].rearrange("o h -> (o h)").partition_broadcast(P)

        mixb = dt_sb[:, 0:8].rearrange("p (a b) t -> p a (b t)", a=TT)

        def skv(i, n):
            return dt_sb[:, i, 0:n]
        Zb, Kb, Tb = skv(0, NT * 16), skv(1, NT * 16), skv(2, NT * 16)
        Ub, Vb, Mb, Sb_ = skv(3, NT * S), skv(4, NT * S), skv(5, NT * S), skv(6, NT * S)
        ub, vb = skv(7, NT * S), skv(8, NT * S)
        Pb, Eb = skv(9, NT * 8), skv(10, NT * 8)
        rs0, rs1 = skv(11, NT), skv(12, NT)
        pm, psu = skv(13, NT * 2), skv(14, NT * 2)
        lnu, lnv = skv(15, NT * S), Mb
        Hall = dt_sb[:, 12, NT:NT + NT * NL].rearrange("p (q l) -> p q l", q=NT)
        pre = acc[:].rearrange("p a (b c) -> p (a b) c", c=C)
        second = [bbc[:, r, :] for r in range(2)]
        TILES = [(b, tt) for b in (2, 3, 0, 1) for tt in range(TT)]

        sink_requests = [[(rs1, rs0, ACT.Ln, 1.0), (rs1, rs1, ACT.Exp, -0.5)],
                         [(Eb, Pb, ACT.Exp, 1.0)],
                         [(Tb, Kb, ACT.Exp, 1.0)], [(Sb_, Sb_, ACT.Ln, 1.0)],
                         [(Tb, Kb, ACT.Exp, 1.0)], [(Sb_, Sb_, ACT.Ln, 1.0)],
                         [(Kb, Zb, ACT.Exp, 1.0)]]
        sink_requests += [[(lnu, ub, ACT.Ln, 1.0), (lnv, vb, ACT.Ln, 1.0)], [(Kb, Zb, ACT.Exp, 1.0)]] * 3

        block = ctx.enter_context(nc.Block())

        @block.sync
        def _(sp):
            sp.sem_inc(s["xc_st0"], 16)
            sp.sem_inc(s["xc_st1"], 16)
            sp.sem_inc(s["z_st0"], 16)
            sp.sem_inc(s["z_st1"], 16)
            for tt in range(TT):
                sp.sem_inc(s[f"x1_st{tt}"], 32)

            first = [(ccol[:], c_cols), (idn[:], ident), (alog[:], A_log), (cw[:], conv_w), (cb[:], conv_b),
                     (gcol[:, 0:1], gate.partition_broadcast(P))]
            later = [(dsc[:], D_param), (xpw[:], x_proj), (dpw[0:R, :], dt_proj), (dpw[R:R + 1, :], dt_bias),
                      (dtln[:], dt_ln), (blnw[:, 0:N], B_ln.partition_broadcast(P)),
                      (blnw[:, N:2 * N], C_ln.partition_broadcast(P)),
                      (wcat[:, :, 0:S * S], W_res), (wcat[:, :, S * S:S * S + S], W_pre),
                      (wcat[:, :, S * S + S:NL], W_post),
                      (base[:, 0:S * S], res_base.partition_broadcast(P)),
                      (base[:, S * S:S * S + S], pre_base.partition_broadcast(P)),
                      (base[:, S * S + S:NL], post_base.partition_broadcast(P)),
                      (wbr[:], W_branch)]
            for dst, src in first:
                sp.dma_start(dst, src).then_inc(s["const_in"], 16)

            modw = slots("modw", 4)

            def load_mod(m):
                if mod_before(m) is not None:
                    sp.wait_ge(s["mod_mm"], mod_before(m) + 1)
                sp.dma_start(mod_w(m), w_mod[MOD_ORDER[m]]).then_inc(modw[MOD_SLOT[m]], 16)

            x_in = slots("x_in", 4)

            def load_x(b):
                for tt in range(TT):
                    sp.dma_start(x4[:, tt, :], x[bass.ds(b, 1), tt].rearrange("o p h -> (o p) h")
                                 ).then_inc(x_in[tt], 16)

            w_slot = slots("w_in", 4)
            xc_st, z_st = slots("xc_st", 2), slots("z_st", 2)
            g_in = slots("g_in", 4)
            x1_st = slots("x1_st", 4)

            def load_gate(b, kt):
                sp.wait_ge(s["gate_done"], b * KD + (kt + 1))
                for slot, src in ((gx[kt % 4], xc_s), (gz[kt % 4], z_s)):
                    sp.dma_start(slot, src[bass.ds(b, 1), kt].rearrange("o p t -> (o p) t")).then_inc(g_in[kt % 4], 16)

            b_in = slots("b_in", 2)

            def dram3(t, b, n):
                return t[bass.ds(b, 1), bass.ds(n, 1)].rearrange("o q p t -> (o q p) t")

            def load_w(b, i, par):
                f = b * N + i * 2 + par
                sp.wait_ge(s["proj_done"], f * 2 + 1)
                sp.dma_start(wring[:, 2 * par], w_in[bass.ds(i * 2 + par, 1)].rearrange("o p k c -> (o p) k c")
                             ).then_inc(w_slot[2 * par], 16)
                sp.wait_ge(s["proj_done"], f * 2 + 2)
                sp.dma_start(wring[:, 2 * par + 1], w_in[bass.ds(i * 2 + (KD + par), 1)].rearrange("o p k c -> (o p) k c")
                             ).then_inc(w_slot[2 * par + 1], 16)

            def store_front(b, i, par):
                f = b * N + i * 2 + par
                sp.wait_ge(s["xc_done"], f + 3)
                sp.dma_start(dram3(xc_s, b, i * 2 + par), xcb[:, par]).then_inc(xc_st[par], 16)
                sp.wait_ge(s["z_done"], f + 2)
                sp.dma_start(dram3(z_s, b, i * 2 + par), szb[:, par]).then_inc(z_st[par], 16)

            def load_b(b, i, par):
                n = b * N + i * 2 + par
                sp.wait_ge(s["v_ready"], n * KD + KD)
                sp.dma_start(bbc[:, par], b_s[bass.ds(b, 1), bass.ds(i * 2 + par, 1)]
                             .rearrange("o n t -> (o n t)").partition_broadcast(P)).then_inc(b_in[par], 16)

            def stores_end(b):
                for par in range(2):
                    sp.wait_ge(xc_st[par], b * (8 * 16) + 9 * 16)
                    sp.wait_ge(z_st[par], b * (8 * 16) + 9 * 16)

            def scan(b, front, k):
                def step(i, first):
                    for par in range(2):
                        if front:
                            load_w(b + 1, i, par)
                        if not first:
                            load_b(b, i, par)
                        if front and not first:
                            store_front(b + 1, i - 1, par)
                step(0, True)
                with sp.Fori(1, N // 2) as i:
                    step(i, False)
                sp.wait_ge(s["scan_done"], (b * N + N) * KD + CR_SCAN)
                alone(sp)
                load_gate(b, 0)
                load_gate(b, 1)
                if front:
                    for par in range(2):
                        store_front(b + 1, N // 2 - 1, par)
                barrier(sp, k)

            wo_in = slots("wo_in", 4)

            u_in = slots("u_in", 4)

            def middle(b, k, gate=True, delta=True, ln=True):
                def load_wo(t):
                    sp.wait_ge(s["wo_done"], b * KD + (t + 1))
                    sp.dma_start(wring[:, t % 4].rearrange("p k c -> p (k c)"), w_out[t]
                                 ).then_inc(wo_in[t % 4], 16)

                def half_rows(t, tt, half):
                    return t[bass.ds(b, 1), tt].rearrange("o p h -> (o p) h")[:, 512 * half:512 * half + 512]

                def load_residual(half):
                    for tt in range(TT):
                        if half:
                            sp.wait_ge(x1_st[tt], b * 32 + 48)
                        sp.dma_start(xres[:, tt, :], half_rows(x, tt, half)).then_inc(s["res_in"], 16)

                def store_x1(half):
                    for tt in range(TT):
                        sp.wait_ge(s["x1_done"], b * 8 + (4 * half + tt + 1))
                        sp.dma_start(half_rows(x1_s, tt, half), xres[:, tt, :]).then_inc(x1_st[tt], 16)

                def load_u(q):
                    sp.dma_start(u_sb[:, 4 * q:4 * q + 4, :],
                                 xc_s[bass.ds(b + 1, 1), 4 * q:4 * q + 4].rearrange("o k p t -> (o p) k t")
                                 ).then_inc(u_in[q], 16)

                if gate:
                    load_wo(0)
                if delta:
                    stores_end(b + 1)
                    alone(sp)
                for kt in range(KD):
                    if gate and kt >= 2:
                        load_gate(b, kt)
                    if delta and kt % 4 == 1:
                        load_u(kt // 4)
                    if gate and kt % 2 and kt > 1:
                        load_wo(kt // 2)
                    if ln and kt == 5:
                        load_x(b + 2)
                if gate:
                    sp.dma_start(row[:], mod_row(b, 2)).then_inc(s["row_in"], 16)
                    load_wo(8)
                    load_wo(9)
                    sp.wait_ge(s["gate_done"], b * KD + 14 + 4)
                    alone(sp)
                    load_residual(0)
                    load_wo(10)
                    load_wo(11)
                if not gate:
                    load_mod(8)
                    load_mod(9)
                if delta:
                    sp.wait_ge(s["n_ev"], b * 2 + 4)
                    sp.dma_start(b_s[bass.ds(b + 1, 1)].rearrange("o n t -> (o n) t"), bT).then_inc(s["bs_st"], 16)
                    sp.wait_ge(s["bs_st"], b * 16 + 32)
                if gate:
                    store_x1(0)
                    load_residual(1)
                    for t in range(12, KD):
                        load_wo(t)
                    store_x1(1)
                if not gate:
                    load_mod(10)
                    load_mod(11)
                    sp.wait_ge(s["mod_ev"], 12)
                    sp.wait_ge(s["mod_rows"], 2)
                    sp.dma_start(mod_s[:, 2 * H:6 * H], modg).then_inc(s["mod_st"], 16)
                    sp.wait_ge(s["mod_st"], 16)
                if delta:
                    load_b(b + 1, 0, 0)
                    load_b(b + 1, 0, 1)
                barrier(sp, k)

            for m in range(MOD_EARLY):
                load_mod(m)
                if m == 0:
                    load_x(0)
            for dst, src in later:
                sp.dma_start(dst, src).then_inc(s["later_in"], 16)

            def front_step(i, first):
                for par in range(2):
                    load_w(0, i, par)
                    if not first:
                        store_front(0, i - 1, par)
            front_step(0, True)
            barrier(sp, 0)
            for m, (lo, hi) in enumerate(((1, 2), (2, 4), (4, 6), (6, N // 2))):
                load_mod(MOD_EARLY + m)
                with sp.Fori(lo, hi) as i:
                    front_step(i, False)
            for par in range(2):
                store_front(0, N // 2 - 1, par)
            sp.wait_ge(s["later_in"], 16 * len(later))
            barrier(sp, 1)

            middle(-1, 2, gate=False)
            with sp.Fori(0, B - 2) as b:
                scan(b, True, ph(b, 0))
                middle(b, ph(b, 1))
            scan(B - 2, True, ph(B - 2, 0))
            middle(B - 2, ph(B - 2, 1), ln=False)
            scan(B - 1, False, ph(B - 1, 0))
            f_in = slots("f_in", 2)
            for tt in range(TT):
                sp.wait_ge(x1_st[tt], 32 + 32)
            sp.dma_start(x1[0], x1_s[0].rearrange("q p h -> p q h")).then_inc(f_in[0], 16)
            middle(B - 1, ph(B - 1, 1), delta=False, ln=False)

            for tt in range(TT):
                sp.wait_ge(x1_st[tt], 32 + 32 * B)
            for b in range(B):
                r = b % 2
                if b >= 2:
                    sp.wait_ge(s["f_mul"], TT * (b - 1))
                if b:
                    sp.dma_start(x1[r], x1_s[b].rearrange("q p h -> p q h")).then_inc(f_in[r], 16)
                sp.dma_start(frow[r][:, 0, :], mod_row(b, 4)).then_inc(f_in[r], 16)
                if b >= 2:
                    sp.wait_ge(s["f_add"], TT * (b - 1))
                sp.dma_start(frow[r][:, 1, :], mod_row(b, 3)).then_inc(f_in[r], 16)
            barrier(sp, TAIL)

            sp.sem_inc(s["phase"], 1)
            t3_in, t3_st = slots("t3_in", 2), slots("t3_st", 2)
            for k, (b, tt) in enumerate(TILES):
                r, late = b % 2, k // TT >= 2
                if k in (0, 2 * TT):
                    for r_ in range(2):
                        b_ = TILES[k + r_ * TT][0]
                        if late:
                            sp.wait_ge(t3_st[r_], 16 * TT)
                            sp.dma_start(x1[r_], x1_s[b_].rearrange("q p h -> p q h")).then_inc(t3_in[r_], 16)
                        sp.dma_start(gbrow[r_], mod_row(b_, 5)).then_inc(t3_in[r_], 16)
                if k < len(TILES) - 1:
                    sp.wait_ge(s["t3_mix"], k + 5)
                else:
                    sp.wait_ge(s["t3_last"], 1)
                sp.dma_start(out[b, tt], x1[r][:, tt, :]).then_inc(t3_st[r], 16)
            for r in range(2):
                sp.wait_ge(t3_st[r], 2 * 16 * TT)

        @block.tensor
        def _(pe):
            pe.wait_ge(s["const_in"], 16 * 6)
            for name, credit in (("proj_done", CR_PROJ), ("th_done", CR_TH), ("wo_done", 4)):
                pe.sem_inc(s[name], credit)
            pe.wait_ge(s["silu_c"], 1)
            modw = slots("modw", 4)

            def turn_ln(b, h, bank, ring):
                pe.wait_ge(s["ne_done"], b * KH + (h + 5 - ring))
                for tt in range(TT):
                    if h == 0:
                        pe.wait_ge(s["xn_done"], b * TT + (tt + 1))
                    mm = pe.transpose(ps[bank][:, tt * P:(tt + 1) * P], x4[:, tt, h * P:(h + 1) * P], idn[:])
                mm.then_inc(s["nt_done"], 1)

            def mod_turn(m):
                pe.wait_ge(modw[MOD_SLOT[m]], 16 * mod_load(m))
                if m >= 2:
                    pe.wait_ge(s["mod_ev"], m - 1)
                for k in range(KH):
                    mm = pe.matmul(ps[4 + m % 2][0:B, :], ccol[:, k, :], mod_w(m)[:, k, :], start=(k == 0), stop=(k == KH - 1))
                mm.then_inc(s["mod_mm"], 1)

            for m in range(MOD_EARLY):
                if m == MOD_EARLY - 1:
                    for h in range(4):
                        turn_ln(0, h, h, 4)
                mod_turn(m)
            pe.wait_ge(s["mod_ev"], 4)
            for j in range(2 * KH):
                mm = pe.transpose(ps[6][:, j * B:(j + 1) * B], modr[:, j * P:(j + 1) * P], idn[0:B, 0:B])
            mm.then_inc(s["mod_tr"], 1)

            w_slot = slots("w_in", 4)

            def project(b, i, par, which, k0, k1):
                f = b * N + i * 2 + par
                if k0 == 0:
                    pe.wait_ge(w_slot[2 * par + which], b * (8 * 16) + i * 16 + 16)
                    pe.wait_ge(s["z_done" if which else "conv_done"], f + 1)
                for k in range(k0, k1):
                    mm = pe.matmul(ps[6 + which][:], wring[:, 2 * par + which, k, :], hT[:, k, :],
                                   start=(k == 0), stop=(k == KH - 1))
                if k1 == KH:
                    mm.then_inc(s["proj_done"], 1)

            def scan(b, front, k):
                def step(i):
                    for par in range(2):
                        for g in range(NG):
                            grp = (b * N + i * 2 + par) * NG + g
                            pe.wait_ge(s["scan_done"], grp * 4 + (CR_SCAN + 4))
                            for tt in range(TT):
                                if lent(front, (g - 1) % NG, tt):
                                    pe.wait_ge(s["lent_out"], (b * N + i * 2 + par) * 2 + (1 + (g + 1) // 2))
                                elif g:
                                    pe.wait_ge(s["stt_done"], sums_before(b, i * 2 + par, g - 1, tt, front) + (CR_STT + 1))
                                else:
                                    back = sums_before(0, 1, 0, 0, front) - sums_before(0, 0, NG - 1, tt, front)
                                    pe.wait_ge(s["stt_done"], sums_before(b, i * 2 + par, 0, 0, front) + (CR_STT + 1 - back))
                                for j in range(4):
                                    mm = pe.transpose(ps[tt][:, j * P:(j + 1) * P],
                                                      hring[:, (4 * g + j) % HR, tt * P:(tt + 1) * P], idn[:])
                                mm.then_inc(s["th_done"], 1)
                                if front:
                                    k0 = 4 * (g % 2) + tt
                                    project(b + 1, i, par, g // 2, k0, k0 + 1)
                with pe.Fori(0, N // 2) as i:
                    step(i)
                barrier(pe, k)

            wo_in = slots("wo_in", 4)

            def middle(b, k, gate=True, delta=True, ln=True):
                def turn(kt):
                    pe.wait_ge(s["gate_done"], b * KD + (kt + 3))
                    for tt in range(TT):
                        mm = pe.transpose(ps[4 + kt % 2][:, tt * P:(tt + 1) * P], y_sb[:, tt, kt * P:(kt + 1) * P], idn[:])
                    mm.then_inc(s["gt_done"], 1)

                def out_products(half, kt, tiles=range(TT)):
                    t = half * 8 + kt // 2
                    if kt % 2 == 0:
                        pe.wait_ge(wo_in[t % 4], b * 64 + 16 * (t // 4 + 1))
                    for tt in tiles:
                        mm = pe.matmul(ps[4 * half + tt][:], gated(kt, tt),
                                       wring[:, t % 4].rearrange("p k c -> p (k c)")[:, (kt % 2) * 512:(kt % 2) * 512 + 512],
                                       start=(kt == 0), stop=(kt == KD - 1))
                        if kt == KD - 1:
                            mm.then_inc(s["out_done"], 1)
                    if kt == KD - 1 and TT - 1 in tiles:
                        pe.drain().then_inc(s["wo_done"], 1)
                    elif kt % 2 and TT - 1 in tiles:
                        mm.then_inc(s["wo_done"], 1)

                def turn_norms():
                    pe.wait_ge(s["bt_ready"], b + 2)
                    alone(pe)
                    for tt in range(TT):
                        mm = pe.transpose(ps[6][0:R, tt * P:(tt + 1) * P], sA[:, tt, 0:R], idn[:])
                    for tt in range(TT):
                        mm = pe.transpose(ps[7][0:N, tt * P:(tt + 1) * P], sA[:, tt, R:R + N], idn[:])
                    mm.then_inc(s["n_tr"], 1)

                def dt_product(kt):
                    if kt == 0:
                        pe.wait_ge(s["n_ev"], b * 2 + 4)
                    if kt < 4 and gate:
                        pe.wait_ge(s["half_done"], b * TT + (kt + 1))
                    pe.wait_ge(s["dt_done"], b * KD + (KD + kt + 1))
                    pe.matmul(ps[kt % 4][:], dpw[:, kt * P:(kt + 1) * P], dtr[:], start=True, stop=True
                              ).then_inc(s["dt_mm"], 1)

                if gate:
                    turn(0)
                    turn(1)
                else:
                    mod_turn(4)
                    mod_turn(5)
                for kt in range(KD):
                    if delta:
                        if kt % 4 == 0:
                            pe.wait_ge(s[f"u_in{kt // 4}"], b * 16 + 32)
                        mm = pe.matmul(ps[6][0:E, :], xpw[:, kt, :], u_sb[:, kt, :], start=(kt == 0), stop=(kt == KD - 1))
                        if kt == KD - 1:
                            mm.then_inc(s["xp_done"], 1)
                    if gate and kt + 2 < KD:
                        turn(kt + 2)
                    if gate:
                        pe.wait_ge(s["gate_done"], b * KD + (kt + 5))
                        out_products(0, kt)
                    if ln and kt >= KD - KH:
                        turn_ln(b + 2, kt - (KD - KH), 7, 1)
                if delta:
                    pe.wait_ge(s["xp_ev"], b + 2)
                    if ln:
                        pe.wait_ge(s["ne_done"], b * KH + (3 * KH + 4))
                    for tt in range(TT):
                        mm = pe.transpose(ps[7][:, tt * E:(tt + 1) * E], ssmT[:, tt * P:(tt + 1) * P], idn[0:E, 0:E])
                    mm.then_inc(s["xp_tr"], 1)
                if gate:
                    split = KD // 2
                    for kt in range(split):
                        out_products(1, kt, range(TT // 2))
                    if delta:
                        turn_norms()
                        pe.wait_ge(s["n_ev"], b * 2 + 4)
                        alone(pe)
                    for kt in range(split):
                        out_products(1, kt, range(TT // 2, TT))
                        if delta:
                            dt_product(kt)
                    count = 0
                    for tt in range(TT):
                        for kt in range(split, KD):
                            out_products(1, kt, [tt])
                            count += 1
                            if delta and count % 3 == 0 and count <= 3 * split:
                                dt_product(split + count // 3 - 1)
                else:
                    mod_turn(6)
                    turn_norms()
                    mod_turn(7)
                    for kt in range(KD):
                        dt_product(kt)
                        if kt in (2, 5, 8, 11):
                            mod_turn(8 + kt // 3)
                barrier(pe, k)

            for h in range(4, KH):
                turn_ln(0, h, h % 4, 4)
            barrier(pe, 0)
            with pe.Fori(0, N // 2) as i:
                for par in range(2):
                    for which in range(2):
                        project(0, i, par, which, 0, KH)
            barrier(pe, 1)
            middle(-1, 2, gate=False)
            with pe.Fori(0, B - 2) as b:
                scan(b, True, ph(b, 0))
                middle(b, ph(b, 1))
            scan(B - 2, True, ph(B - 2, 0))
            middle(B - 2, ph(B - 2, 1), ln=False)
            scan(B - 1, False, ph(B - 1, 0))
            middle(B - 1, ph(B - 1, 1), delta=False, ln=False)

            def logits(b):
                r = b % 2
                pe.wait_ge(s["f_ev"], 8 * (b + 1))
                for h in range(KH):
                    mm = pe.matmul(ps[4 + r][0:NL, :], wcat[:, h, :], h2T[r][:, h, :], start=(h == 0), stop=(h == KH - 1))
                mm.then_inc(s["f_mm"], 1)

            def logits_back(b):
                pe.wait_ge(s["f_lt"], b + 1)
                if b >= 2:
                    pe.wait_ge(s["f_lv"], b - 1)
                for tt in range(TT):
                    mm = pe.transpose(ps[6 + b % 2][:, tt * NL:(tt + 1) * NL], lgT[b % 2][:, tt * P:(tt + 1) * P], idn[0:NL, 0:NL])
                mm.then_inc(s["f_lg"], 1)

            for b in range(B):
                for tt in range(TT):
                    n = b * TT + tt
                    pe.wait_ge(s["f_add"], n + 1)
                    for h in range(KH):
                        bank = (tt % 2) * 2 + h // 4
                        if h % 4 == 0 and n >= 2:
                            pe.wait_ge(s["f_ev"], (n - 2) * 2 + (h // 4 + 1))
                        mm = pe.transpose(ps[bank][:, (h % 4) * P:(h % 4 + 1) * P], h2[b][:, tt, h * P:(h + 1) * P], idn[:])
                        if h % 4 == 3:
                            mm.then_inc(s["f_tr"], 1)
                    if b and tt == 1:
                        logits_back(b - 1)
                logits(b)
            logits_back(B - 1)
            barrier(pe, TAIL)
            barrier(pe, TAIL + 1)
            for k, (b, tt) in enumerate(TILES):
                pe.wait_ge(s["t3_pre"], k + 1)
                for j in range(2):
                    mm = pe.transpose(ps[tt % 2][:, j * P:(j + 1) * P], pre[:, tt, j * P:(j + 1) * P], idn[:])
                mm.then_inc(s["t3_tr"], 1)
                pe.wait_ge(s["t3_ev"], k + 1)
                for j in range(2):
                    mm = pe.matmul(ps[2 + tt % 2][:, 0:C], thx[:, (tt % 2) * C + j * P:(tt % 2) * C + (j + 1) * P],
                                   wbr[:, j, :], start=(j == 0), stop=(j == 1))
                mm.then_inc(s["t3_y"], 1)

        @block.scalar
        def _(act):
            own = Steps(act, s["act_own"])
            act.sem_inc(s["ne_done"], 4)
            act.sem_inc(s["lent_out"], 1)
            act.wait_ge(s["const_in"], 16 * 6)
            cth = sm[:].rearrange("p a b -> p (a b)")[:, 0:KH * B]
            act.activation(cth, ccol[:].rearrange("p k b -> p (k b)"), ACT.Tanh, scale=0.5).then_inc(s["a_ready"], 1)
            act.activation(alog[:], alog[:], ACT.Exp).then_inc(s["a_ready"], 1)
            act.activation(gcol[:, 1:2], gcol[:, 0:1], ACT.Exp, scale=-1.0).then_inc(s["a_ready"], 1)

            def evict_mod(m):
                act.wait_ge(s["mod_mm"], m + 1)
                c = MOD_ORDER[m]
                dst = modr[:, c * T:(c + 1) * T] if c < 4 else modg[:, (c - 4) * T:(c - 3) * T]
                act.activation(dst, ps[4 + m % 2][0:B, :], ACT.Identity, bias=1.0 if c in (8, 9) else 0.0, scale=0.5
                               ).then_inc(s["mod_ev"], 1)

            def ln_rstd(b):
                act.wait_ge(s["var_ready"], b + 1)
                own.link(act.activation(sm[:, 0:TT, 1], sm[:, 0:TT, 0], ACT.Ln))
                act.activation(sm[:, 0:TT, 1], sm[:, 0:TT, 1], ACT.Exp, scale=-0.5).then_inc(s["rstd_ready"], 1)

            for m in range(MOD_EARLY - 1):
                evict_mod(m)
            act.preload_act_table_set("natural_log_exp_and_others")
            ln_rstd(0)
            evict_mod(MOD_EARLY - 1)

            def evict_ln(b, h, bank):
                if h == 0:
                    act.wait_ge(s["mc_ready"], b + 1)
                act.wait_ge(s["nt_done"], b * KH + (h + 1))
                act.activation(hT[:, h, :], ps[bank][:], ACT.Identity, bias=mcur[:, h:h + 1],
                               scale=mcur[:, KH + h:KH + h + 1]).then_inc(s["ne_done"], 1)

            def first_tap(b, i, par):
                f = b * N + i * 2 + par
                act.wait_ge(s["proj_done"], f * 2 + (CR_PROJ + 1))
                act.wait_ge(s["xc_done"], f + 1)
                act.activation(acc[:, par, :], ps[6][:], ACT.Identity, bias=kcur[:, par, F_BIAS:F_BIAS + 1],
                               scale=kcur[:, par, F_TAP + K - 1:F_TAP + K]).then_inc(s["tap_done"], 1)

            def tanh_x(b, i, par):
                f = b * N + i * 2 + par
                act.wait_ge(s["conv_done"], f + 2)
                act.wait_ge(s["xc_done"], f + 2)
                act.activation(thx[:], acc[:, par, :], ACT.Tanh).then_inc(s["thx_done"], 1)

            def tanh_z(b, i, par):
                f = b * N + i * 2 + par
                act.wait_ge(s["proj_done"], f * 2 + (CR_PROJ + 2))
                act.wait_ge(s["z_done"], f + 1)
                act.activation(thz[:], ps[7][:], ACT.Tanh, scale=0.5).then_inc(s["thz_done"], 1)

            def scan(b, front, k):
                def lend(i, par, g):
                    n = b * N + i * 2 + par
                    act.wait_ge(s["th_done"], (n * NG + g) * 4 + (CR_TH + TT))
                    act.wait_ge(s["lent_sum"], n * 2 + (1 + g // 2))
                    act.activation(lent_sb[:, g // 2, :], ps[TT - 1][:], ACT.Copy,
                                   scale=kcur[:, par, F_C + TT - 1:F_C + TT]).then_inc(s["lent_out"], 1)

                def step(i, first):
                    for par in range(2):
                        pi, pp = (i, 0) if par else (i - 1, 1)
                        act.wait_ge(s["kcur_ready"], b * (N + 1) + i * 2 + (N + par + 1))
                        for kt in range(KD):
                            if front and kt == 8 and not (first and par == 0):
                                tanh_z(b + 1, pi, pp)
                            if front and kt == 5 and not (first and par == 0):
                                tanh_x(b + 1, pi, pp)
                            if front and kt == LEND_AT[1] and not (first and par == 0):
                                lend(pi, pp, LENT[1])
                            if front and kt == LEND_AT[0]:
                                lend(i, par, LENT[0])
                            if front and kt == 14:
                                first_tap(b + 1, i, par)
                            g = (b * N + i * 2 + par) * KD + kt
                            act.wait_ge(s["scan_done"], g + (CR_SCAN - 1))
                            act.activation(ps[4 + kt % 2][:], dt_sb[:, kt, :], ACT.Exp, scale=kcur[:, par, kt:kt + 1]
                                           ).then_inc(s["da_ready"], 1)
                step(0, True)
                with act.Fori(1, N // 2) as i:
                    step(i, False)
                if front:
                    lend(N // 2 - 1, 1, LENT[1])
                    tanh_x(b + 1, N // 2 - 1, 1)
                    tanh_z(b + 1, N // 2 - 1, 1)
                barrier(act, k)

            def middle(b, k, gate=True, delta=True, ln=True):
                act.preload_act_table_set("natural_log_exp_and_others")
                if not gate:
                    evict_mod(4)
                    evict_mod(5)
                if ln:
                    ln_rstd(b + 2)
                    for h in range(KH):
                        evict_ln(b + 2, h, 7)
                if delta:
                    act.wait_ge(s["xp_done"], b + 2)
                    act.activation(ssmT, ps[6][0:E, :], ACT.Copy).then_inc(s["xp_ev"], 1)
                if delta:
                    act.wait_ge(s["rms_sq"], b + 2)
                    own.link(act.activation(ms[:, :, 1, :], ms[:, :, 0, :], ACT.Ln))
                    act.activation(ms[:, :, 1, :], ms[:, :, 1, :], ACT.Exp, scale=-0.5).then_inc(s["rms_rs"], 1)
                    if not gate:
                        evict_mod(6)
                    act.wait_ge(s["n_tr"], b + 2)
                    act.activation(dtr[0:R, :], ps[6][0:R, :], ACT.Copy, scale=dtln[:]).then_inc(s["n_ev"], 1)
                    act.activation(bT, ps[7][0:N, :], ACT.Copy).then_inc(s["n_ev"], 1)
                    if not gate:
                        evict_mod(7)
                    for kt in range(KD):
                        if not gate and kt in (4, 7, 10, 13):
                            evict_mod(7 + kt // 3)
                        act.wait_ge(s["dt_mm"], b * KD + (KD + kt + 1))
                        act.wait_ge(s["dt_done"], b * KD + (KD + kt + 2))
                        e = e3[kt % 3]
                        own.link(act.activation(e, ps[kt % 4][:], ACT.Abs))
                        own.link(act.activation(e, e, ACT.Exp, scale=-1.0))
                        act.activation(l3[kt % 3], e, ACT.Ln, bias=1.0).then_inc(s["e_done"], 1)
                barrier(act, k)

            for h in range(KH):
                evict_ln(0, h, h % 4)
            barrier(act, 0)
            with act.Fori(0, N // 2) as i:
                for par in range(2):
                    act.wait_ge(s["kcur_ready"], i * 2 + (par + 1))
                    first_tap(0, i, par)
                    tanh_x(0, i, par)
                    tanh_z(0, i, par)
            barrier(act, 1)
            middle(-1, 2, gate=False)
            per_loop = 1 + 1 + 2 * KD
            with act.Fori(0, B - 2) as b:
                own.enter(b, per_loop)
                scan(b, True, ph(b, 0))
                middle(b, ph(b, 1))
            own.leave(B - 2, per_loop)
            scan(B - 2, True, ph(B - 2, 0))
            middle(B - 2, ph(B - 2, 1), ln=False)
            scan(B - 1, False, ph(B - 1, 0))
            middle(B - 1, ph(B - 1, 1), delta=False, ln=False)

            act.preload_act_table_set("natural_log_exp_and_others")
            act.wait_ge(s["f_var"], 1)
            own.link(act.activation(sm[:, :, 1], sm[:, :, 0], ACT.Ln))
            act.activation(sm[:, :, 1], sm[:, :, 1], ACT.Exp, scale=-0.5).then_inc(s["f_rstd"], 1)
            def logits_out(b):
                act.wait_ge(s["f_mm"], b + 1)
                if b >= 2:
                    act.wait_ge(s["f_lg"], b - 1)
                act.activation(lgT[b % 2], ps[4 + b % 2][0:NL, :], ACT.Copy).then_inc(s["f_lt"], 1)

            for b in range(B):
                for tt in range(TT):
                    n = b * TT + tt
                    for j in range(2):
                        act.wait_ge(s["f_tr"], n * 2 + (j + 1))
                        if b >= 2 and tt == 0 and j == 0:
                            act.wait_ge(s["f_mm"], b - 1)
                        act.activation(h2T[b % 2][:, 4 * j:4 * j + 4, tt * P:(tt + 1) * P],
                                       ps[(tt % 2) * 2 + j][:].rearrange("p (k c) -> p k c", c=P), ACT.Copy
                                       ).then_inc(s["f_ev"], 1)
                    if n:
                        act.wait_ge(s["f_sq"], n)
                    act.activation(trash, h2[b][:, tt, :], ACT.Square, accum_out=Lall[:, n, NL:NL + 1]
                                   ).then_inc(s["f_sq"], 1)
                    if b and tt == 0:
                        logits_out(b - 1)
            logits_out(B - 1)
            barrier(act, TAIL)

            act.preload_act_table_set("natural_log_exp_and_others")
            for k, steps in enumerate(sink_requests):
                act.wait_ge(s["ask"], k + 1)
                for n, (dst, src, func, scale) in enumerate(steps):
                    ins = act.activation(dst, src, func, scale=scale)
                    if n < len(steps) - 1:
                        own.link(ins)
                    else:
                        ins.then_inc(s["answer"], 1)
            barrier(act, TAIL + 1)

            def first_terms(k):
                b, tt = TILES[k]
                if k >= 4:
                    act.wait_ge(s["t3_mix"], k + 1)
                h = h2[b][:, tt, 0:C]
                Hw = Hall[:, b * TT + tt, :]
                act.activation(pre[:, tt, :], h, ACT.Copy, scale=Hw[:, 16:17])
                for j in range(S):
                    ins = act.activation(mixb[:, tt, j * C:(j + 1) * C], h, ACT.Copy, scale=Hw[:, 4 * j:4 * j + 1])
                ins.then_inc(s["t3_first"], 1)
                if k == len(TILES) - 1:
                    return
                if k >= 2:
                    act.wait_ge(s["t3_second"], k - 1)
                for n in range(2):
                    ins = act.activation(second[k % 2][:, n * C:(n + 1) * C], h2[b][:, tt, C:2 * C], ACT.Copy, scale=Hw[:, 4 * n + 1:4 * n + 2])
                ins.then_inc(s["t3_sec"], 1)

            first_terms(0)
            first_terms(1)
            for k, (b, tt) in enumerate(TILES):
                act.wait_ge(s["t3_tr"], k + 1)
                act.activation(thx[:, (tt % 2) * C:(tt % 2) * C + C], ps[tt % 2][:, 0:C], ACT.Copy
                               ).then_inc(s["t3_ev"], 1)
                if k + 2 < len(TILES):
                    first_terms(k + 2)

        @block.gpsimd
        def _(pool):
            pool.sem_inc(s["v_ready"], CR_V)
            pool.sem_inc(s["t3_mix"], 4)
            pool.sem_inc(s["lent_sum"], 2)
            for k in range(2):
                barrier(pool, k)

            def scan(b, front, k):
                b_in = slots("b_in", 2)

                def y_lent(g):
                    return y_sb[:, TT - 1, g * 512:(g + 1) * 512]

                def add_lent(i, par, g):
                    pool.wait_ge(s["lent_out"], (b * N + i * 2 + par) * 2 + (2 + g // 2))
                    pool.tensor_tensor(y_lent(g), y_lent(g), lent_sb[:, g // 2, :], ALU.add).then_inc(s["lent_sum"], 1)

                def step(i, first):
                    for par in range(2):
                        pool.wait_ge(b_in[par], b * (8 * 16) + i * 16 + 16)
                        for kt in range(KD):
                            g = (b * N + i * 2 + par) * KD + kt
                            pool.wait_ge(s["scan_done"], g + (CR_SCAN - VR + 1))
                            if first and par == 0 and kt < TT:
                                pool.wait_ge(s[f"x1_st{kt}"], b * 32 + 32)
                            pool.tensor_tensor(vring[:, kt % VR, :], u_sb[:, kt, :], bbc[:, par, :], ALU.mult
                                               ).then_inc(s["v_ready"], 1)
                            if front and kt in ADD_AT and not (first and par == 0):
                                add_lent(*((i, 0) if par else (i - 1, 1)), LENT[ADD_AT.index(kt)])
                if front:
                    for g in LENT:
                        ins = pool.memset(y_lent(g), 0.0)
                    ins.then_inc(s["y_zero"], 1)
                    pool.wait_ge(s["y_zero"], b + 1)
                step(0, True)
                with pool.Fori(1, N // 2) as i:
                    step(i, False)
                if front:
                    for g in LENT:
                        add_lent(N // 2 - 1, 1, g)
                barrier(pool, k)

            def middle(b, k, delta=True):
                if delta:
                    for kt in range(KD):
                        pool.wait_ge(s["nw_done"], b * KD + (KD + kt + 1))
                        pool.tensor_tensor(c3[kt % 3], e3[kt % 3], c3[kt % 3], ALU.subtract).then_inc(s["q_done"], 1)
                barrier(pool, k)

            middle(-1, 2)
            with pool.Fori(0, B - 2) as b:
                scan(b, True, ph(b, 0))
                middle(b, ph(b, 1))
            scan(B - 2, True, ph(B - 2, 0))
            middle(B - 2, ph(B - 2, 1))
            scan(B - 1, False, ph(B - 1, 0))
            middle(B - 1, ph(B - 1, 1), delta=False)
            for b in range(B):
                for tt in range(TT):
                    pool.wait_ge(s["f_mul"], b * TT + tt + 1)
                    pool.tensor_tensor(h2[b][:, tt, :], h2[b][:, tt, :], frow[b % 2][:, 1, :], ALU.add
                                       ).then_inc(s["f_add"], 1)
            barrier(pool, TAIL)
            barrier(pool, TAIL + 1)
            for k, (b, tt) in enumerate(TILES[:-1]):
                r = b % 2
                if tt == 0:
                    pool.wait_ge(s[f"t3_in{r}"], 16 if k < 2 * TT else 48)
                pool.wait_ge(s["t3_sum"], k + 1)
                pool.wait_ge(s["t3_sec"], k + 1)
                pool.tensor_tensor(mixb[:, tt, 0:2 * C], mixb[:, tt, 0:2 * C], second[k % 2], ALU.add).then_inc(s["t3_second"], 1)
                pool.wait_ge(s["t3_second"], k + 1)
                pool.tensor_tensor(mixb[:, tt, :], mixb[:, tt, :], gbrow[r], ALU.mult).then_inc(s["t3_gb"], 1)
                pool.wait_ge(s["t3_gb"], k + 1)
                pool.tensor_tensor(x1[r][:, tt, :], x1[r][:, tt, :], mixb[:, tt, :], ALU.add
                                   ).then_inc(s["t3_mix"], 1)

        @block.vector
        def _(dve):
            own = Steps(dve, s["dve_own"])
            for name, credit in (("scan_done", CR_SCAN), ("stt_done", CR_STT), ("conv_done", 1), ("z_done", 1),
                                 ("xc_done", 2), ("gate_done", 4), ("dt_done", 4)):
                dve.sem_inc(s[name], credit)

            def ts(out_, in_, a, b_, op0, op1=None):
                return dve.tensor_scalar(out_, in_, a, b_, op0, op1) if op1 is not None else dve.tensor_scalar(out_, in_, a, None, op0)

            def newton(r, v, t):
                own.link(dve.tensor_tensor(t, r, r, ALU.mult))
                own.link(dve.tensor_tensor(t, t, v, ALU.mult))
                own.link(ts(t, t, -0.5, 1.5, ALU.mult, ALU.add))
                own.link(dve.tensor_tensor(r, r, t, ALU.mult))

            own.mark(dve.memset(cols[:], 0.0))
            dve.memset(dtr[R:R + 1, :], 1.0)
            dve.wait_ge(s["const_in"], 16 * 6)
            dve.wait_ge(s["dve_own"], own.done())
            ts(cols[:, 0:N, F_TAP:F_TAP + K], cw[:], 0.5, None, ALU.mult)
            ts(cols[:, 0:N, F_BIAS], cb[:], 0.5, None, ALU.mult)
            dve.wait_ge(s["a_ready"], 2)
            ts(cols[:, 0:N, 0:KD], alog[:], -1.0, None, ALU.mult)
            cth = sm[:].rearrange("p a b -> p (a b)")[:, 0:KH * B]
            ccf = ccol[:].rearrange("p k b -> p (k b)")
            dve.scalar_tensor_tensor(ccf, cth, 1.0, ccf, ALU.add, ALU.mult).then_inc(s["silu_c"], 1)
            dve.wait_ge(s["a_ready"], 3)
            own.link(ts(gcol[:, 1:2], gcol[:, 1:2], 1.0, None, ALU.add))
            own.link(dve.reciprocal(gcol[:, 2:3], gcol[:, 1:2]))
            own.link(ts(gcol[:, 3:4], gcol[:, 2:3], -1.0, 1.0, ALU.mult, ALU.add))
            def norm_stats(b):
                for tt in range(TT):
                    dve.wait_ge(s[f"x_in{tt}"], b * 16 + 16)
                    for half in range(2):
                        ins = dve.bn_stats(st[:, tt, half, :], x4[:, tt, 512 * half:512 * half + 512])
                own.link(ins)
                alone(dve)
                for tt in range(TT):
                    ins = dve.bn_aggr(mv[:, tt, :], st[:, tt].rearrange("p a b -> p (a b)"))
                own.link(ins)
                ts(sm[:, 0:TT, 0], mv[:, :, 1], EPS_LN, None, ALU.add).then_inc(s["var_ready"], 1)

            def mod_columns(b):
                ts(mcur[:], modc[:, bass.ds(b, 1), :].rearrange("p o j -> p (o j)"), 1.0, None, ALU.mult
                   ).then_inc(s["mc_ready"], 1)

            def norm_apply(b):
                dve.wait_ge(s["rstd_ready"], b + 1)
                newton(sm[:, 0:TT, 1], sm[:, 0:TT, 0], sm[:, 0:TT, 2])
                for tt in range(TT):
                    ts(x4[:, tt, :], x4[:, tt, :], mv[:, tt, 0:1], sm[:, tt, 1:2], ALU.subtract, ALU.mult
                       ).then_inc(s["xn_done"], 1)

            dve.wait_ge(s["silu_c"], 1)
            norm_stats(0)
            norm_apply(0)
            dve.wait_ge(s["mod_tr"], 1)
            pv = ps[6][:, 0:2 * KH * B].rearrange("p (j b) -> p b j", b=B)
            dve.tensor_copy(modc[:, :, 0:KH], pv[:, :, 0:KH])
            own.link(ts(modc[:, :, KH:2 * KH], pv[:, :, KH:2 * KH], 1.0, None, ALU.add))
            mod_columns(0)
            barrier(dve, 0)

            def columns(n, par):
                ts(kcur[:, par, :], cols[:, bass.ds(n, 1), :].rearrange("p o j -> p (o j)"), 1.0, None, ALU.mult
                   ).then_inc(s["kcur_ready"], 1)

            def tap(b, i, par, q):
                f = b * N + i * 2 + par
                if q == 1:
                    dve.wait_ge(s["tap_done"], f + 1)
                else:
                    dve.wait_ge(s["dve_own"], own.done())
                ins = dve.scalar_tensor_tensor(acc[:, par, q:T], ps[6][:, 0:T - q], kcur[:, par, F_TAP + K - 1 - q:F_TAP + K - q],
                                               acc[:, par, q:T], ALU.mult, ALU.add)
                if q == K - 1:
                    ins.then_inc(s["conv_done"], 1)
                else:
                    own.mark(ins)

            def finish_x(b, i, par):
                f = b * N + i * 2 + par
                dve.wait_ge(s["thx_done"], f + 1)
                dve.wait_ge(s[f"xc_st{par}"], b * (8 * 16) + i * 16 + 16)
                dve.scalar_tensor_tensor(xcb[:, par, :], thx[:], 1.0, acc[:, par, :], ALU.add, ALU.mult
                                         ).then_inc(s["xc_done"], 1)

            def finish_z(b, i, par):
                f = b * N + i * 2 + par
                dve.wait_ge(s["thz_done"], f + 1)
                dve.wait_ge(s[f"z_st{par}"], b * (8 * 16) + i * 16 + 16)
                dve.scalar_tensor_tensor(szb[:, par, :], thz[:], 1.0, ps[7][:], ALU.add, ALU.mult
                                         ).then_inc(s["z_done"], 1)

            def scan(b, front, k):
                def over_states(b, i, par, g, tt, zeroth):
                    grp = (b * N + i * 2 + par) * NG + g
                    dve.wait_ge(s["th_done"], grp * 4 + (CR_TH + tt + 1))
                    yv = y_sb[:, tt, g * 512:(g + 1) * 512]
                    c_n = kcur[:, par, F_C + tt:F_C + tt + 1]
                    if zeroth:
                        ins = ts(yv, ps[tt][:], c_n, None, ALU.mult)
                    else:
                        ins = dve.scalar_tensor_tensor(yv, ps[tt][:], c_n, yv, ALU.mult, ALU.add)
                    ins.then_inc(s["stt_done"], 1)

                def step(i, first):
                    for par in range(2):
                        pi, pp = (i, 0) if par else (i - 1, 1)
                        before = not (first and par == 0)
                        for kt in range(KD):
                            g = (b * N + i * 2 + par) * KD + kt
                            grp = (b * N + i * 2 + par) * NG + kt // 4
                            if kt % 4 == 0:
                                dve.wait_ge(s["th_done"], grp * 4 + 4)
                            dve.wait_ge(s["v_ready"], g + (CR_V + 1))
                            dve.wait_ge(s["da_ready"], g + 1)
                            dve.tensor_tensor_scan(hring[:, kt % HR, :], ps[4 + kt % 2][:], vring[:, kt % VR, :], 0.0,
                                                   ALU.mult, ALU.add).then_inc(s["scan_done"], 1)
                            if kt == 4:
                                dve.wait_ge(s["kcur_ready"], b * (N + 1) + i * 2 + (N + par + 1))
                            if not lent(front, (kt // 4 - 1) % NG, kt % 4):
                                if kt >= 4:
                                    over_states(b, i, par, kt // 4 - 1, kt % 4, first and par == 0)
                                elif before:
                                    over_states(b, pi, pp, NG - 1, kt % 4, first and par == 1)
                            if kt == 8:
                                columns(i * 2 + (par + 1), 1 - par)
                            if front and before:
                                if kt < 3:
                                    tap(b + 1, pi, pp, kt + 1)
                                if kt == 7:
                                    finish_x(b + 1, pi, pp)
                                if kt == 10:
                                    finish_z(b + 1, pi, pp)
                per = 4 if front else 0
                columns(0, 0)
                step(0, True)
                with dve.Fori(1, N // 2) as i:
                    own.enter(i - 1, per)
                    step(i, False)
                own.leave(N // 2 - 1, per)
                for tt in range(TT):
                    if not lent(front, NG - 1, tt):
                        over_states(b, N // 2 - 1, 1, NG - 1, tt, False)
                if front:
                    for q in range(1, K):
                        tap(b + 1, N // 2 - 1, 1, q)
                    finish_x(b + 1, N // 2 - 1, 1)
                    finish_z(b + 1, N // 2 - 1, 1)
                barrier(dve, k)

            def middle(b, k, gate=True, delta=True, ln=True):
                def evict(half, tt):
                    dve.wait_ge(s["out_done"], b * 8 + (4 * half + tt + 1))
                    if tt == 0:
                        dve.wait_ge(s["res_in"], b * 128 + 64 * (half + 1))
                    if tt == 0 and half == 0:
                        dve.wait_ge(s["row_in"], b * 16 + 16)
                        if ln:
                            dve.wait_ge(s["nt_done"], b * KH + 3 * KH)
                    ins = dve.tensor_tensor(prod[:, tt % 2, :], ps[4 * half + tt][:], row[:, 512 * half:512 * half + 512], ALU.mult)
                    if half == 0:
                        ins.then_inc(s["half_done"], 1)
                        dve.wait_ge(s["half_done"], b * TT + (tt + 1))
                    else:
                        own.link(ins)
                    own.link(dve.tensor_tensor(xres[:, tt, :], prod[:, tt % 2, :], xres[:, tt, :], ALU.add))
                    dve.bn_stats(st2[:, tt, half, :], xres[:, tt, :]).then_inc(s["x1_done"], 1)
                    if half:
                        dve.wait_ge(s["x1_done"], b * 8 + (4 + tt + 1))
                        alone(dve)
                        ins = dve.bn_aggr(mv2[:, tt, :], st2[:, tt].rearrange("p a b -> p (a b)"))
                    if half and tt == TT - 1:
                        own.link(ins)
                        ts(mv2all[:].rearrange("p (b q) l -> p b (q l)", b=B)[:, bass.ds(b, 1), :].rearrange("p o j -> p (o j)"),
                           mv2[:].rearrange("p q l -> p (q l)"), 1.0, None, ALU.mult)

                for kt in range(KD):
                    if gate:
                        dve.wait_ge(s["gt_done"], b * KD + (kt + 1))
                        dve.wait_ge(s[f"g_in{kt % 4}"], b * (4 * 32) + 32 * (kt // 4 + 1))
                        own.link(dve.scalar_tensor_tensor(acc[:, kt % 2, :], gx[kt % 4], dsc[:, kt:kt + 1],
                                                          ps[4 + kt % 2][:], ALU.mult, ALU.add))
                        dve.scalar_tensor_tensor(y_sb[:, :, kt * P:(kt + 1) * P],
                                                 acc[:, kt % 2, :].rearrange("p (q c) -> p q c", q=TT), 0.5,
                                                 gz[kt % 4].rearrange("p (q c) -> p q c", q=TT), ALU.mult, ALU.mult
                                                 ).then_inc(s["gate_done"], 1)
                    if ln and kt == 6:
                        mod_columns(b + 2)
                        norm_stats(b + 2)
                    if ln and kt == 7:
                        norm_apply(b + 2)
                if not gate:
                    finish_mod(2, 6)
                if delta:
                    norms(b + 1)
                if gate:
                    for tt in range(TT):
                        evict(0, tt)
                after = {10: 0, 13: 1, 15: 2} if gate and delta else {}
                if delta:
                    softplus(b + 1, not gate, lambda kt: kt in after and evict(1, after[kt]))
                if gate:
                    for tt in range(len(after), TT):
                        evict(1, tt)
                barrier(dve, k)

            def norms(b):
                dve.wait_ge(s["xp_tr"], b + 1)
                own.link(dve.tensor_copy(sA, ps[7][:, 0:TT * E].rearrange("p (q e) -> p q e", q=TT)))
                own.link(dve.tensor_tensor(sq, sA, sA, ALU.mult))
                for j, (lo, hi) in enumerate(((0, R), (R, R + N), (R + N, E))):
                    own.link(dve.tensor_reduce(ms[:, :, 0, j], sq[:, :, lo:hi], AX, ALU.add))
                    ins = ts(ms[:, :, 0, j], ms[:, :, 0, j], 1.0 / (hi - lo), EPS_RMS, ALU.mult, ALU.add)
                ins.then_inc(s["rms_sq"], 1)
                dve.wait_ge(s["rms_rs"], b + 1)
                newton(ms[:, :, 1, :], ms[:, :, 0, :], ms[:, :, 2, :])
                for tt in range(TT):
                    for j, (lo, hi) in enumerate(((0, R), (R, R + N), (R + N, E))):
                        ins = ts(sA[:, tt, lo:hi], sA[:, tt, lo:hi], ms[:, tt, 1, j:j + 1], None, ALU.mult)
                own.link(ins)
                for tt in range(TT):
                    dve.tensor_tensor(sA[:, tt, R:R + N], sA[:, tt, R:R + N], blnw[:, 0:N], ALU.mult)
                    ins = dve.tensor_tensor(cols[:, 0:N, F_C + tt], sA[:, tt, R + N:E], blnw[:, N:2 * N], ALU.mult)
                ins.then_inc(s["bt_ready"], 1)

            def finish_mod(j, turns):
                dve.wait_ge(s["mod_ev"], turns)
                g = modg[:, (j - 2) * H:(j - 1) * H]
                t0, t1 = acc[0:B].rearrange("p a t -> p (a t)"), row[0:B, :]
                own.link(ts(t0, g, -1.0, None, ALU.mult))
                own.link(dve.tensor_tensor(t0, t0, g, ALU.max))
                own.link(ts(t0, t0, G_MIN, None, ALU.max))
                own.link(ts(t1, g, 0.0, 2.0, ALU.is_ge, ALU.mult))
                dve.scalar_tensor_tensor(g, t1, -1.0, t0, ALU.add, ALU.mult).then_inc(s["mod_rows"], 1)
                dve.wait_ge(s["mod_rows"], 1 if j == 2 else 2)

            def softplus(b, mod, between):
                def rounded(kt):
                    dve.wait_ge(s["e_done"], b * KD + (kt + 1))
                    ts(c3[kt % 3], e3[kt % 3], 1.0, -1.0, ALU.add, ALU.add).then_inc(s["nw_done"], 1)
                    own.mark(dve.scalar_tensor_tensor(dt_sb[:, kt, :], ps[kt % 4][:], 0.0, l3[kt % 3], ALU.max, ALU.add))
                rounded(0)
                for kt in range(KD):
                    if mod and kt == 4:
                        finish_mod(5, 8)
                    summed = own.done()
                    if kt + 1 < KD:
                        rounded(kt + 1)
                    dve.wait_ge(s["dve_own"], summed)
                    dve.wait_ge(s["q_done"], b * KD + (kt + 1))
                    own.link(dve.tensor_tensor(dt_sb[:, kt, :], dt_sb[:, kt, :], c3[kt % 3], ALU.add))
                    dve.tensor_tensor(u_sb[:, kt, :], dt_sb[:, kt, :], u_sb[:, kt, :], ALU.mult).then_inc(s["dt_done"], 1)
                    between(kt)

            with dve.Fori(0, N // 2) as i:
                own.enter(i, 4)
                for par in range(2):
                    columns(i * 2 + par, par)
                    dve.wait_ge(s["kcur_ready"], i * 2 + (par + 1))
                    for q in range(1, K):
                        tap(0, i, par, q)
                    finish_x(0, i, par)
                    finish_z(0, i, par)
            own.leave(N // 2, 4)
            barrier(dve, 1)
            middle(-1, 2, gate=False)
            per_loop = 2 * N + (KD + 6 + 3 * TT + 1) + (2 + 3 + 4 + 1) + 2 * KD
            with dve.Fori(0, B - 2) as b:
                own.enter(b, per_loop)
                scan(b, True, ph(b, 0))
                middle(b, ph(b, 1))
            own.leave(B - 2, per_loop)
            scan(B - 2, True, ph(B - 2, 0))
            middle(B - 2, ph(B - 2, 1), ln=False)
            scan(B - 1, False, ph(B - 1, 0))
            middle(B - 1, ph(B - 1, 1), delta=False, ln=False)

            ts(sm[:, :, 0], mv2all[:, :, 1], EPS_LN, None, ALU.add).then_inc(s["f_var"], 1)
            dve.wait_ge(s["f_rstd"], 1)
            newton(sm[:, :, 1], sm[:, :, 0], sm[:, :, 2])
            own.link(dve.tensor_copy(mv2all[:, :, 1], sm[:, :, 1]))
            def logits(b):
                dve.wait_ge(s["f_lg"], b + 1)
                dve.tensor_copy(Lall[:, b * TT:(b + 1) * TT, 0:NL],
                                ps[6 + b % 2][:, 0:TT * NL].rearrange("p (q l) -> p q l", q=TT)).then_inc(s["f_lv"], 1)

            for b in range(B):
                r = b % 2
                dve.wait_ge(s[f"f_in{r}"], 48 * (b // 2 + 1))
                for tt in range(TT):
                    n = b * TT + tt
                    own.link(ts(h2[b][:, tt, :], x1[r][:, tt, :], mv2all[:, n, 0:1], mv2all[:, n, 1:2], ALU.subtract, ALU.mult))
                    dve.tensor_tensor(h2[b][:, tt, :], h2[b][:, tt, :], frow[r][:, 0, :], ALU.mult).then_inc(s["f_mul"], 1)
                if b:
                    logits(b - 1)
            logits(B - 1)
            barrier(dve, TAIL)

            asked = [0]

            def ask(ins):
                asked[0] += 1
                ins.then_inc(s["ask"], 1)
                dve.wait_ge(s["answer"], asked[0])

            def v4(t):
                return t.rearrange("p (q i j) -> p q i j", i=S, j=S)

            def flat(t):
                return t.rearrange("p (r j) -> p r j", j=S)

            def tt_i(dst, a, v, op):
                w = v.rearrange("p (q o j) -> p q o j", o=1, j=S).to_broadcast([P, v.shape[1] // S, S, S])
                return dve.tensor_tensor(v4(dst), v4(a), w, op)

            def tt_j(dst, a, u, op):
                w = u.rearrange("p (r o) -> p r o", o=1).to_broadcast([P, u.shape[1], S])
                return dve.tensor_tensor(flat(dst), flat(a), w, op)

            def red_j(dst, a, op):
                return dve.tensor_reduce(dst.rearrange("p (r o) -> p r o", o=1), flat(a), AX, op)

            def red_i(dst, a, op):
                return dve.tensor_reduce(flat(dst), a.rearrange("p (q i j) -> p q j i", i=S, j=S), AX, op)

            dve.wait_ge(s["f_lv"], B)
            ask(ts(rs0, Lall[:, :, NL], 1.0 / H, EPS_FFN, ALU.mult, ALU.add))
            newton(rs1, rs0, skv(13, NT))
            for q in range(NT):
                own.mark(dve.scalar_tensor_tensor(Lall[:, q, 0:NL], Lall[:, q, 0:NL], rs1[:, q:q + 1], base[:], ALU.mult, ALU.add))
            dve.wait_ge(s["dve_own"], own.done())
            PL = Lall[:, :, S * S:NL].rearrange("p q (g j) -> p q g j", g=2)
            pm3 = pm.rearrange("p (q g) -> p q g", q=NT)
            psu3 = psu.rearrange("p (q g) -> p q g", q=NT)
            pmb = pm.rearrange("p (q g o) -> p q g o", q=NT, o=1).to_broadcast([P, NT, 2, S])
            psb = psu.rearrange("p (q g o) -> p q g o", q=NT, o=1).to_broadcast([P, NT, 2, S])
            Pv = Pb.rearrange("p (q g j) -> p q g j", q=NT, g=2)
            Ev = Eb.rearrange("p (q g j) -> p q g j", q=NT, g=2)
            own.link(dve.tensor_reduce(pm3, PL, AX, ALU.max))
            ask(dve.tensor_tensor(Pv, PL, pmb, ALU.subtract))
            own.link(dve.tensor_reduce(psu3, Ev, AX, ALU.add))
            own.link(dve.reciprocal(psu, psu))
            own.link(dve.tensor_tensor(Hall[:, :, S * S:NL].rearrange("p q (g j) -> p q g j", g=2), Ev, psb, ALU.mult))
            own.link(ts(Zb.rearrange("p (q r) -> p q r", q=NT), Lall[:, :, 0:S * S], 1.0 / TAU, None, ALU.mult))
            own.link(red_j(Mb, Zb, ALU.max))
            ask(tt_j(Kb, Zb, Mb, ALU.subtract))
            ask(red_j(Sb_, Tb, ALU.add))
            own.link(dve.scalar_tensor_tensor(Ub, Sb_, -1.0, Mb, ALU.mult, ALU.subtract))
            own.link(tt_j(Zb, Zb, Ub, ALU.add))
            own.link(red_i(Mb, Zb, ALU.max))
            ask(tt_i(Kb, Zb, Mb, ALU.subtract))
            ask(red_i(Sb_, Tb, ALU.add))
            own.link(dve.scalar_tensor_tensor(Vb, Sb_, -1.0, Mb, ALU.mult, ALU.subtract))
            ask(tt_i(Zb, Zb, Vb, ALU.add))
            def halves(t):
                n = t.shape[1] // 2
                return [t[:, 0:n], t[:, n:2 * n]]

            Kh, Th, Sh, uh, vh = [halves(t) for t in (Kb, Tb, Sb_, ub, vb)]

            def balance(last):
                steps = [lambda a: tt_i(Th[a], Kh[a], vh[a], ALU.mult),
                         lambda a: red_j(Sh[a], Th[a], ALU.add),
                         lambda a: dve.reciprocal(uh[a], Sh[a]),
                         lambda a: tt_j(Th[a], Kh[a], uh[a], ALU.mult),
                         lambda a: red_i(Sh[a], Th[a], ALU.add),
                         lambda a: dve.reciprocal(vh[a], Sh[a])]
                for k, step in enumerate(steps):
                    for a in range(2):
                        dve.wait_ge(s["dve_own"], own.done() - 1)
                        ins = step(a)
                        if last and k == len(steps) - 1 and a:
                            last(ins)
                        else:
                            own.mark(ins)

            left = ITERS - 1
            for r in range(3):
                turns = left if r == 2 else REFRESH
                left -= turns
                loops, rest = (turns - 1) // STEP, (turns - 1) % STEP
                own.link(dve.memset(vb, 1.0))
                with dve.Fori(0, loops) as it:
                    own.enter(it, 12 * STEP)
                    for _ in range(STEP):
                        balance(None)
                own.leave(loops, 12 * STEP)
                for _ in range(rest):
                    balance(None)
                balance(ask)
                own.link(tt_j(Zb, Zb, lnu, ALU.add))
                ask(tt_i(Zb, Zb, lnv, ALU.add))
            own.link(ts(Hall[:, :, 0:S * S], Kb.rearrange("p (q r) -> p q r", q=NT), gcol[:, 2:3], None, ALU.mult))
            own.link(ts(Hall[:, :, 0:S * S:S + 1], Hall[:, :, 0:S * S:S + 1], gcol[:, 3:4], None, ALU.add))
            barrier(dve, TAIL + 1)

            def sums(k):
                b, tt = TILES[k]
                h = [h2[b][:, tt, j * C:(j + 1) * C] for j in range(S)]
                Hw = Hall[:, b * TT + tt, :]
                dve.wait_ge(s["t3_first"], k + 1)
                for j in range(1, S):
                    ins = dve.scalar_tensor_tensor(pre[:, tt, :], h[j], Hw[:, 16 + j:17 + j], pre[:, tt, :], ALU.mult, ALU.add)
                    if j == S - 1:
                        ins.then_inc(s["t3_pre"], 1)
                    for n in range(2 if j == 1 and k < len(TILES) - 1 else 0, S):
                        mo = mixb[:, tt, n * C:(n + 1) * C]
                        ins = dve.scalar_tensor_tensor(mo, h[j], Hw[:, 4 * n + j:4 * n + j + 1], mo, ALU.mult, ALU.add)
                    own.mark(ins)
                    if j < S - 1:
                        dve.wait_ge(s["dve_own"], own.done())

            def combine(k, summed):
                b, tt = TILES[k]
                dve.wait_ge(s["dve_own"], summed)
                dve.wait_ge(s["t3_y"], k + 1)
                for n in range(S):
                    mo = mixb[:, tt, n * C:(n + 1) * C]
                    ins = dve.scalar_tensor_tensor(mo, ps[2 + tt % 2][:, 0:C], Hall[:, b * TT + tt, 20 + n:21 + n], mo, ALU.mult, ALU.add)
                ins.then_inc(s["t3_sum"], 1)

            for k in range(len(TILES)):
                sums(k)
                if k:
                    combine(k - 1, summed)
                summed = own.done()
            combine(len(TILES) - 1, summed)
            dve.wait_ge(s["t3_sum"], len(TILES))
            b, tt = TILES[-1]
            dve.wait_ge(s[f"t3_in{b % 2}"], 48)
            own.link(dve.tensor_tensor(mixb[:, tt, :], mixb[:, tt, :], gbrow[b % 2], ALU.mult))
            dve.tensor_tensor(x1[b % 2][:, tt, :], x1[b % 2][:, tt, :], mixb[:, tt, :], ALU.add).then_inc(s["t3_last"], 1)


def kernel(**inputs):
    import numpy as np
    import concourse.bacc as bacc
    from concourse.bass_utils import run_bass_kernel_spmd as run

    a = {k: np.asarray(v) for k, v in inputs.items()}

    def cols(w, k):
        return w.reshape(k, P, *w.shape[1:]).swapaxes(0, 1)

    att = {k[len("L0_attn_"):]: v for k, v in a.items() if k.startswith("L0_attn_")}
    ffn = {k[len("L0_ffn_"):]: v for k, v in a.items() if k.startswith("L0_ffn_")}
    arrays = {
        "x": att["hidden_states"].reshape(B, TT, P, H),
        "ident": np.eye(P, dtype=np.float32),
        "w_in": att["in_proj_w"].reshape(KH, P, 2 * KD, P).transpose(2, 1, 0, 3),
        "conv_w": cols(att["conv_w"], KD),
        "conv_b": cols(att["conv_b"], KD),
        "x_proj": cols(att["x_proj_w"].T, KD),
        "dt_proj": att["dt_proj_w"].T,
        "dt_bias": att["dt_bias"].reshape(1, DIN),
        "A_log": att["A_log"].reshape(KD, P, N).transpose(1, 2, 0),
        "D_param": cols(att["D_param"], KD),
        "w_out": att["out_proj_w"].T.reshape(KD // 2, 2, P, 2, 512).transpose(3, 0, 2, 1, 4).reshape(KD, P, 2 * 512),
        "dt_ln": att["dt_ln_w"].reshape(R, 1),
        "B_ln": att["B_ln_w"],
        "C_ln": att["C_ln_w"],
        "W_res": cols(ffn["W_res"].T, KH),
        "W_pre": cols(ffn["W_pre"].T, KH),
        "W_post": cols(ffn["W_post"].T, KH),
        "res_base": ffn["H_res_base"].reshape(S * S),
        "pre_base": ffn["H_pre_base"],
        "post_base": ffn["H_post_base"],
        "gate": ffn["gate"],
        "W_branch": cols(ffn["W_branch"], C // P),
        "c_cols": cols(a["L0_c"].T, KH),
        "w_mod": a["L0_wmod"].reshape(KH, P, 12, 512).transpose(2, 1, 0, 3),
    }
    nc = bacc.Bacc("TRN2", target_bir_lowering=False, num_devices=1)
    args, maps = {}, {}
    for name, v in arrays.items():
        v = np.ascontiguousarray(v)
        maps[f"in_{name}"] = v
        args[name] = nc.dram_tensor(f"in_{name}", v.shape, mybir.dt.from_np(v.dtype), kind="ExternalInput").ap()
    out = nc.dram_tensor("out_y", (B, TT, P, H), F32, kind="ExternalOutput").ap()
    build(nc, out=out, **args)
    r = run(nc, [maps], core_ids=[0])
    return r.results[0]["out_y"].reshape(B, T, H)
```
